# Optimizing a Trainium2 kernel written in Bass

```python
import numpy as np
import jax
import jax.numpy as jnp

def _softmax(x, axis=-1):
    return jax.nn.softmax(x, axis=axis)

def _gelu(x):
    return jax.nn.gelu(x, approximate=True)

def _silu(x):
    return jax.nn.silu(x)

def _sigmoid(x):
    return jax.nn.sigmoid(x)

def _layernorm(x, axis=-1, eps=1e-05):
    m = jnp.mean(x, axis=axis, keepdims=True)
    v = jnp.var(x, axis=axis, keepdims=True)
    return (x - m) / jnp.sqrt(v + eps)

def _scatter_add(tgt, idx, src, axis=0):
    return tgt.at[idx].add(src)

def _segment_sum(src, seg, n):
    return jax.ops.segment_sum(src, seg, n)
kernel_name = 'mk_xattn_ffn_d2_seqx_r8_e76bcb'

def setup_inputs(seed: int=0):
    np.random.seed(seed)
    _w = jnp.asarray

    def _rec_inputs():
        import jax
        import jax.numpy as jnp
        _rk = jax.random.key(seed)
        x = 0.01048 + 0.1018 * jax.random.normal(jax.random.fold_in(_rk, 1), (4, 256, 256), jnp.float32)
        _lenS = 256 - jax.random.randint(jax.random.fold_in(_rk, 7), (4,), 0, max(1, 256 // 4) + 1, jnp.int32)
        _lenS2 = 256 - jax.random.randint(jax.random.fold_in(_rk, 8), (4,), 0, max(1, 256 // 4) + 1, jnp.int32)
        _ctx_512P = jax.random.normal(jax.random.fold_in(_rk, 11), (4, 16, 64), jnp.float32)
        _ctx_512c = jax.random.dirichlet(jax.random.fold_in(_rk, 511), 0.3 * jnp.ones((16,), jnp.float32), (4, 256))
        _ctx_512t = jnp.einsum('bsk,bkd->bsd', _ctx_512c, _ctx_512P)
        _ctx_512t = _ctx_512t * jax.lax.rsqrt(jnp.mean(jnp.square(_ctx_512t)) + 1e-12) * 0.953939
        ctx_512 = -0.000292821 + 1.00034 * (_ctx_512t + 0.3 * jax.random.normal(jax.random.fold_in(_rk, 611), (4, 256, 64), jnp.float32))
        return (x, ctx_512)
    x, ctx_512 = _rec_inputs()

    def _L0_xattn_setup():
        import jax, jax.numpy as jnp
        import numpy as np
        LRELU_ALPHA = 0.2
        MASK_VAL = -10000000000.0
        B, N, F_IN = (4, 256, 64)
        H, F_OUT = (8, 32)
        F_HID = H * F_OUT

        def gat_layer(x, adj, W, a_self, a_neigh, b):
            feat = jnp.einsum('nf,hfo->hno', x, W)
            attn_self = jnp.einsum('hno,ho->hn', feat, a_self)
            attn_neigh = jnp.einsum('hno,ho->hn', feat, a_neigh)
            e = attn_self[:, :, None] + attn_neigh[:, None, :]
            e = jax.nn.leaky_relu(e, LRELU_ALPHA)
            e = e + MASK_VAL * (1.0 - adj)[None, :, :]
            alpha = jax.nn.softmax(e, axis=-1)
            out = jnp.einsum('hnm,hmo->hno', alpha, feat) + b[:, None, :]
            out = jnp.transpose(out, (1, 0, 2)).reshape(out.shape[1], -1)
            return jax.nn.elu(out)
        key = jax.random.key(seed)
        ks = jax.random.split(key, 10)
        feats = jax.random.normal(ks[0], (B, N, F_IN), dtype=jnp.float32)
        a = (jax.random.uniform(ks[1], (B, N, N)) < 0.01).astype(jnp.float32)
        adj = jnp.maximum(a, jnp.eye(N, dtype=jnp.float32)[None])
        s0 = 1.0 / np.sqrt(F_IN)
        s1 = 1.0 / np.sqrt(F_HID)
        return {'feats': feats, 'adj': adj, 'W0': jax.random.normal(ks[2], (H, F_IN, F_OUT), dtype=jnp.float32) * s0, 'a_self0': jax.random.normal(ks[3], (H, F_OUT), dtype=jnp.float32) * 0.1, 'a_neigh0': jax.random.normal(ks[4], (H, F_OUT), dtype=jnp.float32) * 0.1, 'b0': jnp.zeros((H, F_OUT), dtype=jnp.float32), 'W1': jax.random.normal(ks[5], (H, F_HID, F_OUT), dtype=jnp.float32) * s1, 'a_self1': jax.random.normal(ks[6], (H, F_OUT), dtype=jnp.float32) * 0.1, 'a_neigh1': jax.random.normal(ks[7], (H, F_OUT), dtype=jnp.float32) * 0.1, 'b1': jnp.zeros((H, F_OUT), dtype=jnp.float32)}
    _L0_xattn_all = _L0_xattn_setup()
    _L0_xattn_in = {k: v for k, v in _L0_xattn_all.items() if k in ('W0', 'a_self0', 'a_neigh0', 'b0', 'W1', 'a_self1', 'a_neigh1', 'b1')}
    del _L0_xattn_all

    def _L0_ffn_setup():
        import jax, jax.numpy as jnp
        import numpy as np
        NUM_EXPERTS = 8
        TOP_K = 2
        HIDDEN = 256
        INTER = 512
        GATE_MULT = 0.5
        DOWN_MULT = 0.25
        key = jax.random.key(seed)
        k1, k2, k3, k4, k5 = jax.random.split(key, 5)
        s_h = 1.0 / np.sqrt(HIDDEN)
        s_i = 1.0 / np.sqrt(INTER)
        return {'hidden_states': jax.random.normal(k1, (4, 256, HIDDEN), dtype=jnp.float32), 'w_router': jax.random.normal(k2, (HIDDEN, NUM_EXPERTS), dtype=jnp.float32) * s_h, 'w_gate': jax.random.normal(k3, (NUM_EXPERTS, HIDDEN, INTER), dtype=jnp.float32) * s_h, 'w_up': jax.random.normal(k4, (NUM_EXPERTS, HIDDEN, INTER), dtype=jnp.float32) * s_h, 'w_down': jax.random.normal(k5, (NUM_EXPERTS, INTER, HIDDEN), dtype=jnp.float32) * s_i}
    _L0_ffn_all = _L0_ffn_setup()
    _L0_ffn_in = {k: v for k, v in _L0_ffn_all.items() if k in ('w_router', 'w_gate', 'w_up', 'w_down')}
    del _L0_ffn_all

    def _L1_xattn_setup():
        import jax, jax.numpy as jnp
        import numpy as np
        B, N, D = (16, 256, 64)
        H = 4
        TOP_K_RATIO = 0.3
        key = jax.random.key(seed)
        k1, k2, k3, k4 = jax.random.split(key, 4)
        h = jax.random.normal(k1, (B, N, D), dtype=jnp.float32)
        adj_raw = jax.random.uniform(k2, (B, N, N), dtype=jnp.float32)
        lim = 1.0 / np.sqrt(D)
        Wq = jax.random.uniform(k3, (D, D), minval=-lim, maxval=lim, dtype=jnp.float32)
        Wk = jax.random.uniform(k4, (D, D), minval=-lim, maxval=lim, dtype=jnp.float32)
        gamma_raw = jnp.float32(-0.85)
        return {'h': h, 'adj_raw': adj_raw, 'Wq': Wq, 'Wk': Wk, 'gamma_raw': gamma_raw}
    _L1_xattn_all = _L1_xattn_setup()
    _L1_xattn_in = {k: v for k, v in _L1_xattn_all.items() if k in ('Wq', 'Wk', 'gamma_raw')}
    del _L1_xattn_all

    def _L1_ffn_setup():
        import jax, jax.numpy as jnp
        import numpy as np
        H = 256
        NH = 32
        KVH = 4
        HD = 128
        E = 32
        TOPK = 8
        I = 128
        EPS = 1e-05
        THETA = 10000.0

        def _rmsnorm(x, w, eps=EPS):
            xf = x.astype(jnp.float32)
            var = jnp.mean(xf * xf, axis=-1, keepdims=True)
            return (w * (xf * jax.lax.rsqrt(var + eps))).astype(x.dtype)

        def _rope(x, pos):
            d = x.shape[-1]
            inv_freq = 1.0 / THETA ** (jnp.arange(0, d, 2, dtype=jnp.float32) / d)
            ang = pos.astype(jnp.float32)[:, None] * inv_freq[None, :]
            cos = jnp.cos(ang)[None, :, None, :]
            sin = jnp.sin(ang)[None, :, None, :]
            x1, x2 = jnp.split(x, 2, axis=-1)
            return jnp.concatenate([x1 * cos - x2 * sin, x1 * sin + x2 * cos], axis=-1)
        key = jax.random.key(seed)
        ks = jax.random.split(key, 16)
        s = 0.02
        n = lambda k, shape: jax.random.normal(k, shape, dtype=jnp.float32) * s
        return {'hidden_states': jax.random.normal(ks[0], (1, 64, H), dtype=jnp.float32), 'ln1_w': jnp.ones((H,), jnp.float32), 'ln2_w': jnp.ones((H,), jnp.float32), 'Wq': n(ks[1], (H, NH * HD)), 'Wk': n(ks[2], (H, KVH * HD)), 'Wv': n(ks[3], (H, KVH * HD)), 'Wo': n(ks[4], (NH * HD, H)), 'Wr': n(ks[5], (H, E)), 'expert_bias': jax.random.normal(ks[6], (E,), dtype=jnp.float32) * 0.1, 'Wg': n(ks[7], (E, H, I)), 'Wu': n(ks[8], (E, H, I)), 'Wd': n(ks[9], (E, I, H)), 'Wsg': n(ks[10], (H, I)), 'Wsu': n(ks[11], (H, I)), 'Wsd': n(ks[12], (I, H))}
    _L1_ffn_all = _L1_ffn_setup()
    _L1_ffn_in = {k: v for k, v in _L1_ffn_all.items() if k in ('ln1_w', 'ln2_w', 'Wq', 'Wk', 'Wv', 'Wo', 'Wr', 'expert_bias', 'Wg', 'Wu', 'Wd', 'Wsg', 'Wsu', 'Wsd')}
    del _L1_ffn_all
    return {'x': x, 'ctx_512': ctx_512, 'L0_xattn_W0': _L0_xattn_in['W0'], 'L0_xattn_a_self0': _L0_xattn_in['a_self0'], 'L0_xattn_a_neigh0': _L0_xattn_in['a_neigh0'], 'L0_xattn_b0': _L0_xattn_in['b0'], 'L0_xattn_W1': _L0_xattn_in['W1'], 'L0_xattn_a_self1': _L0_xattn_in['a_self1'], 'L0_xattn_a_neigh1': _L0_xattn_in['a_neigh1'], 'L0_xattn_b1': _L0_xattn_in['b1'], 'L0_ffn_w_router': _L0_ffn_in['w_router'], 'L0_ffn_w_gate': _L0_ffn_in['w_gate'], 'L0_ffn_w_up': _L0_ffn_in['w_up'], 'L0_ffn_w_down': _L0_ffn_in['w_down'], 'L1_xattn_Wq': _L1_xattn_in['Wq'], 'L1_xattn_Wk': _L1_xattn_in['Wk'], 'L1_xattn_gamma_raw': _L1_xattn_in['gamma_raw'], 'L1_ffn_ln1_w': _L1_ffn_in['ln1_w'], 'L1_ffn_ln2_w': _L1_ffn_in['ln2_w'], 'L1_ffn_Wq': _L1_ffn_in['Wq'], 'L1_ffn_Wk': _L1_ffn_in['Wk'], 'L1_ffn_Wv': _L1_ffn_in['Wv'], 'L1_ffn_Wo': _L1_ffn_in['Wo'], 'L1_ffn_Wr': _L1_ffn_in['Wr'], 'L1_ffn_expert_bias': _L1_ffn_in['expert_bias'], 'L1_ffn_Wg': _L1_ffn_in['Wg'], 'L1_ffn_Wu': _L1_ffn_in['Wu'], 'L1_ffn_Wd': _L1_ffn_in['Wd'], 'L1_ffn_Wsg': _L1_ffn_in['Wsg'], 'L1_ffn_Wsu': _L1_ffn_in['Wsu'], 'L1_ffn_Wsd': _L1_ffn_in['Wsd']}

def reference(x, ctx_512, L0_xattn_W0, L0_xattn_a_self0, L0_xattn_a_neigh0, L0_xattn_b0, L0_xattn_W1, L0_xattn_a_self1, L0_xattn_a_neigh1, L0_xattn_b1, L0_ffn_w_router, L0_ffn_w_gate, L0_ffn_w_up, L0_ffn_w_down, L1_xattn_Wq, L1_xattn_Wk, L1_xattn_gamma_raw, L1_ffn_ln1_w, L1_ffn_ln2_w, L1_ffn_Wq, L1_ffn_Wk, L1_ffn_Wv, L1_ffn_Wo, L1_ffn_Wr, L1_ffn_expert_bias, L1_ffn_Wg, L1_ffn_Wu, L1_ffn_Wd, L1_ffn_Wsg, L1_ffn_Wsu, L1_ffn_Wsd):
    import jax
    import jax.numpy as jnp

    def _L0_xattn_ref(feats, adj, W0, a_self0, a_neigh0, b0, W1, a_self1, a_neigh1, b1):
        import jax, jax.numpy as jnp
        import numpy as np
        LRELU_ALPHA = 0.2
        MASK_VAL = -10000000000.0
        B, N, F_IN = (4, 256, 64)
        H, F_OUT = (8, 32)
        F_HID = H * F_OUT

        def gat_layer(x, adj, W, a_self, a_neigh, b):
            feat = jnp.einsum('nf,hfo->hno', x, W)
            attn_self = jnp.einsum('hno,ho->hn', feat, a_self)
            attn_neigh = jnp.einsum('hno,ho->hn', feat, a_neigh)
            e = attn_self[:, :, None] + attn_neigh[:, None, :]
            e = jax.nn.leaky_relu(e, LRELU_ALPHA)
            e = e + MASK_VAL * (1.0 - adj)[None, :, :]
            alpha = jax.nn.softmax(e, axis=-1)
            out = jnp.einsum('hnm,hmo->hno', alpha, feat) + b[:, None, :]
            out = jnp.transpose(out, (1, 0, 2)).reshape(out.shape[1], -1)
            return jax.nn.elu(out)

        def per_graph(x, a):
            h = gat_layer(x, a, W0, a_self0, a_neigh0, b0)
            return gat_layer(h, a, W1, a_self1, a_neigh1, b1)
        return jax.vmap(per_graph)(feats, adj)

    def _L0_ffn_ref(hidden_states, w_router, w_gate, w_up, w_down):
        import jax, jax.numpy as jnp
        import numpy as np
        NUM_EXPERTS = 8
        TOP_K = 2
        HIDDEN = 256
        INTER = 512
        GATE_MULT = 0.5
        DOWN_MULT = 0.25
        orig_shape = hidden_states.shape
        x = hidden_states.reshape(-1, orig_shape[-1])
        router_logits = x @ w_router
        probs = jax.nn.softmax(router_logits, axis=-1)
        top_vals, top_idx = jax.lax.top_k(probs, TOP_K)
        out = jnp.zeros_like(x)
        for e in range(NUM_EXPERTS):
            w_e = jnp.sum(jnp.where(top_idx == e, top_vals, 0.0), axis=-1)
            g = x @ w_gate[e] * GATE_MULT
            u = x @ w_up[e]
            h = jax.nn.silu(g) * u @ w_down[e] * DOWN_MULT
            out = out + w_e[:, None] * h
        return out.reshape(orig_shape)

    def _L1_xattn_ref(h, adj_raw, Wq, Wk, gamma_raw):
        import jax, jax.numpy as jnp
        import numpy as np
        B, N, D = (16, 256, 64)
        H = 4
        TOP_K_RATIO = 0.3
        b, n, dm = h.shape
        d = dm // H
        Q = (h @ Wq.T).reshape(b, n, H, d).transpose(0, 2, 1, 3)
        K = (h @ Wk.T).reshape(b, n, H, d).transpose(0, 2, 1, 3)
        sim = jnp.einsum('bhnd,bhmd->bnm', Q, K) / (jnp.sqrt(jnp.float32(d)) * H)
        k = max(1, int(n * TOP_K_RATIO))
        topk_vals = jax.lax.top_k(sim, k)[0]
        threshold = topk_vals[:, :, -1:]
        sparse_mask = (sim >= threshold).astype(sim.dtype)
        A_learned = jax.nn.sigmoid(sim) * sparse_mask
        A_learned = (A_learned + jnp.swapaxes(A_learned, -1, -2)) * 0.5
        gamma = jax.nn.sigmoid(gamma_raw)
        return (1.0 - gamma) * adj_raw + gamma * A_learned

    def _L1_ffn_ref(hidden_states, ln1_w, ln2_w, Wq, Wk, Wv, Wo, Wr, expert_bias, Wg, Wu, Wd, Wsg, Wsu, Wsd):
        import jax, jax.numpy as jnp
        import numpy as np
        H = 256
        NH = 32
        KVH = 4
        HD = 128
        E = 32
        TOPK = 8
        I = 128
        EPS = 1e-05
        THETA = 10000.0

        def _rmsnorm(x, w, eps=EPS):
            xf = x.astype(jnp.float32)
            var = jnp.mean(xf * xf, axis=-1, keepdims=True)
            return (w * (xf * jax.lax.rsqrt(var + eps))).astype(x.dtype)

        def _rope(x, pos):
            d = x.shape[-1]
            inv_freq = 1.0 / THETA ** (jnp.arange(0, d, 2, dtype=jnp.float32) / d)
            ang = pos.astype(jnp.float32)[:, None] * inv_freq[None, :]
            cos = jnp.cos(ang)[None, :, None, :]
            sin = jnp.sin(ang)[None, :, None, :]
            x1, x2 = jnp.split(x, 2, axis=-1)
            return jnp.concatenate([x1 * cos - x2 * sin, x1 * sin + x2 * cos], axis=-1)
        B, S, _ = hidden_states.shape
        resid = hidden_states
        h = _rmsnorm(hidden_states, ln1_w)
        pos = jnp.arange(S)
        q = (h @ Wq).reshape(B, S, NH, HD)
        k = (h @ Wk).reshape(B, S, KVH, HD)
        v = (h @ Wv).reshape(B, S, KVH, HD)
        q = _rope(q, pos)
        k = _rope(k, pos)
        rep = NH // KVH
        k = jnp.repeat(k, rep, axis=2)
        v = jnp.repeat(v, rep, axis=2)
        scores = jnp.einsum('bqhd,bkhd->bhqk', q, k) / jnp.sqrt(jnp.float32(HD))
        causal = jnp.tril(jnp.ones((S, S), dtype=bool))
        scores = jnp.where(causal[None, None], scores, jnp.float32(-1000000000.0))
        attn = jax.nn.softmax(scores, axis=-1)
        o = jnp.einsum('bhqk,bkhd->bqhd', attn, v).reshape(B, S, NH * HD) @ Wo
        x = resid + o
        resid = x
        h = _rmsnorm(x, ln2_w)
        t = h.reshape(-1, H)
        T = t.shape[0]
        router_scores = jax.nn.sigmoid(t @ Wr)
        _, idx = jax.lax.top_k(router_scores + expert_bias[None, :], TOPK)
        w = jnp.take_along_axis(router_scores, idx, axis=1)
        w = w / jnp.sum(w, axis=-1, keepdims=True)
        wfull = jnp.zeros((T, E), jnp.float32).at[jnp.arange(T)[:, None], idx].set(w)
        g = jnp.einsum('th,ehi->tei', t, Wg)
        u = jnp.einsum('th,ehi->tei', t, Wu)
        act = jax.nn.silu(g) * u
        moe = jnp.einsum('tei,te,eih->th', act, wfull, Wd)
        shared = jax.nn.silu(t @ Wsg) * (t @ Wsu) @ Wsd
        return resid + (moe + shared).reshape(B, S, H)
    x = x + _L0_xattn_ref(ctx_512, _layernorm(x, axis=-1), L0_xattn_W0, L0_xattn_a_self0, L0_xattn_a_neigh0, L0_xattn_b0, L0_xattn_W1, L0_xattn_a_self1, L0_xattn_a_neigh1, L0_xattn_b1)
    x = x + _L0_ffn_ref(_layernorm(x, axis=-1), L0_ffn_w_router, L0_ffn_w_gate, L0_ffn_w_up, L0_ffn_w_down)
    x = x + _L1_xattn_ref(ctx_512, _layernorm(x, axis=-1), L1_xattn_Wq, L1_xattn_Wk, L1_xattn_gamma_raw)
    x = x + _L1_ffn_ref(_layernorm(x, axis=-1), L1_ffn_ln1_w, L1_ffn_ln2_w, L1_ffn_Wq, L1_ffn_Wk, L1_ffn_Wv, L1_ffn_Wo, L1_ffn_Wr, L1_ffn_expert_bias, L1_ffn_Wg, L1_ffn_Wu, L1_ffn_Wd, L1_ffn_Wsg, L1_ffn_Wsu, L1_ffn_Wsd)
    return x

_drawn_inputs = setup_inputs


def setup_inputs(seed=0):
    import zlib

    import numpy as np

    out = dict(_drawn_inputs(seed))
    spreads = {'L0_xattn_b0': (0.0, 0.1),
     'L0_xattn_b1': (0.0, 0.1),
     'L1_ffn_ln1_w': (1.0, 0.6),
     'L1_ffn_ln2_w': (1.0, 0.6)}
    factors = {'L1_ffn_Wq': 8.0,
     'L1_ffn_Wk': 8.0,
     'L1_ffn_Wr': 8.0,
     'L1_ffn_expert_bias': 8.0,
     'L1_ffn_Wg': 8.0,
     'L1_ffn_Wu': 8.0,
     'L1_ffn_Wd': 8.0,
     'L1_ffn_Wsg': 8.0,
     'L1_ffn_Wsu': 8.0,
     'L1_ffn_Wsd': 8.0}
    for name, (base, spread) in spreads.items():
        noise = np.random.default_rng([zlib.crc32(name.encode()), seed]).standard_normal(out[name].shape)
        drawn = base * np.exp(spread * noise) if base else spread * noise
        out[name] = jnp.asarray(drawn.astype(out[name].dtype))
    for name, factor in factors.items():
        out[name] = (out[name] * factor).astype(out[name].dtype)
    return out
```

```python
from contextlib import ExitStack

import numpy as np
import concourse.bass as bass
from concourse import mybir

P = 128
B, N, D = 4, 256, 256
T = B * N // P
NT = N // P
HC = D // P
FC = 64
GH, GO = 8, 32
E0, I0, K0 = 8, 512, 2
E1, I1, K1 = 32, 128, 8
TOPK = int(N * 0.3)
NH, KV, HD = 32, 4, 128
REP = NH // KV
EPS = 1e-5
MASK = 1e10
NEG = 0.2
ZK = 40
TROW = 32

F32 = mybir.dt.float32
ALU = mybir.AluOpType
ACT = mybir.ActivationFunctionType
X = mybir.AxisListType.X


def bcast(ap, where, count):
    return ap.unsqueeze(where).to_broadcast(
        list(ap.shape[:where]) + [count] + list(ap.shape[where:]))


class Chain:

    def __init__(self, eng, sem):
        self.eng, self.sem, self.n = eng, sem, 0

    def link(self, ins):
        self.n += 1
        ins.then_inc(self.sem, 1)
        self.eng.wait_ge(self.sem, self.n)

    def restart(self):
        self.eng.sem_clear(self.sem)
        self.n = 0


def expert_steps(eng, steps, body):
    body(0, 0)
    body(1, 1)
    turns = (steps - 3) // 4
    with eng.Fori(0, turns) as i:
        for m in range(4):
            body(i * 4 + (2 + m), (2 + m) % 4)
    for s in range(2 + 4 * turns, steps):
        body(s, s % 4)


def build(nc, x, ctxT, W0, W1, a_self0, a_neigh0, b0, a_self1, a_neigh1, b1,
          w_router, w_gate, w_up, w_down, WqT, WkT, gamma, ln1, ln2, Wq, Wk, Wv, Wo, Wr, ebias,
          Wg, Wu, Wd, ident_in, r_init, delta_in, l_init, rope_q, rope_k, causal_in, out):
    with ExitStack() as ctx:
        def sb(name, shape, dt=F32):
            return ctx.enter_context(nc.sbuf_tensor(name, shape, dt))

        def sem(name):
            return ctx.enter_context(nc.semaphore(name))

        bank = [ctx.enter_context(nc.psum_tensor(f"bank{i}", [P, 512], F32)) for i in range(8)]

        xs = sb("xs", [P, T, D])
        actT = sb("actT", [P, HC, B * N])
        norm = sb("norm", [P, 2, D])
        ident = sb("ident", [P, P])
        stats = sb("stats", [P, T, 6])
        mv = sb("mv", [P, T, 2])
        sd = sb("sd", [P, T])
        rstd = sb("rstd", [P, T])
        eps = sb("eps", [P, 1])
        sq = sb("sq", [P, D])
        lnw = sb("lnw", [P, 2, HC])

        rq = sb("rq", [P, 2, N])
        rk = sb("rk", [P, 2, N])
        causal = sb("causal", [P, 2 * P])
        ctx_all = sb("ctx_all", [FC, B * N])
        wqk = sb("wqk", [FC, 2, FC])
        qkT = sb("qkT", [FC, 2, B * N])
        sim = sb("sim", [P, T, N])
        sig = sb("sig", [P, T, N])
        x3 = sim
        work = sb("work", [P, N])
        top8 = sb("top8", [P, 8])
        gam = sb("gam", [P, 4])
        sym = sb("sym", [P, 2, N])

        route = sb("route", [P, 6, T, E1])
        rcol = sb("rcol", [P, 4, T])
        padded = sb("padded", [P, T, 16])
        kept = sb("kept", [P, T, 16])
        rtop = sb("rtop", [P, T, 8])
        wt0 = sb("wt0", [P, E0, T])
        wt1 = sb("wt1", [P, E1 + 1, T])
        wr0 = sb("wr0", [P, HC, E0])
        wr1 = sb("wr1", [P, HC, E1])
        eb = sb("eb", [P, E1])
        gate_w = sb("gate_w", [P, 2, HC, I0])
        up_w = sb("up_w", [P, 2, HC, I0])
        down_w = sb("down_w", [P, 2, I0 // P, D])
        silu = sb("silu", [P, 2, 512])
        hidT = sb("hidT", [P, 2, I0 // P, 512])

        early = ctx.enter_context(ExitStack())

        def sb_early(name, shape, dt=F32):
            return early.enter_context(nc.sbuf_tensor(name, shape, dt))

        ctx_b = sb_early("ctx_b", [FC, 2, N])
        w0 = sb_early("w0", [FC, D])
        w1 = sb_early("w1", [P, HC, D])
        avec = sb_early("avec", [P, 4, D])
        bvec = sb_early("bvec", [P, 2, D])
        wa_tmp = sb_early("wa_tmp", [P, 6, D])
        wa0 = sb_early("wa0", [FC, ZK])
        wa1 = sb_early("wa1", [P, HC, ZK])
        zl_l = sb_early("zl_l", [ZK, 2, N])
        zl_r = sb_early("zl_r", [ZK, 2, GH * N])
        delta = sb_early("delta", [ZK, GH * N])
        t_row = sb_early("t_row", [ZK, N])
        feat = sb_early("feat", [P, 2, NT, GH, GO + 1])
        adj = sb_early("adj", [P, 2, NT, N])
        lrelu = sb_early("lrelu", [P, 2, 2 * N])
        edge = sb_early("edge", [P, 2, 2 * N])
        edge_min = sb_early("edge_min", [P, 2, 2])
        alpha = sb_early("alpha", [P, 2, 2 * N])
        alphaT = sb_early("alphaT", [P, 2, 2 * N])
        rsum = sb_early("rsum", [P, 2, GH])
        g_out = sb_early("g_out", [P, 2, D])
        g_neg = sb_early("g_neg", [P, 2, D])
        g_pos = sb_early("g_pos", [P, 2, D])
        h1 = sb_early("h1", [P, 2, D])
        h1T = sb_early("h1T", [P, 2, HC, N])

        early.close()

        wq_g = sb("wq_g", [P, HC, REP * HD])
        wk_g = sb("wk_g", [P, HC, HD])
        wv_g = sb("wv_g", [P, HC, HD])
        wo_g = sb("wo_g", [P, REP, D])
        swap = sb("swap", [P, 512])
        rot_c = sb("rot_c", [P, 512])
        rot_s = sb("rot_s", [P, 512])
        kT = sb("kT", [P, B * N])
        vt = sb("vt", [P, T, HD])
        qT = sb("qT", [P, 2, B * N])
        prob = sb("prob", [P, 4, 3 * P])
        pmin = sb("pmin", [P, 4, 2])
        psum_ = sb("psum_", [P, 4, 2])
        pinv = sb("pinv", [P, 4, 2])
        probT = sb("probT", [P, 2, 3 * P])
        oT = sb("oT", [P, REP, B * N])

        S = {n: sem(n) for n in (
            "x_in", "const_in", "gat_in", "sim_in", "ctx_in0", "ctx_in1", "exp_in0", "exp_in1",
            "att_in", "wq_in", "wkv_in", "wo_in", "moe_in0", "moe_in1",
            "dve_held", "pe_held", "pool_held", "sp_held",
            "dve_chain", "pool_chain", "act_chain",
            "zero_done", "wa_done", "sd_done",
            "qk_ready", "qk_copied", "sim_ready", "sim_copied", "sig_done", "gam_done",
            "st_ready", "feat_ready", "feat_copied", "st_copied", "r_ready", "adj_ready",
            "adj_bias", "z_ready", "lrelu_done", "edge_done", "alpha_done", "alphaT_ready",
            "alphaT_copied", "av_done", "g_norm", "g_min", "g_exp", "h1_done", "h1T_ready",
            "h1T_copied",
            "sq_done", "rstd_done", "norm_done", "normT_ready", "normT_copied", "norm_free",
            "aT_ready", "x3_done", "y_done",
            "logit_ready", "rexp_done", "rmax_done", "rw_done",
            "gu0", "silu0", "hid0", "down0", "acc0",
            "gu1", "silu1", "hid1", "down1", "acc1",
            "q_ready", "q_swapped", "q_cos", "q_sin", "q_rot", "v_ready", "v_copied",
            "s_ready", "s_shift", "p_exp", "p_inv", "p_norm", "pT_ready", "pT_copied",
            "o_ready", "o_copied", "wo_ready", "wo_added",
            "out_done")}

        expert_in = {0: (S["exp_in0"], S["exp_in1"]), 1: (S["moe_in0"], S["moe_in1"])}
        mix = {
            0: dict(E=E0, IC=I0 // P, scale=0.5, wt=wt0, gu=S["gu0"], silu=S["silu0"],
                    hid=S["hid0"], down=S["down0"], acc=S["acc0"], src=(w_gate, w_up, w_down)),
            1: dict(E=E1 + 1, IC=I1 // P, scale=1.0, wt=wt1, gu=S["gu1"], silu=S["silu1"],
                    hid=S["hid1"], down=S["down1"], acc=S["acc1"], src=(Wg, Wu, Wd)),
        }
        ROUNDS = 4
        UNITS = 2 * NT * GH // 2 // 2
        TURNS = B // 2

        ALL = ROUNDS * UNITS
        LAST = ALL + 8

        def prep_at(k):
            if k == -1:
                return 0
            r = (k - 6) // UNITS + 1
            return r if (k - 6) % UNITS == 0 and 1 <= r < ROUNDS else None

        def post_at(k, lag):
            q = k - lag - 7
            if q % 4 == 0 and 0 <= q // 4 < 2 * ROUNDS:
                return q // 4 // 2, q // 4 % 2
            return None

        Q_BANK, S_BANK, PT_BANK, O_BANK = bank[0:2], bank[2:4], bank[4:6], bank[6:8]
        AU = REP * B

        block = ctx.enter_context(nc.Block())

        @block.sync
        def _(sp):
            sp.dma_start(xs[:], x.rearrange("b (u p) c -> p (b u) c", p=P)).then_inc(S["x_in"], 16)
            sp.dma_start(ident[:], ident_in).then_inc(S["const_in"], 16)
            sp.dma_start(ctx_all[:], ctxT.rearrange("c b n -> c (b n)")).then_inc(S["sim_in"], 16)
            sp.dma_start(wqk[:, 0, :], WqT).then_inc(S["sim_in"], 16)
            sp.dma_start(wqk[:, 1, :], WkT).then_inc(S["sim_in"], 16)
            sp.dma_start(gam[:, 0:1], gamma.partition_broadcast(P)).then_inc(S["sim_in"], 16)
            sp.dma_start(w0[:], W0).then_inc(S["gat_in"], 16)
            sp.dma_start(w1[:], W1.rearrange("(c p) n -> p c n", p=P)).then_inc(S["gat_in"], 16)
            for j, a in enumerate((a_self0, a_neigh0, a_self1, a_neigh1)):
                sp.dma_start(avec[:, j, :], a.partition_broadcast(P)).then_inc(S["gat_in"], 16)
            sp.dma_start(bvec[:, 0, :], b0.partition_broadcast(P)).then_inc(S["gat_in"], 16)
            sp.dma_start(bvec[:, 1, :], b1.partition_broadcast(P)).then_inc(S["gat_in"], 16)
            sp.dma_start(delta[:], delta_in).then_inc(S["gat_in"], 16)
            for p in range(2):
                sp.dma_start(zl_l[:, p, :], l_init).then_inc(S["gat_in"], 16)
                sp.dma_start(zl_r[:, p, :], r_init).then_inc(S["gat_in"], 16)
            sp.dma_start(wr0[:], w_router.rearrange("(c p) n -> p c n", p=P)).then_inc(S["const_in"], 16)
            sp.dma_start(wr1[:], Wr.rearrange("(c p) n -> p c n", p=P)).then_inc(S["const_in"], 16)
            sp.dma_start(eb[:], ebias.partition_broadcast(P)).then_inc(S["const_in"], 16)
            sp.dma_start(lnw[:, 0, :], ln1).then_inc(S["const_in"], 16)
            sp.dma_start(lnw[:, 1, :], ln2).then_inc(S["const_in"], 16)
            sp.dma_start(rq[:], rope_q).then_inc(S["att_in"], 16)
            sp.dma_start(rk[:], rope_k).then_inc(S["att_in"], 16)
            sp.dma_start(causal[:], causal_in).then_inc(S["att_in"], 16)
            with sp.Fori(0, TURNS) as i:
                for p in range(2):
                    sp.dma_start(ctx_b[:, p, :], ctxT[:, bass.ds(i * 2 + p, 1), :].rearrange(
                        "c b n -> c (b n)")).then_inc(S[f"ctx_in{p}"], 16)
                sp.wait_ge(S["feat_ready"], i * ROUNDS + 2)
                sp.sem_inc(S["sp_held"])

            def load_expert(which, e, par):
                m = mix[which]
                g, u, d = m["src"]
                I = m["IC"] * P
                s = expert_in[which][par]
                sel = (lambda w: w[bass.ds(e, 1)].rearrange("e (c p) n -> p (e c) n", p=P))
                sp.dma_start(gate_w[:, par, :, 0:I], sel(g)).then_inc(s, 16)
                sp.dma_start(up_w[:, par, :, 0:I], sel(u)).then_inc(s, 16)
                sp.dma_start(down_w[:, par, 0:m["IC"], :], sel(d)).then_inc(s, 16)

            def load_experts(which):
                m = mix[which]
                for e in range(2):
                    load_expert(which, e, e)
                pairs = (m["E"] - 2) // 2
                with sp.Fori(0, pairs) as i:
                    for par in range(2):
                        e = i * 2 + (2 + par)
                        sp.wait_ge(m["down"], e * 4 - 4)
                        sp.sem_inc(S["sp_held"])
                        load_expert(which, e, par)
                for e in range(2 + 2 * pairs, m["E"]):
                    sp.wait_ge(m["down"], 4 * e - 4)
                    load_expert(which, e, e % 2)

            load_experts(0)
            with sp.Fori(0, KV) as g:
                for w, dst, n in ((Wq, wq_g, REP * HD),):
                    sp.dma_start(dst[:], w.rearrange("(c p) n -> p c n", p=P)[
                        :, :, bass.ds(g * n, n)]).then_inc(S["wq_in"], 16)
                for w, dst in ((Wk, wk_g), (Wv, wv_g)):
                    sp.dma_start(dst[:], w.rearrange("(c p) n -> p c n", p=P)[
                        :, :, bass.ds(g * HD, HD)]).then_inc(S["wkv_in"], 16)
                sp.dma_start(wo_g[:], Wo.rearrange("(g r p) n -> g p r n", g=KV, p=P)[
                    bass.ds(g, 1)].rearrange("g p r n -> p (g r) n")).then_inc(S["wo_in"], 16)
                sp.wait_ge(S["wo_ready"], (g + 1) * (T // 2))
                sp.sem_inc(S["sp_held"])
            load_experts(1)
            for half in range(2):
                sp.wait_ge(mix[1]["acc"], 4 * E1 + 2 * half + 2)
                sp.dma_start(out.rearrange("b (u p) c -> p (b u) c", p=P)[:, 4 * half:4 * half + 4],
                             xs[:, 4 * half:4 * half + 4, :]).then_inc(S["out_done"], 16)
            sp.wait_ge(S["out_done"], 32)

        @block.tensor
        def _(pe):
            def similarity():
                pe.wait_ge(S["sim_in"], 64)
                for j in range(2):
                    for half in range(2):
                        if j == 1:
                            pe.wait_ge(S["qk_copied"], half + 1)
                        pe.matmul(bank[half][0:FC, :], wqk[:, j, :], ctx_all[:, 512 * half:512 * half + 512],
                                  start=True, stop=True).then_inc(S["qk_ready"], 1)
                pe.wait_ge(S["qk_copied"], 4)
                for t in range(T):
                    if t >= 4:
                        pe.wait_ge(S["sim_copied"], t - 3)
                    pe.matmul(bank[2 + t % 4][:, 0:N], qkT[:, 0, t * P:t * P + P],
                              qkT[:, 1, t // NT * N:t // NT * N + N], start=True, stop=True
                              ).then_inc(S["sim_ready"], 1)

            def graph_attention():
                FEAT, MISC, ZB, PTB, OB = bank[0], bank[1], bank[2:4], bank[4:6], bank[6:8]
                pe.wait_ge(S["wa_done"], 1)
                pe.wait_ge(S["sim_copied"], T)
                with pe.Fori(0, TURNS) as i:
                    def prep(r):
                        layer, p = divmod(r, 2)
                        if layer == 0:
                            pe.wait_ge(S[f"ctx_in{p}"], i * 16 + 16)
                        else:
                            pe.wait_ge(S["h1T_copied"], i * 4 + 2 * p + 2)
                        if r >= 1:
                            pe.wait_ge(S["st_copied"], i * ROUNDS + r)
                            pe.wait_ge(S["feat_copied"], i * ROUNDS + r)
                        ks = 1 if layer == 0 else HC
                        src = (lambda c: ctx_b[:, p, :]) if layer == 0 else (lambda c: h1T[:, p, c, :])
                        wa = (lambda c: wa0[:]) if layer == 0 else (lambda c: wa1[:, c, :])
                        w = (lambda c: w0[:]) if layer == 0 else (lambda c: w1[:, c, :])
                        pe.sem_inc(S["pe_held"])
                        for c in range(ks):
                            mm = pe.matmul(MISC[0:ZK, 0:N], wa(c), src(c), start=c == 0, stop=c == ks - 1)
                        mm.then_inc(S["st_ready"], 1)
                        for nt in range(NT):
                            for c in range(ks):
                                mm = pe.matmul(FEAT[:, nt * D:nt * D + D], src(c)[:, nt * P:nt * P + P],
                                               w(c), start=c == 0, stop=c == ks - 1)
                        mm.then_inc(S["feat_ready"], 1)

                    def outer_sum(k):
                        r, u = divmod(k, UNITS)
                        nt, hp = divmod(u, GH // 2)
                        if u == 0:
                            pe.wait_ge(S["r_ready"], i * ROUNDS + r + 1)
                            pe.wait_ge(S["st_copied"], i * ROUNDS + r + 1)
                        if k >= 2:
                            pe.wait_ge(S["lrelu_done"], i * ALL + k - 1)
                        pe.matmul(ZB[k % 2][:], zl_l[:, r % 2, nt * P:nt * P + P],
                                  zl_r[:, r % 2, hp * 2 * N:(hp + 1) * 2 * N], start=True, stop=True
                                  ).then_inc(S["z_ready"], 1)

                    def turn(k):
                        pe.wait_ge(S["alpha_done"], i * ALL + k + 1)
                        if k >= 2:
                            pe.wait_ge(S["alphaT_copied"], i * ALL + k - 1)
                        for j in range(4):
                            mm = pe.transpose(PTB[k % 2][:, j * P:j * P + P],
                                              alpha[:, k % 2, j * P:j * P + P], ident[:])
                        mm.then_inc(S["alphaT_ready"], 1)

                    def weigh(k):
                        r, u = divmod(k, UNITS)
                        nt, hp = divmod(u, GH // 2)
                        pe.wait_ge(S["alphaT_copied"], i * ALL + k + 1)
                        if u == 0:
                            pe.wait_ge(S["feat_copied"], i * ROUNDS + r + 1)
                        if hp == 0 and r >= 1:
                            pe.wait_ge(S["g_norm"], i * 2 * ROUNDS + 2 * (r - 1) + nt + 1)
                        for h2 in range(2):
                            h = 2 * hp + h2
                            for mc in range(NT):
                                mm = pe.matmul(OB[nt][:, h * (GO + 1):(h + 1) * (GO + 1)],
                                               alphaT[:, k % 2, (2 * h2 + mc) * P:(2 * h2 + mc + 1) * P],
                                               feat[:, r % 2, mc, h, :], start=mc == 0, stop=mc == NT - 1)
                        mm.then_inc(S["av_done"], 1)

                    def turn_h1(r, nt):
                        if r >= 2:
                            return
                        pe.wait_ge(S["h1_done"], i * 2 * ROUNDS + 2 * r + nt + 1)
                        if r * 2 + nt >= 1:
                            pe.wait_ge(S["h1T_copied"], i * 4 + 2 * r + nt)
                        pe.wait_ge(S["st_copied"], i * ROUNDS + r + 1 + (nt == 1 and r == 0))
                        for c in range(HC):
                            mm = pe.transpose(MISC[:, N + c * P:N + c * P + P], h1[:, nt, c * P:c * P + P], ident[:])
                        mm.then_inc(S["h1T_ready"], 1)

                    for k in range(-1, LAST):
                        if (r := prep_at(k)) is not None:
                            prep(r)
                        if 0 <= k < ALL:
                            outer_sum(k)
                        if 0 <= k - 2 < ALL:
                            turn(k - 2)
                        if 0 <= k - 3 < ALL:
                            weigh(k - 3)
                        if (q := post_at(k, 2)) is not None:
                            turn_h1(*q)

            def turn_norm(which):
                for t in range(T):
                    pe.wait_ge(S["norm_done"], which * T + t + 1)
                    if which * T + t >= 2:
                        pe.wait_ge(S["normT_copied"], which * T + t - 1)
                    for c in range(HC):
                        mm = pe.transpose(bank[t % 2][:, c * P:c * P + P], norm[:, t % 2, c * P:c * P + P], ident[:])
                    mm.then_inc(S["normT_ready"], 1)

            def router(which, w, E):
                pe.wait_ge(S["normT_copied"], (1 + 2 * which) * T)
                pe.wait_ge(S["const_in"], 16 * 6)
                for t in range(T):
                    for c in range(HC):
                        mm = pe.matmul(bank[2][:, t * E:t * E + E], actT[:, c, t * P:t * P + P], w[:, c, :],
                                       start=c == 0, stop=c == HC - 1)
                mm.then_inc(S["logit_ready"], 1)

            def mixture(which):
                m = mix[which]
                IC, steps = m["IC"], 2 * m["E"]
                GB, UB, DB = bank[0:2], bank[2:4], bank[4:8]

                def gate_up(s, mod):
                    half, par = mod % 2, mod // 2
                    if half == 0:
                        if isinstance(s, int):
                            pe.wait_ge(expert_in[which][par], 48 * (s // 4 + 1))
                        else:
                            pe.wait_ge(expert_in[which][par], s * 12 + (48 - 12 * mod))
                    for ic in range(IC):
                        q = s * IC + ic
                        if not isinstance(s, int) or q >= 2:
                            pe.wait_ge(m["hid"], q - 1)
                        qp = (mod * IC + ic) % 2
                        for dst, w in ((GB[qp], gate_w), (UB[qp], up_w)):
                            for c in range(HC):
                                mm = pe.matmul(dst[:], w[:, par, c, ic * P:ic * P + P],
                                               actT[:, c, half * 512:half * 512 + 512],
                                               start=c == 0, stop=c == HC - 1)
                        mm.then_inc(m["gu"], 1)

                def down(s, mod):
                    pe.wait_ge(m["hid"], s * IC + IC)
                    if not isinstance(s, int) or s >= 2:
                        pe.wait_ge(m["acc"], s * 2 - 2)
                    for j in range(4):
                        for ic in range(IC):
                            mm = pe.matmul(DB[2 * (mod % 2) + j // 2][:, j % 2 * D:j % 2 * D + D],
                                           hidT[:, mod % 2, ic, j * P:j * P + P], down_w[:, mod // 2, ic, :],
                                           start=ic == 0, stop=ic == IC - 1)
                        if j % 2 == 1:
                            mm.then_inc(m["down"], 1)

                def body(s, mod):
                    if not isinstance(s, int) or s + 1 < steps:
                        gate_up(s + 1, (mod + 1) % 4)
                    down(s, mod)

                pe.wait_ge(S["rmax_done"], which + 1)
                gate_up(0, 0)
                expert_steps(pe, steps, body)

            def symmetric():
                pe.wait_ge(S["acc0"], 4 * E0)
                for t in range(T):
                    b, nt = divmod(t, NT)
                    if t >= 2:
                        pe.wait_ge(S["x3_done"], t - 1)
                    for mt in range(NT):
                        mm = pe.transpose(bank[2 + t % 2][:, mt * P:mt * P + P],
                                          sig[:, b * NT + mt, nt * P:nt * P + P], ident[:])
                    mm.then_inc(S["aT_ready"], 1)

            def attention():
                pe.wait_ge(S["normT_copied"], 2 * T)
                with pe.Fori(0, KV) as g:
                    def project(w, col, n):
                        for half in range(2):
                            if n:
                                pe.wait_ge(S["q_cos"], g * 2 * (REP + 1) + 2 * n + half - 1)
                                pe.wait_ge(S["q_swapped"], g * 2 * (REP + 1) + 2 * n + half - 1)
                            if n == 1:
                                pe.wait_ge(S["v_copied"], g * 2 + half + 1)
                            for c in range(HC):
                                mm = pe.matmul(Q_BANK[half][:], w[:, c, col:col + HD],
                                               actT[:, c, half * 512:half * 512 + 512],
                                               start=c == 0, stop=c == HC - 1)
                            mm.then_inc(S["q_ready"], 1)

                    def values():
                        for half in range(2):
                            for j in range(4):
                                t = 4 * half + j
                                for c in range(HC):
                                    mm = pe.matmul(S_BANK[half][:, j * HD:j * HD + HD], actT[:, c, t * P:t * P + P],
                                                   wv_g[:, c, :], start=c == 0, stop=c == HC - 1)
                            mm.then_inc(S["v_ready"], 1)

                    def scores(k):
                        h, b = divmod(k, B)
                        if b == 0:
                            pe.wait_ge(S["q_rot"], g * 2 * (REP + 1) + 2 * (h + 2))
                        if k < 2:
                            pe.wait_ge(S["v_copied"], g * 2 + 2)
                        if k >= 2:
                            pe.wait_ge(S["s_shift"], g * AU + k - 1)
                        for nt in range(NT):
                            mm = pe.matmul(S_BANK[k % 2][:, nt * P:nt * P + (nt + 1) * P],
                                           qT[:, h % 2, b * N + nt * P:b * N + nt * P + P],
                                           kT[:, b * N:b * N + (nt + 1) * P], start=True, stop=True)
                        mm.then_inc(S["s_ready"], 1)

                    def turn(k):
                        pe.wait_ge(S["p_norm"], g * AU + k + 1)
                        if k >= 2:
                            pe.wait_ge(S["pT_copied"], g * AU + k - 1)
                        for j in range(3):
                            mm = pe.transpose(PT_BANK[k % 2][:, j * P:j * P + P], prob[:, k % 4, j * P:j * P + P], ident[:])
                        mm.then_inc(S["pT_ready"], 1)

                    def weigh(k):
                        b = k % B
                        pe.wait_ge(S["pT_copied"], g * AU + k + 1)
                        if k >= 2:
                            pe.wait_ge(S["o_copied"], g * AU + k - 1)
                        pe.matmul(O_BANK[k % 2][:, 0:N], vt[:, b * NT, :], probT[:, k % 2, 0:N],
                                  start=True, stop=False)
                        pe.matmul(O_BANK[k % 2][:, P:N], vt[:, b * NT + 1, :], probT[:, k % 2, N:N + P],
                                  start=False, stop=True).then_inc(S["o_ready"], 1)

                    def project_out():
                        pe.wait_ge(S["o_copied"], g * AU + AU)
                        pe.wait_ge(S["wo_in"], g * 16 + 16)
                        for t in range(T):
                            if t >= 4 and t % 2 == 0:
                                pe.wait_ge(S["wo_added"], g * (T // 2) + t // 2 - 1)
                            for h in range(REP):
                                mm = pe.matmul(Q_BANK[t // 2 % 2][:, t % 2 * D:t % 2 * D + D],
                                               oT[:, h, t * P:t * P + P], wo_g[:, h, :],
                                               start=h == 0, stop=h == REP - 1)
                            if t % 2 == 1:
                                mm.then_inc(S["wo_ready"], 1)

                    pe.wait_ge(S["wkv_in"], g * 32 + 32)
                    pe.wait_ge(S["wq_in"], g * 16 + 16)
                    project(wk_g, 0, 0)
                    values()
                    project(wq_g, 0, 1)
                    for k in range(AU + 3):
                        if k < AU and k % B == 1 and k // B + 1 < REP:
                            project(wq_g, (k // B + 1) * HD, k // B + 2)
                        if k < AU:
                            scores(k)
                        if 0 <= k - 2 < AU:
                            turn(k - 2)
                        if 0 <= k - 3 < AU:
                            weigh(k - 3)
                    project_out()
                    pe.wait_ge(S["wo_added"], g * (T // 2) + T // 2)

            pe.wait_ge(S["const_in"], 16 * 6)
            similarity()
            graph_attention()
            turn_norm(0)
            router(0, wr0, E0)
            mixture(0)
            symmetric()
            turn_norm(1)
            attention()
            turn_norm(2)
            router(1, wr1, E1)
            mixture(1)

        @block.scalar
        def _(act):
            chain = Chain(act, S["act_chain"])

            def roots(src, scale):
                act.activation(sd[:], src, ACT.Sqrt, bias=eps[:, 0:1], scale=scale).then_inc(S["sd_done"], 1)

            def graph_attention():
                FEAT, ZB = bank[0], bank[2:4]
                with act.Fori(0, TURNS) as i:
                    def prep(r):
                        act.wait_ge(S["feat_ready"], i * ROUNDS + r + 1)
                        act.activation(feat[:, r % 2, :, :, 0:GO],
                                       FEAT.rearrange("p (u h o) -> p u h o", u=NT, h=GH), ACT.Copy
                                       ).then_inc(S["feat_copied"], 1)

                    def leaky(k):
                        act.wait_ge(S["z_ready"], i * ALL + k + 1)
                        if k >= 2:
                            act.wait_ge(S["edge_done"], i * ALL + k - 1)
                        act.activation(lrelu[:, k % 2, :], ZB[k % 2][:], ACT.Copy, scale=-1.0
                                       ).then_inc(S["lrelu_done"], 1)

                    def exps(k):
                        act.wait_ge(S["edge_done"], i * ALL + k + 1)
                        if k >= 2:
                            act.wait_ge(S["alphaT_ready"], i * ALL + k - 1)
                        for h2 in range(2):
                            ins = act.activation(alpha[:, k % 2, h2 * N:h2 * N + N], edge[:, k % 2, h2 * N:h2 * N + N],
                                                 ACT.Exp, bias=edge_min[:, k % 2, h2:h2 + 1], scale=-1.0)
                        ins.then_inc(S["alpha_done"], 1)

                    def post(r, nt):
                        act.wait_ge(S["g_min"], i * 2 * ROUNDS + 2 * r + nt + 1)
                        act.activation(g_neg[:, nt, :], g_neg[:, nt, :], ACT.Exp).then_inc(S["g_exp"], 1)

                    for k in range(-1, LAST):
                        if (r := prep_at(k)) is not None:
                            prep(r)
                        if 0 <= k < ALL:
                            leaky(k)
                        if 0 <= k - 1 < ALL:
                            exps(k - 1)
                        if (q := post_at(k, 1)) is not None:
                            post(*q)

            def mixture(which):
                m = mix[which]
                IC = m["IC"]

                def body(s, mod):
                    for ic in range(IC):
                        q = s * IC + ic
                        qp = (mod * IC + ic) % 2
                        act.wait_ge(m["gu"], q + 1)
                        if not isinstance(s, int) or q >= 2:
                            act.wait_ge(m["hid"], q - 1)
                        act.activation(silu[:, qp, :], bank[qp][:], ACT.Silu, scale=m["scale"]
                                       ).then_inc(m["silu"], 1)

                expert_steps(act, 2 * m["E"], body)

            def squares(which):
                for t in range(T):
                    if which == 0:
                        act.wait_ge(S["y_done"], t + 1)
                    if which == 1 and t == 0:
                        act.wait_ge(S["wo_added"], KV * (T // 2))
                    chain.link(act.activation(sq[:], xs[:, t, :], ACT.Square, accum_out=mv[:, t, 0:1]))
                roots(mv[:, :, 0], 1.0 / D)

            def scaled_copy(which, w):
                for t in range(T):
                    act.wait_ge(S["normT_ready"], which * T + t + 1)
                    for c in range(HC):
                        ins = act.activation(actT[:, c, t * P:t * P + P], bank[t % 2][:, c * P:c * P + P],
                                             ACT.Copy, scale=lnw[:, w, c:c + 1])
                    ins.then_inc(S["normT_copied"], 1)

            def attention():
                act.wait_ge(S["att_in"], 48)
                with act.Fori(0, KV) as g:
                    def swap_halves(n):
                        for half in range(2):
                            act.wait_ge(S["q_ready"], g * 2 * (REP + 1) + 2 * n + half + 1)
                            if n or half:
                                act.wait_ge(S["q_sin"], g * 2 * (REP + 1) + 2 * n + half)
                            act.activation(swap[0:64, :], Q_BANK[half][64:P, :], ACT.Copy)
                            act.activation(swap[64:P, :], Q_BANK[half][0:64, :], ACT.Copy).then_inc(S["q_swapped"], 1)

                    def exps(k):
                        act.wait_ge(S["s_shift"], g * AU + k + 1)
                        for nt in range(NT):
                            ins = act.activation(prob[:, k % 4, nt * P:nt * P + (nt + 1) * P],
                                                 prob[:, k % 4, nt * P:nt * P + (nt + 1) * P], ACT.Exp,
                                                 bias=pmin[:, k % 4, nt:nt + 1], scale=-1.0,
                                                 accum_out=psum_[:, k % 4, nt:nt + 1])
                        ins.then_inc(S["p_exp"], 1)

                    def copy_T(k):
                        act.wait_ge(S["pT_ready"], g * AU + k + 1)
                        if k >= 2:
                            act.wait_ge(S["o_ready"], g * AU + k - 1)
                        act.activation(probT[:, k % 2, :], PT_BANK[k % 2][:, 0:3 * P], ACT.Copy).then_inc(S["pT_copied"], 1)

                    swap_halves(0)
                    swap_halves(1)
                    for k in range(AU + 3):
                        if k < AU and k % B == 1 and k // B + 1 < REP:
                            swap_halves(k // B + 2)
                        if k < AU:
                            exps(k)
                        if 0 <= k - 2 < AU:
                            copy_T(k - 2)

            act.wait_ge(S["sim_in"], 64)
            act.wait_ge(S["zero_done"], 1)
            act.activation(gam[:, 1:2], gam[:, 0:1], ACT.Sigmoid).then_inc(S["gam_done"], 1)
            for t in range(T):
                act.wait_ge(S["sim_copied"], t + 1)
                act.activation(sig[:, t, :], sim[:, t, :], ACT.Sigmoid, scale=1.0 / 16).then_inc(S["sig_done"], 1)
            act.wait_ge(S["rstd_done"], 1)
            roots(mv[:, :, 1], 1.0)
            graph_attention()
            act.wait_ge(S["rstd_done"], 2)
            roots(mv[:, :, 1], 1.0)
            act.wait_ge(S["rmax_done"], 1)
            act.activation(route[:, 0, :, 0:E0], route[:, 0, :, 0:E0], ACT.Exp).then_inc(S["rexp_done"], 1)
            mixture(0)
            act.wait_ge(S["rstd_done"], 3)
            roots(mv[:, :, 1], 1.0)
            act.wait_ge(S["rstd_done"], 4)
            roots(mv[:, :, 1], 1.0)
            squares(0)
            scaled_copy(1, 0)
            attention()
            squares(1)
            scaled_copy(2, 1)
            act.wait_ge(S["logit_ready"], 2)
            act.activation(route[:, 0, :, :], bank[2][:, 0:T * E1].rearrange("p (t e) -> p t e", t=T),
                           ACT.Sigmoid).then_inc(S["rexp_done"], 1)
            mixture(1)

        @block.gpsimd
        def _(pool):
            chain = Chain(pool, S["pool_chain"])
            def signal(ins, name, count):
                ins.then_inc(S[name], 1)
                pool.wait_ge(S[name], count)
                pool.sem_inc(S["pool_held"])

            pool.wait_ge(S["gat_in"], 16 * 13)
            with pool.Fori(0, TURNS) as i:
                chain.restart()
                link = chain.link

                def prep(r):
                    layer, p = divmod(r, 2)
                    if layer == 0:
                        pool.wait_ge(S["adj_ready"], i * 2 + p + 1)
                        pool.sem_inc(S["pool_held"])
                        for nt in range(NT):
                            link(pool.tensor_scalar(adj[:, p, nt, :], adj[:, p, nt, :], -1.0, 1.0, ALU.mult, ALU.add))
                            ins = pool.tensor_scalar(adj[:, p, nt, :], adj[:, p, nt, :], MASK, None, ALU.mult)
                            signal(ins, "adj_bias", i * 4 + (2 * r + nt + 1))
                    pool.wait_ge(S["st_copied"], i * ROUNDS + r + 1)
                    signal(pool.tensor_tensor(
                        zl_r[TROW:ZK, p, :].rearrange("k (h m) -> k h m", h=GH),
                        bcast(t_row[TROW:ZK, :], 1, GH),
                        delta[TROW:ZK, :].rearrange("k (h m) -> k h m", h=GH), ALU.mult),
                        "r_ready", i * ROUNDS + (r + 1))

                def before_exp(r, nt):
                    pool.wait_ge(S["g_norm"], i * 2 * ROUNDS + 2 * r + nt + 1)
                    pool.sem_inc(S["pool_held"])
                    link(pool.tensor_tensor(g_out[:, nt, :], g_out[:, nt, :], bvec[:, r // 2, :], ALU.add))
                    signal(pool.tensor_scalar(g_neg[:, nt, :], g_out[:, nt, :], 0.0, None, ALU.min),
                           "g_min", i * 2 * ROUNDS + (2 * r + nt + 1))
                    link(pool.tensor_scalar(g_pos[:, nt, :], g_out[:, nt, :], 0.0, -1.0, ALU.max, ALU.add))

                def after_exp(r, nt):
                    layer, p = divmod(r, 2)
                    pool.wait_ge(S["g_exp"], i * 2 * ROUNDS + 2 * r + nt + 1)
                    if layer == 0:
                        signal(pool.tensor_tensor(h1[:, nt, :], g_pos[:, nt, :], g_neg[:, nt, :], ALU.add),
                               "h1_done", i * 2 * ROUNDS + (2 * r + nt + 1))
                    else:
                        link(pool.tensor_tensor(g_pos[:, nt, :], g_pos[:, nt, :], g_neg[:, nt, :], ALU.add))
                        row = xs[:, bass.ds(i * 4 + (2 * p + nt), 1), :].rearrange("p u c -> p (u c)")
                        signal(pool.tensor_tensor(row, row, g_pos[:, nt, :], ALU.add),
                               "h1_done", i * 2 * ROUNDS + (2 * r + nt + 1))

                for k in range(-1, LAST):
                    if (r := prep_at(k)) is not None:
                        prep(r)
                    if (q := post_at(k, 0)) is not None:
                        before_exp(*q)
                    if (q := post_at(k, 1)) is not None:
                        after_exp(*q)
            chain.restart()
            pool.wait_ge(S["att_in"], 48)
            with pool.Fori(0, KV) as g:
                chain.restart()
                link = chain.link

                def sines(n):
                    tab = rk if n == 0 else rq
                    for half in range(2):
                        pool.wait_ge(S["q_swapped"], g * 2 * (REP + 1) + 2 * n + half + 1)
                        if n or half:
                            pool.wait_ge(S["q_rot"], g * 2 * (REP + 1) + 2 * n + half)
                        signal(pool.tensor_tensor(rot_s.rearrange("p (b n) -> p b n", b=2),
                                                swap.rearrange("p (b n) -> p b n", b=2),
                                                bcast(tab[:, 1, :], 1, 2), ALU.mult),
                               "q_sin", g * 2 * (REP + 1) + (2 * n + half + 1))

                def normalise(k):
                    pool.wait_ge(S["p_inv"], g * AU + k + 1)
                    pool.sem_inc(S["pool_held"])
                    for nt in range(NT):
                        ins = pool.tensor_scalar(prob[:, k % 4, nt * P:nt * P + (nt + 1) * P],
                                                 prob[:, k % 4, nt * P:nt * P + (nt + 1) * P],
                                                 pinv[:, k % 4, nt:nt + 1], None, ALU.mult)
                        if nt == 0:
                            link(ins)
                    signal(ins, "p_norm", g * AU + (k + 1))

                sines(0)
                sines(1)
                for k in range(AU + 3):
                    if k < AU and k % B == 1 and k // B + 1 < REP:
                        sines(k // B + 2)
                    if 0 <= k - 1 < AU:
                        normalise(k - 1)
            chain.restart()

        @block.vector
        def _(dve):
            chain = Chain(dve, S["dve_chain"])

            def statistics(src):
                for t in range(T):
                    dve.bn_stats(stats[:, t, :], src[:, t, :])
                chain.link(dve.engine_nop())
                for t in range(T):
                    ins = dve.bn_aggr(mv[:, t, :], stats[:, t, :])
                ins.then_inc(S["rstd_done"], 1)

            def inverses(n):
                dve.wait_ge(S["sd_done"], n + 1)
                chain.link(dve.reciprocal(rstd[:], sd[:]))

            def layer_norm_tile(dst, t, src=xs):
                return dve.tensor_scalar(dst, src[:, t, :], mv[:, t, 0:1], rstd[:, t:t + 1], ALU.subtract, ALU.mult)

            def prepare_vectors():
                dve.wait_ge(S["gat_in"], 16 * 13)
                chain.link(dve.memset(wa0[:], 0.0))
                chain.link(dve.memset(wa1[:], 0.0))
                for j in range(2):
                    chain.link(dve.tensor_tensor(wa_tmp[0:FC, j, :], w0[:], avec[0:FC, j, :], ALU.mult))
                    chain.link(dve.tensor_reduce(wa0[:, TROW * j:TROW * j + GH], wa_tmp[0:FC, j, :].rearrange(
                        "p (h o) -> p h o", h=GH), X, ALU.add))
                    for c in range(HC):
                        chain.link(dve.tensor_tensor(wa_tmp[:, 2 + 2 * c + j, :], w1[:, c, :], avec[:, 2 + j, :], ALU.mult))
                        chain.link(dve.tensor_reduce(wa1[:, c, TROW * j:TROW * j + GH], wa_tmp[:, 2 + 2 * c + j, :].rearrange(
                            "p (h o) -> p h o", h=GH), X, ALU.add))
                dve.memset(feat[:, :, :, :, GO:GO + 1], 1.0).then_inc(S["wa_done"], 1)

            def graph_attention():
                MISC, PTB, OB = bank[1], bank[4:6], bank[6:8]
                with dve.Fori(0, TURNS) as i:
                    chain.restart()

                    def prep(r):
                        layer, p = divmod(r, 2)
                        if layer == 0:
                            for nt in range(NT):
                                t = i * 4 + (2 * p + nt)
                                ins = dve.tensor_scalar(
                                    adj[:, p, nt, :], xs[:, bass.ds(t, 1), :].rearrange("p u c -> p (u c)"),
                                    mv[:, bass.ds(t, 1), 0:1].rearrange("p u c -> p (u c)"), rstd[:, bass.ds(t, 1)],
                                    ALU.subtract, ALU.mult)
                            ins.then_inc(S["adj_ready"], 1)
                        dve.wait_ge(S["st_ready"], i * ROUNDS + r + 1)
                        if r >= 1:
                            dve.wait_ge(S["r_ready"], i * ROUNDS + r)
                        dve.tensor_copy(zl_l[0:GH, p, :], MISC[0:GH, 0:N])
                        dve.tensor_copy(t_row[TROW:ZK, :], MISC[TROW:ZK, 0:N]).then_inc(S["st_copied"], 1)

                    def edges(k):
                        r, u = divmod(k, UNITS)
                        nt = u // (GH // 2)
                        dve.wait_ge(S["lrelu_done"], i * ALL + k + 1)
                        if u == 0 and r < 2:
                            dve.wait_ge(S["adj_bias"], i * 4 + 2 * r + 2)
                        if k >= 2:
                            dve.wait_ge(S["alpha_done"], i * ALL + k - 1)
                        chain.link(dve.scalar_tensor_tensor(lrelu[:, k % 2, :], lrelu[:, k % 2, :], NEG,
                                                            lrelu[:, k % 2, :], ALU.mult, ALU.min))
                        for h2 in range(2):
                            ins = dve.tensor_tensor_reduce(
                                out=edge[:, k % 2, h2 * N:h2 * N + N], in0=lrelu[:, k % 2, h2 * N:h2 * N + N],
                                in1=adj[:, r % 2, nt, :], scale=1.0, scalar=3.0e38, op0=ALU.add, op1=ALU.min,
                                accum_out=edge_min[:, k % 2, h2:h2 + 1])
                        ins.then_inc(S["edge_done"], 1)

                    def copy_T(k):
                        dve.wait_ge(S["alphaT_ready"], i * ALL + k + 1)
                        if k >= 2:
                            dve.wait_ge(S["av_done"], i * ALL + k - 1)
                        dve.tensor_copy(alphaT[:, k % 2, :], PTB[k % 2][:]).then_inc(S["alphaT_copied"], 1)

                    def post(r, nt):
                        o = OB[nt][:, 0:GH * (GO + 1)].rearrange("p (h o) -> p h o", h=GH)
                        dve.wait_ge(S["av_done"], i * ALL + r * UNITS + 4 * nt + 4)
                        chain.link(dve.reciprocal(rsum[:, nt, :], o[:, :, GO]))
                        if r >= 1:
                            dve.wait_ge(S["h1_done"], i * 2 * ROUNDS + 2 * (r - 1) + nt + 1)
                        dve.tensor_tensor(g_out[:, nt, :].rearrange("p (h o) -> p h o", h=GH), o[:, :, 0:GO],
                                          bcast(rsum[:, nt, :], 2, GO), ALU.mult).then_inc(S["g_norm"], 1)

                    def copy_h1T(r, nt):
                        if r >= 2:
                            return
                        dve.wait_ge(S["h1T_ready"], i * 4 + 2 * r + nt + 1)
                        dve.tensor_copy(h1T[:, r, :, nt * P:nt * P + P], MISC[:, N:2 * N].rearrange(
                            "p (c n) -> p c n", c=HC)).then_inc(S["h1T_copied"], 1)

                    for k in range(-1, LAST):
                        if (r := prep_at(k)) is not None:
                            prep(r)
                        if 0 <= k < ALL:
                            edges(k)
                        if 0 <= k - 2 < ALL:
                            copy_T(k - 2)
                        if (q := post_at(k, 0)) is not None:
                            post(*q)
                        if (q := post_at(k, 2)) is not None:
                            copy_h1T(*q)
                    dve.wait_ge(S["h1_done"], i * 2 * ROUNDS + 2 * ROUNDS)
                chain.restart()

            def router0():
                R = lambda j: route[:, j, :, 0:E0]
                logits = bank[2][:, 0:T * E0].rearrange("p (t e) -> p t e", t=T)
                dve.wait_ge(S["logit_ready"], 1)
                chain.link(dve.tensor_reduce(rcol[:, 0, :], logits, X, ALU.max))
                dve.tensor_tensor(R(0), logits, bcast(rcol[:, 0, :], 2, E0), ALU.subtract).then_inc(S["rmax_done"], 1)
                dve.wait_ge(S["rexp_done"], 1)
                chain.link(dve.tensor_reduce(rcol[:, 1, :], R(0), X, ALU.add))
                chain.link(dve.reciprocal(rcol[:, 2, :], rcol[:, 1, :]))
                chain.link(dve.memset(padded[:], -1.0))
                chain.link(dve.tensor_tensor(padded[:, :, 0:E0], R(0), bcast(rcol[:, 2, :], 2, E0), ALU.mult))
                for t in range(T):
                    chain.link(dve.max(rtop[:, t, :], padded[:, t, 0:8]))
                chain.link(dve.memset(rtop[:, :, K0:8], -1.0))
                for t in range(T):
                    chain.link(dve.match_replace(kept[:, t, :], rtop[:, t, :], padded[:, t, :], -2.0))
                chain.link(dve.tensor_tensor(R(1), kept[:, :, 0:E0], padded[:, :, 0:E0], ALU.not_equal))
                chain.link(dve.scalar_tensor_tensor(wt0.rearrange("p e t -> p t e"), R(1), 0.25,
                                                    padded[:, :, 0:E0], ALU.mult, ALU.mult))

            def router1():
                dve.wait_ge(S["rexp_done"], 2)
                chain.link(dve.tensor_tensor(route[:, 1], route[:, 0], bcast(eb[:], 1, T), ALU.add))
                for t in range(T):
                    chain.link(dve.max(rtop[:, t, :], route[:, 1, t, :]))
                    chain.link(dve.match_replace(route[:, 2, t, :], rtop[:, t, :], route[:, 1, t, :], -3.0e38))
                chain.link(dve.tensor_tensor(route[:, 3], route[:, 2], route[:, 1], ALU.not_equal))
                chain.link(dve.tensor_tensor(route[:, 4], route[:, 3], route[:, 0], ALU.mult))
                chain.link(dve.tensor_reduce(rcol[:, 0, :], route[:, 4], X, ALU.add))
                chain.link(dve.reciprocal(rcol[:, 1, :], rcol[:, 0, :]))
                dve.memset(wt1[:, E1, :], 1.0)
                chain.link(dve.tensor_tensor(wt1[:, 0:E1, :].rearrange("p e t -> p t e"), route[:, 4],
                                             bcast(rcol[:, 1, :], 2, E1), ALU.mult))
                chain.link(dve.engine_nop())

            def keep_top(e):
                row = (lambda a: a[:, bass.ds(e, 1), :].rearrange("p u c -> p (u c)"))
                chain.link(dve.tensor_copy(work[:], row(sim)))
                for r in range(TOPK // 8):
                    chain.link(dve.max(top8[:], work[:]))
                    chain.link(dve.match_replace(work[:], top8[:], work[:], -3.0e38))
                chain.link(dve.max(top8[:], work[:]))
                rest = TOPK % 8
                chain.link(dve.scalar_tensor_tensor(row(sig), row(sim), top8[:, rest - 1:rest], row(sig),
                                                    ALU.is_ge, ALU.mult))

            def mixture(which):
                m = mix[which]
                IC, wt = m["IC"], m["wt"]
                DB = bank[4:8]

                def multiply(s, mod):
                    if not isinstance(s, int) or s >= 2:
                        dve.wait_ge(m["down"], s * 2 - 2)
                    for ic in range(IC):
                        qp = (mod * IC + ic) % 2
                        dve.wait_ge(m["silu"], s * IC + (ic + 1))
                        dve.tensor_tensor(hidT[:, mod % 2, ic, :], silu[:, qp, :], bank[2 + qp][:], ALU.mult
                                          ).then_inc(m["hid"], 1)

                def add(s, mod):
                    e = s // 2 if isinstance(s, int) else None
                    for j in range(4):
                        t = 4 * (mod % 2) + j
                        if j % 2 == 0:
                            dve.wait_ge(m["down"], s * 2 + (j // 2 + 1))
                        if j == 0 and (e is None or s >= 2):
                            dve.wait_ge(m["acc"], s * 2 - 2)
                        if e is not None:
                            w = wt[:, e, t:t + 1]
                        else:
                            w = wt[:, bass.ds((s - (mod % 2)) // 2, 1), t:t + 1].rearrange("p e t -> p (e t)")
                        ins = dve.scalar_tensor_tensor(xs[:, t, :], DB[2 * (mod % 2) + j // 2][:, j % 2 * D:j % 2 * D + D],
                                                       w, xs[:, t, :], ALU.mult, ALU.add)
                        if j % 2 == 1:
                            ins.then_inc(m["acc"], 1)

                steps = 2 * m["E"]
                multiply(0, 0)

                def body(s, mod):
                    if not isinstance(s, int) or s + 1 < steps:
                        multiply(s + 1, (mod + 1) % 4)
                    add(s, mod)

                expert_steps(dve, steps, body)

            def normalised(which, subtract):
                for t in range(T):
                    if which * T + t >= 2:
                        dve.wait_ge(S["normT_ready"], which * T + t - 1)
                    if subtract:
                        ins = layer_norm_tile(norm[:, t % 2, :], t)
                    else:
                        ins = dve.tensor_scalar(norm[:, t % 2, :], xs[:, t, :], rstd[:, t:t + 1], None, ALU.mult)
                    ins.then_inc(S["norm_done"], 1)
                    if subtract and t >= 1:
                        copy_norm(which, t - 1)
                if subtract:
                    copy_norm(which, T - 1)

            def copy_norm(which, t):
                dve.wait_ge(S["normT_ready"], which * T + t + 1)
                dve.tensor_copy(actT[:, :, t * P:t * P + P], bank[t % 2][:, 0:D].rearrange("p (c n) -> p c n", c=HC)
                                ).then_inc(S["normT_copied"], 1)

            def third():
                dve.wait_ge(S["gam_done"], 1)
                chain.link(dve.tensor_scalar(gam[:, 2:3], gam[:, 1:2], 0.5, None, ALU.mult))
                chain.link(dve.tensor_scalar(gam[:, 3:4], gam[:, 1:2], -1.0, 1.0, ALU.mult, ALU.add))
                for t in range(T):
                    chain.link(layer_norm_tile(sym[:, 0, :], t))
                    chain.link(dve.scalar_tensor_tensor(xs[:, t, :], sym[:, 0, :], gam[:, 3:4], xs[:, t, :],
                                                        ALU.mult, ALU.add))
                    dve.wait_ge(S["aT_ready"], t + 1)
                    chain.link(dve.tensor_tensor(sym[:, 1, :], bank[2 + t % 2][:, 0:N], sig[:, t, :], ALU.add))
                    dve.scalar_tensor_tensor(x3[:, t, :], sym[:, 1, :], gam[:, 2:3], xs[:, t, :],
                                             ALU.mult, ALU.add).then_inc(S["x3_done"], 1)

            def attention():
                dve.wait_ge(S["att_in"], 48)
                with dve.Fori(0, KV) as g:
                    def cosines(n):
                        tab = rk if n == 0 else rq
                        for half in range(2):
                            dve.wait_ge(S["q_swapped"], g * 2 * (REP + 1) + 2 * n + half + 1)
                            if n or half:
                                dve.wait_ge(S["q_rot"], g * 2 * (REP + 1) + 2 * n + half)
                            dve.tensor_tensor(rot_c.rearrange("p (b n) -> p b n", b=2),
                                              Q_BANK[half].rearrange("p (b n) -> p b n", b=2),
                                              bcast(tab[:, 0, :], 1, 2), ALU.mult).then_inc(S["q_cos"], 1)
                            dve.wait_ge(S["q_cos"], g * 2 * (REP + 1) + 2 * n + half + 1)
                            dve.wait_ge(S["q_sin"], g * 2 * (REP + 1) + 2 * n + half + 1)
                            dst = kT[:, half * 512:half * 512 + 512] if n == 0 else \
                                qT[:, (n - 1) % 2, half * 512:half * 512 + 512]
                            dve.tensor_tensor(dst, rot_c[:], rot_s[:], ALU.add).then_inc(S["q_rot"], 1)

                    def shift(k):
                        dve.wait_ge(S["s_ready"], g * AU + k + 1)
                        if k >= 4:
                            dve.wait_ge(S["pT_ready"], g * AU + k - 3)
                        dve.sem_inc(S["dve_held"])
                        for nt in range(NT):
                            ins = dve.tensor_tensor_reduce(
                                out=prob[:, k % 4, nt * P:nt * P + (nt + 1) * P],
                                in0=S_BANK[k % 2][:, nt * P:nt * P + (nt + 1) * P],
                                in1=causal[:, P - nt * P:2 * P], scale=1.0, scalar=3.0e38, op0=ALU.add, op1=ALU.min,
                                accum_out=pmin[:, k % 4, nt:nt + 1])
                        ins.then_inc(S["s_shift"], 1)

                    def invert(k):
                        dve.wait_ge(S["p_exp"], g * AU + k + 1)
                        dve.reciprocal(pinv[:, k % 4, :], psum_[:, k % 4, :]).then_inc(S["p_inv"], 1)

                    def copy_out(k):
                        h, b = divmod(k, B)
                        dve.wait_ge(S["o_ready"], g * AU + k + 1)
                        dve.tensor_copy(oT[:, h, b * N:b * N + N], O_BANK[k % 2][:, 0:N]).then_inc(S["o_copied"], 1)

                    cosines(0)
                    for half in range(2):
                        dve.wait_ge(S["v_ready"], g * 2 + half + 1)
                        dve.tensor_copy(vt[:, 4 * half:4 * half + 4, :], S_BANK[half].rearrange(
                            "p (t n) -> p t n", t=4)).then_inc(S["v_copied"], 1)
                    cosines(1)
                    for k in range(AU + 4):
                        if k < AU and k % B == 1 and k // B + 1 < REP:
                            cosines(k // B + 2)
                        if k < AU:
                            shift(k)
                        if 0 <= k - 1 < AU:
                            invert(k - 1)
                        if 0 <= k - 3 < AU:
                            copy_out(k - 3)
                    for j in range(T // 2):
                        dve.wait_ge(S["wo_ready"], g * (T // 2) + j + 1)
                        rows = xs[:, 2 * j:2 * j + 2, :]
                        dve.tensor_tensor(rows, Q_BANK[j % 2].rearrange("p (t c) -> p t c", t=2), rows,
                                          ALU.add).then_inc(S["wo_added"], 1)

            dve.memset(eps[:], EPS).then_inc(S["zero_done"], 1)
            for j in range(2):
                for half in range(2):
                    dve.wait_ge(S["qk_ready"], 2 * j + half + 1)
                    dve.tensor_copy(qkT[:, j, 512 * half:512 * half + 512], bank[half][0:FC, :]).then_inc(S["qk_copied"], 1)
            for t in range(T):
                dve.wait_ge(S["sim_ready"], t + 1)
                dve.tensor_copy(sim[:, t, :], bank[2 + t % 4][:, 0:N]).then_inc(S["sim_copied"], 1)
            dve.wait_ge(S["x_in"], 16)
            statistics(xs)
            prepare_vectors()
            inverses(0)
            graph_attention()
            statistics(xs)
            inverses(1)
            normalised(0, True)
            router0()
            dve.wait_ge(S["sig_done"], T)
            with dve.Fori(0, T) as e:
                chain.restart()
                keep_top(e)
            chain.restart()
            mixture(0)
            dve.wait_ge(S["acc0"], 4 * E0)
            statistics(xs)
            inverses(2)
            third()
            dve.wait_ge(S["x3_done"], T)
            statistics(x3)
            inverses(3)
            for t in range(T):
                layer_norm_tile(xs[:, t, :], t, x3).then_inc(S["y_done"], 1)
            inverses(4)
            normalised(1, False)
            attention()
            inverses(5)
            dve.wait_ge(S["wo_added"], KV * (T // 2))
            normalised(2, False)
            dve.wait_ge(S["rexp_done"], 2)
            dve.engine_nop().then_inc(S["rmax_done"], 1)
            chain.link(dve.tensor_tensor(xs[:], xs[:], x3[:], ALU.add))
            router1()
            mixture(1)


def kernel(**inputs):
    import concourse.bacc as bacc
    from concourse.bass_utils import run_bass_kernel_spmd

    a = {k: np.asarray(v) for k, v in inputs.items()}
    flat = lambda name: a[name].reshape(-1)
    heads_last = lambda w: np.transpose(w, (1, 0, 2)).reshape(w.shape[1], -1)

    pos = np.arange(N, dtype=np.float32)
    inv = (1.0 / 10000.0 ** (np.arange(0, HD, 2, dtype=np.float32) / HD)).astype(np.float32)
    ang = (pos[:, None] * inv[None, :]).astype(np.float32).T
    cos, sin = np.cos(ang), np.sin(ang)
    rope_k = np.stack([np.concatenate([cos, cos]), np.concatenate([-sin, sin])], 1).astype(np.float32)
    rope_q = (rope_k * np.float32(-1.0 / np.sqrt(HD))).astype(np.float32)
    causal = np.zeros((P, 2 * P), np.float32)
    causal[:, P:] = np.triu(np.full((P, P), 1e9, np.float32), 1)
    r_init = np.zeros((ZK, GH, N), np.float32)
    delta = np.zeros((ZK, GH, N), np.float32)
    for h in range(GH):
        r_init[h, h] = 1.0
        delta[TROW + h, h] = 1.0
    l_init = np.zeros((ZK, N), np.float32)
    l_init[TROW:] = 1.0

    arrays = dict(
        x=a["x"], ctxT=np.transpose(a["ctx_512"], (2, 0, 1)),
        W0=heads_last(a["L0_xattn_W0"]), W1=heads_last(a["L0_xattn_W1"]),
        a_self0=flat("L0_xattn_a_self0"), a_neigh0=flat("L0_xattn_a_neigh0"), b0=flat("L0_xattn_b0"),
        a_self1=flat("L0_xattn_a_self1"), a_neigh1=flat("L0_xattn_a_neigh1"), b1=flat("L0_xattn_b1"),
        w_router=a["L0_ffn_w_router"], w_gate=a["L0_ffn_w_gate"], w_up=a["L0_ffn_w_up"],
        w_down=a["L0_ffn_w_down"], WqT=a["L1_xattn_Wq"].T, WkT=a["L1_xattn_Wk"].T,
        gamma=flat("L1_xattn_gamma_raw"), ln1=a["L1_ffn_ln1_w"].reshape(HC, P).T,
        ln2=a["L1_ffn_ln2_w"].reshape(HC, P).T, Wq=a["L1_ffn_Wq"], Wk=a["L1_ffn_Wk"],
        Wv=a["L1_ffn_Wv"], Wo=a["L1_ffn_Wo"], Wr=a["L1_ffn_Wr"], ebias=a["L1_ffn_expert_bias"],
        Wg=np.concatenate([a["L1_ffn_Wg"], a["L1_ffn_Wsg"][None]]),
        Wu=np.concatenate([a["L1_ffn_Wu"], a["L1_ffn_Wsu"][None]]),
        Wd=np.concatenate([a["L1_ffn_Wd"], a["L1_ffn_Wsd"][None]]),
        ident_in=np.eye(P, dtype=np.float32), r_init=r_init.reshape(ZK, -1),
        delta_in=delta.reshape(ZK, -1), l_init=l_init, rope_q=rope_q, rope_k=rope_k, causal_in=causal)

    nc = bacc.Bacc("TRN2", target_bir_lowering=False, num_devices=1)
    feeds, args = {}, {}
    for name, v in arrays.items():
        v = np.ascontiguousarray(v)
        feeds[f"in_{name}"] = v
        args[name] = nc.dram_tensor(f"in_{name}", v.shape, mybir.dt.from_np(v.dtype), kind="ExternalInput").ap()
    args["out"] = nc.dram_tensor("out_0", (B, N, D), F32, kind="ExternalOutput").ap()
    build(nc, **args)
    r = run_bass_kernel_spmd(nc, [feeds], core_ids=[0])
    return r.results[0]["out_0"]
```

```python
from contextlib import ExitStack

import numpy as np
import concourse.bass as bass
from concourse import mybir

P = 128
B, N, D = 4, 256, 256
T = B * N // P
NT = N // P
HC = D // P
FC = 64
GH, GO = 8, 32
E0, I0, K0 = 8, 512, 2
E1, I1, K1 = 32, 128, 8
TOPK = int(N * 0.3)
NH, KV, HD = 32, 4, 128
REP = NH // KV
EPS = 1e-5
MASK = 1e10
NEG = 0.2
ZK = 40
TROW = 32

F32 = mybir.dt.float32
F32R = mybir.dt.float32r
ALU = mybir.AluOpType
ACT = mybir.ActivationFunctionType
X = mybir.AxisListType.X


def split_product(pe, out, lhs, rhs, first, last):
    pe.matmul(out, lhs[0], rhs[0], start=first, stop=False)
    pe.matmul(out, lhs[0], rhs[1], start=False, stop=False)
    return pe.matmul(out, lhs[1], rhs[0], start=False, stop=last)


def bcast(ap, where, count):
    return ap.unsqueeze(where).to_broadcast(
        list(ap.shape[:where]) + [count] + list(ap.shape[where:]))


class Chain:

    def __init__(self, eng, sem):
        self.eng, self.sem, self.n = eng, sem, 0

    def link(self, ins):
        self.n += 1
        ins.then_inc(self.sem, 1)
        self.eng.wait_ge(self.sem, self.n)

    def restart(self):
        self.eng.sem_clear(self.sem)
        self.n = 0


def expert_steps(eng, steps, body):
    body(0, 0)
    body(1, 1)
    turns = (steps - 3) // 4
    with eng.Fori(0, turns) as i:
        for m in range(4):
            body(i * 4 + (2 + m), (2 + m) % 4)
    for s in range(2 + 4 * turns, steps):
        body(s, s % 4)


def build(nc, x, ctxT, W0, W1, a_self0, a_neigh0, b0, a_self1, a_neigh1, b1,
          w_router, w_gate, w_up, w_down, WqT, WkT, gamma, ln1, ln2, Wq, Wk, Wv, Wo, Wr, ebias,
          Wg, Wu, Wd, ident_in, r_init, delta_in, l_init, rope_q, rope_k, causal_in, out):
    with ExitStack() as ctx:
        def sb(name, shape, dt=F32):
            return ctx.enter_context(nc.sbuf_tensor(name, shape, dt))

        def sem(name):
            return ctx.enter_context(nc.semaphore(name))

        bank = [ctx.enter_context(nc.psum_tensor(f"bank{i}", [P, 512], F32)) for i in range(8)]

        xs = sb("xs", [P, T, D])
        actT = sb("actT", [P, HC, B * N])
        actT_r = sb("actT_r", [P, 2, HC, B * N], F32R)
        norm = sb("norm", [P, 2, D])
        ident = sb("ident", [P, P])
        stats = sb("stats", [P, T, 6])
        mv = sb("mv", [P, T, 2])
        sd = sb("sd", [P, T])
        rstd = sb("rstd", [P, T])
        eps = sb("eps", [P, 1])
        sq = sb("sq", [P, D])
        lnw = sb("lnw", [P, 2, HC])

        rq = sb("rq", [P, 2, N])
        rk = sb("rk", [P, 2, N])
        causal = sb("causal", [P, 2 * P])
        ctx_all = sb("ctx_all", [FC, B * N])
        wqk = sb("wqk", [FC, 2, FC])
        qkT = sb("qkT", [FC, 2, B * N])
        sim = sb("sim", [P, T, N])
        sig = sb("sig", [P, T, N])
        x3 = sim
        work = sb("work", [P, N])
        top8 = sb("top8", [P, 8])
        gam = sb("gam", [P, 4])
        sym = sb("sym", [P, 2, N])

        route = sb("route", [P, 6, T, E1])
        rcol = sb("rcol", [P, 4, T])
        padded = sb("padded", [P, T, 16])
        kept = sb("kept", [P, T, 16])
        rtop = sb("rtop", [P, T, 8])
        wt0 = sb("wt0", [P, E0, T])
        wt1 = sb("wt1", [P, E1 + 1, T])
        wr0 = sb("wr0", [P, HC, E0])
        wr1 = sb("wr1", [P, HC, E1])
        eb = sb("eb", [P, E1])
        gate_w = sb("gate_w", [P, 2, HC, I0])
        up_w = sb("up_w", [P, 2, HC, I0])
        down_w = sb("down_w", [P, 2, I0 // P, D])
        silu = sb("silu", [P, 2, 512])
        hidf = sb("hidf", [P, 2, 512])

        early = ctx.enter_context(ExitStack())

        def sb_early(name, shape, dt=F32):
            return early.enter_context(nc.sbuf_tensor(name, shape, dt))

        ctx_b = sb_early("ctx_b", [FC, 2, N])
        w0 = sb_early("w0", [FC, D])
        w1 = sb_early("w1", [P, HC, D])
        avec = sb_early("avec", [P, 4, D])
        bvec = sb_early("bvec", [P, 2, D])
        wa_tmp = sb_early("wa_tmp", [P, 6, D])
        wa0 = sb_early("wa0", [FC, ZK])
        wa1 = sb_early("wa1", [P, HC, ZK])
        zl_l = sb_early("zl_l", [ZK, 2, N])
        zl_r = sb_early("zl_r", [ZK, 2, GH * N])
        delta = sb_early("delta", [ZK, GH * N])
        t_row = sb_early("t_row", [ZK, N])
        feat = sb_early("feat", [P, 2, NT, GH, GO + 1])
        adj = sb_early("adj", [P, 2, NT, N])
        lrelu = sb_early("lrelu", [P, 2, 2 * N])
        edge = sb_early("edge", [P, 2, 2 * N])
        edge_min = sb_early("edge_min", [P, 2, 2])
        alpha = sb_early("alpha", [P, 2, 2 * N])
        alphaT = sb_early("alphaT", [P, 2, 2 * N])
        rsum = sb_early("rsum", [P, 2, GH])
        g_out = sb_early("g_out", [P, 2, D])
        g_neg = sb_early("g_neg", [P, 2, D])
        g_pos = sb_early("g_pos", [P, 2, D])
        h1 = sb_early("h1", [P, 2, D])
        h1T = sb_early("h1T", [P, 2, HC, N])

        early.close()

        parts = ctx.enter_context(ExitStack())

        def sb_parts(name, shape):
            return parts.enter_context(nc.sbuf_tensor(name, shape, F32R))

        gate_r = sb_parts("gate_r", [P, 2, 2, HC, I0])
        up_r = sb_parts("up_r", [P, 2, 2, HC, I0])
        down_r = sb_parts("down_r", [P, 2, 2, I0 // P, D])
        hidT = sb_parts("hidT", [P, 2, 2, I0 // P, 512])
        parts.close()

        wq_g = sb("wq_g", [P, HC, REP * HD])
        wk_g = sb("wk_g", [P, HC, HD])
        wv_g = sb("wv_g", [P, HC, HD])
        wo_g = sb("wo_g", [P, REP, D])
        swap = sb("swap", [P, 2, 512])
        rot_c = sb("rot_c", [P, 2, 512])
        rot_s = sb("rot_s", [P, 2, 512])
        kT = sb("kT", [P, B * N])
        vt = sb("vt", [P, T, HD])
        qT = sb("qT", [P, 2, B * N])
        prob = sb("prob", [P, 4, 3 * P])
        pmin = sb("pmin", [P, 4, 2])
        psum_ = sb("psum_", [P, 4, 2])
        pinv = sb("pinv", [P, 4, 2])
        probT = sb("probT", [P, 2, 3 * P])
        oT = sb("oT", [P, REP, B * N])

        S = {n: sem(n) for n in (
            "x_in", "const_in", "gat_in", "sim_in", "ctx_in0", "ctx_in1", "exp_in0", "exp_in1",
            "att_in", "wq_in", "wkv_in", "wo_in", "moe_in0", "moe_in1",
            "dve_held", "pe_held", "pool_held", "sp_held",
            "dve_chain", "pool_chain", "act_chain",
            "zero_done", "wa_done", "sd_done",
            "qk_ready", "qk_copied", "sim_ready", "sim_copied", "sig_done", "gam_done",
            "st_ready", "feat_ready", "feat_copied", "st_copied", "r_ready", "adj_ready",
            "adj_bias", "z_ready", "lrelu_done", "edge_done", "alpha_done", "alphaT_ready",
            "alphaT_copied", "av_done", "g_norm", "g_min", "g_exp", "h1_done", "h1T_ready",
            "h1T_copied",
            "sq_done", "rstd_done", "norm_done", "normT_ready", "normT_copied", "norm_free",
            "aT_ready", "x3_done", "y_done",
            "logit_ready", "rexp_done", "rmax_done", "rw_done",
            "gu0", "silu0", "hid0", "down0", "acc0", "whi0", "wlo0", "hidf0", "hidh0",
            "gu1", "silu1", "hid1", "down1", "acc1", "whi1", "wlo1", "hidf1", "hidh1", "actT_hi", "actT_lo",
            "q_ready", "q_swapped", "q_cos", "q_sin", "q_rot", "v_ready", "v_copied",
            "s_ready", "s_shift", "p_exp", "p_inv", "p_norm", "pT_ready", "pT_copied",
            "o_ready", "o_copied", "wo_ready", "wo_added",
            "out_done")}

        expert_in = {0: (S["exp_in0"], S["exp_in1"]), 1: (S["moe_in0"], S["moe_in1"])}
        mix = {
            0: dict(E=E0, IC=I0 // P, scale=0.5, wt=wt0, gu=S["gu0"], silu=S["silu0"],
                    hid=S["hid0"], down=S["down0"], acc=S["acc0"], whi=S["whi0"], wlo=S["wlo0"],
                    hidf=S["hidf0"], hidh=S["hidh0"], src=(w_gate, w_up, w_down)),
            1: dict(E=E1 + 1, IC=I1 // P, scale=1.0, wt=wt1, gu=S["gu1"], silu=S["silu1"],
                    hid=S["hid1"], down=S["down1"], acc=S["acc1"], whi=S["whi1"], wlo=S["wlo1"],
                    hidf=S["hidf1"], hidh=S["hidh1"], src=(Wg, Wu, Wd)),
        }
        ROUNDS = 4
        UNITS = 2 * NT * GH // 2 // 2
        TURNS = B // 2

        ALL = ROUNDS * UNITS
        LAST = ALL + 8

        def prep_at(k):
            if k == -1:
                return 0
            r = (k - 6) // UNITS + 1
            return r if (k - 6) % UNITS == 0 and 1 <= r < ROUNDS else None

        def post_at(k, lag):
            q = k - lag - 7
            if q % 4 == 0 and 0 <= q // 4 < 2 * ROUNDS:
                return q // 4 // 2, q // 4 % 2
            return None

        Q_BANK, S_BANK, PT_BANK, O_BANK = bank[0:2], bank[2:4], bank[4:6], bank[6:8]
        AU = REP * B
        PROJ = 2 * (REP + 1)

        block = ctx.enter_context(nc.Block())

        @block.sync
        def _(sp):
            sp.dma_start(xs[:], x.rearrange("b (u p) c -> p (b u) c", p=P)).then_inc(S["x_in"], 16)
            sp.dma_start(ident[:], ident_in).then_inc(S["const_in"], 16)
            sp.dma_start(ctx_all[:], ctxT.rearrange("c b n -> c (b n)")).then_inc(S["sim_in"], 16)
            sp.dma_start(wqk[:, 0, :], WqT).then_inc(S["sim_in"], 16)
            sp.dma_start(wqk[:, 1, :], WkT).then_inc(S["sim_in"], 16)
            sp.dma_start(gam[:, 0:1], gamma.partition_broadcast(P)).then_inc(S["sim_in"], 16)
            sp.dma_start(w0[:], W0).then_inc(S["gat_in"], 16)
            sp.dma_start(w1[:], W1.rearrange("(c p) n -> p c n", p=P)).then_inc(S["gat_in"], 16)
            for j, a in enumerate((a_self0, a_neigh0, a_self1, a_neigh1)):
                sp.dma_start(avec[:, j, :], a.partition_broadcast(P)).then_inc(S["gat_in"], 16)
            sp.dma_start(bvec[:, 0, :], b0.partition_broadcast(P)).then_inc(S["gat_in"], 16)
            sp.dma_start(bvec[:, 1, :], b1.partition_broadcast(P)).then_inc(S["gat_in"], 16)
            sp.dma_start(delta[:], delta_in).then_inc(S["gat_in"], 16)
            for p in range(2):
                sp.dma_start(zl_l[:, p, :], l_init).then_inc(S["gat_in"], 16)
                sp.dma_start(zl_r[:, p, :], r_init).then_inc(S["gat_in"], 16)
            sp.dma_start(wr0[:], w_router.rearrange("(c p) n -> p c n", p=P)).then_inc(S["const_in"], 16)
            sp.dma_start(wr1[:], Wr.rearrange("(c p) n -> p c n", p=P)).then_inc(S["const_in"], 16)
            sp.dma_start(eb[:], ebias.partition_broadcast(P)).then_inc(S["const_in"], 16)
            sp.dma_start(lnw[:, 0, :], ln1).then_inc(S["const_in"], 16)
            sp.dma_start(lnw[:, 1, :], ln2).then_inc(S["const_in"], 16)
            sp.dma_start(rq[:], rope_q).then_inc(S["att_in"], 16)
            sp.dma_start(rk[:], rope_k).then_inc(S["att_in"], 16)
            sp.dma_start(causal[:], causal_in).then_inc(S["att_in"], 16)
            with sp.Fori(0, TURNS) as i:
                for p in range(2):
                    sp.dma_start(ctx_b[:, p, :], ctxT[:, bass.ds(i * 2 + p, 1), :].rearrange(
                        "c b n -> c (b n)")).then_inc(S[f"ctx_in{p}"], 16)
                sp.wait_ge(S["feat_ready"], i * ROUNDS + 2)
                sp.sem_inc(S["sp_held"])

            def load_expert(which, e, par):
                m = mix[which]
                g, u, d = m["src"]
                I = m["IC"] * P
                s = expert_in[which][par]
                sel = (lambda w: w[bass.ds(e, 1)].rearrange("e (c p) n -> p (e c) n", p=P))
                sp.dma_start(gate_w[:, par, :, 0:I], sel(g)).then_inc(s, 16)
                sp.dma_start(up_w[:, par, :, 0:I], sel(u)).then_inc(s, 16)
                sp.dma_start(down_w[:, par, 0:m["IC"], :], sel(d)).then_inc(s, 16)

            def load_experts(which):
                m = mix[which]
                for e in range(2):
                    load_expert(which, e, e)
                pairs = (m["E"] - 2) // 2
                with sp.Fori(0, pairs) as i:
                    for par in range(2):
                        e = i * 2 + (2 + par)
                        sp.wait_ge(m["wlo"], e * 3 - 3)
                        sp.sem_inc(S["sp_held"])
                        load_expert(which, e, par)
                for e in range(2 + 2 * pairs, m["E"]):
                    sp.wait_ge(m["wlo"], 3 * e - 3)
                    load_expert(which, e, e % 2)

            load_experts(0)
            def load_projections(g):
                sp.dma_start(wq_g[:], Wq.rearrange("(c p) n -> p c n", p=P)[
                    :, :, bass.ds(g * (REP * HD), REP * HD)]).then_inc(S["wq_in"], 16)
                for w, dst in ((Wk, wk_g), (Wv, wv_g)):
                    sp.dma_start(dst[:], w.rearrange("(c p) n -> p c n", p=P)[
                        :, :, bass.ds(g * HD, HD)]).then_inc(S["wkv_in"], 16)

            sp.wait_ge(mix[0]["down"], 4 * E0)
            load_projections(0)

            def load_output(g):
                sp.dma_start(wo_g[:], Wo.rearrange("(g r p) n -> g p r n", g=KV, p=P)[
                    bass.ds(g, 1)].rearrange("g p r n -> p (g r) n")).then_inc(S["wo_in"], 16)

            with sp.Fori(0, KV - 1) as g:
                load_output(g)
                sp.wait_ge(S["q_ready"], (g + 1) * PROJ)
                sp.sem_inc(S["sp_held"])
                load_projections(g + 1)
                sp.wait_ge(S["wo_ready"], (g + 1) * (T // 2))
                sp.sem_inc(S["sp_held"])
            load_output(KV - 1)
            load_experts(1)
            for half in range(2):
                sp.wait_ge(mix[1]["acc"], 4 * E1 + 2 * half + 2)
                sp.dma_start(out.rearrange("b (u p) c -> p (b u) c", p=P)[:, 4 * half:4 * half + 4],
                             xs[:, 4 * half:4 * half + 4, :]).then_inc(S["out_done"], 16)
            sp.wait_ge(S["out_done"], 32)

        @block.tensor
        def _(pe):
            def similarity():
                pe.wait_ge(S["sim_in"], 64)
                for j in range(2):
                    for half in range(2):
                        if j == 1:
                            pe.wait_ge(S["qk_copied"], half + 1)
                        pe.matmul(bank[half][0:FC, :], wqk[:, j, :], ctx_all[:, 512 * half:512 * half + 512],
                                  start=True, stop=True).then_inc(S["qk_ready"], 1)
                pe.wait_ge(S["qk_copied"], 4)
                for t in range(T):
                    if t >= 4:
                        pe.wait_ge(S["sim_copied"], t - 3)
                    pe.matmul(bank[2 + t % 4][:, 0:N], qkT[:, 0, t * P:t * P + P],
                              qkT[:, 1, t // NT * N:t // NT * N + N], start=True, stop=True
                              ).then_inc(S["sim_ready"], 1)

            def graph_attention():
                FEAT, MISC, ZB, PTB, OB = bank[0], bank[1], bank[2:4], bank[4:6], bank[6:8]
                pe.wait_ge(S["wa_done"], 1)
                pe.wait_ge(S["sim_copied"], T)
                with pe.Fori(0, TURNS) as i:
                    def prep(r):
                        layer, p = divmod(r, 2)
                        if layer == 0:
                            pe.wait_ge(S[f"ctx_in{p}"], i * 16 + 16)
                        else:
                            pe.wait_ge(S["h1T_copied"], i * 4 + 2 * p + 2)
                        if r >= 1:
                            pe.wait_ge(S["st_copied"], i * ROUNDS + r)
                            pe.wait_ge(S["feat_copied"], i * ROUNDS + r)
                        ks = 1 if layer == 0 else HC
                        src = (lambda c: ctx_b[:, p, :]) if layer == 0 else (lambda c: h1T[:, p, c, :])
                        wa = (lambda c: wa0[:]) if layer == 0 else (lambda c: wa1[:, c, :])
                        w = (lambda c: w0[:]) if layer == 0 else (lambda c: w1[:, c, :])
                        pe.sem_inc(S["pe_held"])
                        for c in range(ks):
                            mm = pe.matmul(MISC[0:ZK, 0:N], wa(c), src(c), start=c == 0, stop=c == ks - 1)
                        mm.then_inc(S["st_ready"], 1)
                        for nt in range(NT):
                            for c in range(ks):
                                mm = pe.matmul(FEAT[:, nt * D:nt * D + D], src(c)[:, nt * P:nt * P + P],
                                               w(c), start=c == 0, stop=c == ks - 1)
                        mm.then_inc(S["feat_ready"], 1)

                    def outer_sum(k):
                        r, u = divmod(k, UNITS)
                        nt, hp = divmod(u, GH // 2)
                        if u == 0:
                            pe.wait_ge(S["r_ready"], i * ROUNDS + r + 1)
                            pe.wait_ge(S["st_copied"], i * ROUNDS + r + 1)
                        if k >= 2:
                            pe.wait_ge(S["lrelu_done"], i * ALL + k - 1)
                        pe.matmul(ZB[k % 2][:], zl_l[:, r % 2, nt * P:nt * P + P],
                                  zl_r[:, r % 2, hp * 2 * N:(hp + 1) * 2 * N], start=True, stop=True
                                  ).then_inc(S["z_ready"], 1)

                    def turn(k):
                        pe.wait_ge(S["alpha_done"], i * ALL + k + 1)
                        if k >= 2:
                            pe.wait_ge(S["alphaT_copied"], i * ALL + k - 1)
                        for j in range(4):
                            mm = pe.transpose(PTB[k % 2][:, j * P:j * P + P],
                                              alpha[:, k % 2, j * P:j * P + P], ident[:])
                        mm.then_inc(S["alphaT_ready"], 1)

                    def weigh(k):
                        r, u = divmod(k, UNITS)
                        nt, hp = divmod(u, GH // 2)
                        pe.wait_ge(S["alphaT_copied"], i * ALL + k + 1)
                        if u == 0:
                            pe.wait_ge(S["feat_copied"], i * ROUNDS + r + 1)
                        if hp == 0 and r >= 1:
                            pe.wait_ge(S["g_norm"], i * 2 * ROUNDS + 2 * (r - 1) + nt + 1)
                        for h2 in range(2):
                            h = 2 * hp + h2
                            for mc in range(NT):
                                mm = pe.matmul(OB[nt][:, h * (GO + 1):(h + 1) * (GO + 1)],
                                               alphaT[:, k % 2, (2 * h2 + mc) * P:(2 * h2 + mc + 1) * P],
                                               feat[:, r % 2, mc, h, :], start=mc == 0, stop=mc == NT - 1)
                        mm.then_inc(S["av_done"], 1)

                    def turn_h1(r, nt):
                        if r >= 2:
                            return
                        pe.wait_ge(S["h1_done"], i * 2 * ROUNDS + 2 * r + nt + 1)
                        if r * 2 + nt >= 1:
                            pe.wait_ge(S["h1T_copied"], i * 4 + 2 * r + nt)
                        pe.wait_ge(S["st_copied"], i * ROUNDS + r + 1 + (nt == 1 and r == 0))
                        for c in range(HC):
                            mm = pe.transpose(MISC[:, N + c * P:N + c * P + P], h1[:, nt, c * P:c * P + P], ident[:])
                        mm.then_inc(S["h1T_ready"], 1)

                    for k in range(-1, LAST):
                        if (r := prep_at(k)) is not None:
                            prep(r)
                        if 0 <= k < ALL:
                            outer_sum(k)
                        if 0 <= k - 2 < ALL:
                            turn(k - 2)
                        if 0 <= k - 3 < ALL:
                            weigh(k - 3)
                        if (q := post_at(k, 2)) is not None:
                            turn_h1(*q)

            def turn_norm(which):
                for t in range(T):
                    pe.wait_ge(S["norm_done"], which * T + t + 1)
                    if which * T + t >= 2:
                        pe.wait_ge(S["normT_copied"], which * T + t - 1)
                    for c in range(HC):
                        mm = pe.transpose(bank[t % 2][:, c * P:c * P + P], norm[:, t % 2, c * P:c * P + P], ident[:])
                    mm.then_inc(S["normT_ready"], 1)

            def router(which, w, E):
                pe.wait_ge(S["normT_copied"], (1 + 2 * which) * T)
                pe.wait_ge(S["const_in"], 16 * 6)
                for t in range(T):
                    for c in range(HC):
                        mm = pe.matmul(bank[2][:, t * E:t * E + E], actT[:, c, t * P:t * P + P], w[:, c, :],
                                       start=c == 0, stop=c == HC - 1)
                mm.then_inc(S["logit_ready"], 1)

            def mixture(which):
                m = mix[which]
                IC, steps = m["IC"], 2 * m["E"]
                GB, UB, DB = bank[0:2], bank[2:4], bank[4:8]

                def gate_up(s, mod):
                    half, par = mod % 2, mod // 2
                    if half == 0:
                        pe.wait_ge(m["wlo"], 3 * (s // 2) + 3 if isinstance(s, int) else (s // 2) * 3 + 3)
                    for ic in range(IC):
                        q = s * IC + ic
                        if not isinstance(s, int) or q >= 2:
                            pe.wait_ge(m["hid"], q - 1)
                        qp = (mod * IC + ic) % 2
                        for dst, w in ((GB[qp], gate_r), (UB[qp], up_r)):
                            for c in range(HC):
                                mm = split_product(
                                    pe, dst[:], [w[:, par, j, c, ic * P:ic * P + P] for j in range(2)],
                                    [actT_r[:, j, c, half * 512:half * 512 + 512] for j in range(2)],
                                    c == 0, c == HC - 1)
                        mm.then_inc(m["gu"], 1)

                def down(s, mod):
                    pe.wait_ge(m["hid"], s * IC + IC)
                    if not isinstance(s, int) or s >= 2:
                        pe.wait_ge(m["acc"], s * 2 - 2)
                    for j in range(4):
                        for ic in range(IC):
                            mm = split_product(
                                pe, DB[2 * (mod % 2) + j // 2][:, j % 2 * D:j % 2 * D + D],
                                [hidT[:, mod % 2, r, ic, j * P:j * P + P] for r in range(2)],
                                [down_r[:, mod // 2, r, ic, :] for r in range(2)], ic == 0, ic == IC - 1)
                        if j % 2 == 1:
                            mm.then_inc(m["down"], 1)

                def body(s, mod):
                    if not isinstance(s, int) or s + 1 < steps:
                        gate_up(s + 1, (mod + 1) % 4)
                    down(s, mod)

                pe.wait_ge(S["rmax_done"], which + 1)
                pe.wait_ge(S["actT_lo"], which + 1)
                gate_up(0, 0)
                expert_steps(pe, steps, body)

            def symmetric():
                pe.wait_ge(S["acc0"], 4 * E0)
                for t in range(T):
                    b, nt = divmod(t, NT)
                    if t >= 2:
                        pe.wait_ge(S["x3_done"], t - 1)
                    for mt in range(NT):
                        mm = pe.transpose(bank[2 + t % 2][:, mt * P:mt * P + P],
                                          sig[:, b * NT + mt, nt * P:nt * P + P], ident[:])
                    mm.then_inc(S["aT_ready"], 1)

            def attention():
                pe.wait_ge(S["normT_copied"], 2 * T)

                def project(g, n):
                    w, col = (wk_g, 0) if n == 0 else (wq_g, (n - 1) * HD)
                    for half in range(2):
                        if n:
                            pe.wait_ge(S["q_cos"], g * PROJ + (2 * n + half - 1))
                        for c in range(HC):
                            mm = pe.matmul(Q_BANK[half][:], w[:, c, col:col + HD],
                                           actT[:, c, half * 512:half * 512 + 512],
                                           start=c == 0, stop=c == HC - 1)
                        mm.then_inc(S["q_ready"], 1)

                def keys(g):
                    pe.wait_ge(S["wkv_in"], g * 32 + 32)
                    pe.wait_ge(S["wq_in"], g * 16 + 16)
                    project(g, 0)

                def values():
                    for half in range(2):
                        for j in range(4):
                            t = 4 * half + j
                            for c in range(HC):
                                mm = pe.matmul(S_BANK[half][:, j * HD:j * HD + HD], actT[:, c, t * P:t * P + P],
                                               wv_g[:, c, :], start=c == 0, stop=c == HC - 1)
                        mm.then_inc(S["v_ready"], 1)

                def group(g, last):
                    def scores(k):
                        h, b = divmod(k, B)
                        if b == 0:
                            pe.wait_ge(S["q_rot"], g * PROJ + 2 * (h + 2))
                        if k < 2:
                            pe.wait_ge(S["v_copied"], g * 2 + (k + 1))
                        if k >= 2:
                            pe.wait_ge(S["s_shift"], g * AU + (k - 1))
                        for nt in range(NT):
                            mm = pe.matmul(S_BANK[k % 2][:, nt * P:nt * P + (nt + 1) * P],
                                           qT[:, h % 2, b * N + nt * P:b * N + nt * P + P],
                                           kT[:, b * N:b * N + (nt + 1) * P], start=True, stop=True)
                        mm.then_inc(S["s_ready"], 1)

                    def turn(k):
                        pe.wait_ge(S["p_norm"], g * AU + (k + 1))
                        if k >= 2:
                            pe.wait_ge(S["pT_copied"], g * AU + (k - 1))
                        elif not isinstance(g, int):
                            pe.wait_ge(S["wo_added"], g * (T // 2))
                        for j in range(3):
                            mm = pe.transpose(PT_BANK[k % 2][:, j * P:j * P + P], prob[:, k % 4, j * P:j * P + P], ident[:])
                        mm.then_inc(S["pT_ready"], 1)

                    def weigh(k):
                        b = k % B
                        pe.wait_ge(S["pT_copied"], g * AU + (k + 1))
                        if k >= 2:
                            pe.wait_ge(S["o_copied"], g * AU + (k - 1))
                        pe.matmul(O_BANK[k % 2][:, 0:N], vt[:, b * NT, :], probT[:, k % 2, 0:N],
                                  start=True, stop=False)
                        pe.matmul(O_BANK[k % 2][:, P:N], vt[:, b * NT + 1, :], probT[:, k % 2, N:N + P],
                                  start=False, stop=True).then_inc(S["o_ready"], 1)

                    def project_out(pairs):
                        for j in pairs:
                            if j >= 2:
                                pe.wait_ge(S["wo_added"], g * (T // 2) + (j - 1))
                            for u in range(2):
                                t = 2 * j + u
                                for h in range(REP):
                                    mm = pe.matmul(PT_BANK[j % 2][:, u * D:u * D + D],
                                                   oT[:, h, t * P:t * P + P], wo_g[:, h, :],
                                                   start=h == 0, stop=h == REP - 1)
                            mm.then_inc(S["wo_ready"], 1)

                    for k in range(AU + 3):
                        if k < AU and k % B == 0 and k // B + 1 < REP:
                            project(g, k // B + 2)
                        if k == AU and not last:
                            keys(g + 1)
                        if k < AU:
                            scores(k)
                        if 0 <= k - 2 < AU:
                            turn(k - 2)
                        if 0 <= k - 3 < AU:
                            weigh(k - 3)
                    if not last:
                        values()
                    pe.wait_ge(S["o_copied"], g * AU + AU)
                    pe.wait_ge(S["wo_in"], g * 16 + 16)
                    project_out((0, 1))
                    if not last:
                        project(g + 1, 1)
                    project_out((2, 3))

                keys(0)
                values()
                project(0, 1)
                with pe.Fori(0, KV - 1) as g:
                    group(g, False)
                group(KV - 1, True)

            pe.wait_ge(S["const_in"], 16 * 6)
            similarity()
            graph_attention()
            turn_norm(0)
            router(0, wr0, E0)
            mixture(0)
            symmetric()
            turn_norm(1)
            attention()
            turn_norm(2)
            router(1, wr1, E1)
            mixture(1)

        @block.scalar
        def _(act):
            chain = Chain(act, S["act_chain"])

            def roots(src, scale):
                act.activation(sd[:], src, ACT.Sqrt, bias=eps[:, 0:1], scale=scale).then_inc(S["sd_done"], 1)

            def graph_attention():
                FEAT, ZB = bank[0], bank[2:4]
                with act.Fori(0, TURNS) as i:
                    def prep(r):
                        act.wait_ge(S["feat_ready"], i * ROUNDS + r + 1)
                        act.activation(feat[:, r % 2, :, :, 0:GO],
                                       FEAT.rearrange("p (u h o) -> p u h o", u=NT, h=GH), ACT.Copy
                                       ).then_inc(S["feat_copied"], 1)

                    def leaky(k):
                        act.wait_ge(S["z_ready"], i * ALL + k + 1)
                        if k >= 2:
                            act.wait_ge(S["edge_done"], i * ALL + k - 1)
                        act.activation(lrelu[:, k % 2, :], ZB[k % 2][:], ACT.Copy, scale=-1.0
                                       ).then_inc(S["lrelu_done"], 1)

                    def exps(k):
                        act.wait_ge(S["edge_done"], i * ALL + k + 1)
                        if k >= 2:
                            act.wait_ge(S["alphaT_ready"], i * ALL + k - 1)
                        for h2 in range(2):
                            ins = act.activation(alpha[:, k % 2, h2 * N:h2 * N + N], edge[:, k % 2, h2 * N:h2 * N + N],
                                                 ACT.Exp, bias=edge_min[:, k % 2, h2:h2 + 1], scale=-1.0)
                        ins.then_inc(S["alpha_done"], 1)

                    def post(r, nt):
                        act.wait_ge(S["g_min"], i * 2 * ROUNDS + 2 * r + nt + 1)
                        act.activation(g_neg[:, nt, :], g_neg[:, nt, :], ACT.Exp).then_inc(S["g_exp"], 1)

                    for k in range(-1, LAST):
                        if (r := prep_at(k)) is not None:
                            prep(r)
                        if 0 <= k < ALL:
                            leaky(k)
                        if 0 <= k - 1 < ALL:
                            exps(k - 1)
                        if (q := post_at(k, 1)) is not None:
                            post(*q)

            def mixture(which):
                m = mix[which]
                IC = m["IC"]
                last = 2 * m["E"] - 2

                def high_parts(e, par):
                    act.wait_ge(expert_in[which][par], e * 24 + (48 - 24 * par))
                    if not isinstance(e, int) or e >= 2:
                        act.wait_ge(m["down"], e * 4 - 4)
                    I = IC * P
                    for w, r in ((gate_w[:, par, :, 0:I], gate_r[:, par, 0, :, 0:I]),
                                 (up_w[:, par, :, 0:I], up_r[:, par, 0, :, 0:I]),
                                 (down_w[:, par, 0:IC, :], down_r[:, par, 0, 0:IC, :])):
                        act.activation(r, w, ACT.Copy).then_inc(m["whi"], 1)

                act.wait_ge(S["rstd_done"], 2)
                high_parts(0, 0)

                def body(s, mod):
                    for ic in range(IC):
                        q = s * IC + ic
                        qp = (mod * IC + ic) % 2
                        act.wait_ge(m["gu"], q + 1)
                        if not isinstance(s, int) or q >= 2:
                            act.wait_ge(m["hid"], q - 1)
                        act.activation(silu[:, qp, :], bank[qp][:], ACT.Silu, scale=m["scale"]
                                       ).then_inc(m["silu"], 1)
                    if mod % 2 == 0 and (not isinstance(s, int) or s < last):
                        high_parts(s // 2 + 1, (mod // 2 + 1) % 2)

                expert_steps(act, 2 * m["E"], body)

            def squares(which):
                for t in range(T):
                    if which == 0:
                        act.wait_ge(S["y_done"], t + 1)
                    if which == 1 and t == 0:
                        act.wait_ge(S["wo_added"], KV * (T // 2))
                    chain.link(act.activation(sq[:], xs[:, t, :], ACT.Square, accum_out=mv[:, t, 0:1]))
                roots(mv[:, :, 0], 1.0 / D)

            def scaled_copy(which, w):
                for t in range(T):
                    act.wait_ge(S["normT_ready"], which * T + t + 1)
                    for c in range(HC):
                        ins = act.activation(actT[:, c, t * P:t * P + P], bank[t % 2][:, c * P:c * P + P],
                                             ACT.Copy, scale=lnw[:, w, c:c + 1])
                    ins.then_inc(S["normT_copied"], 1)

            def attention():
                act.wait_ge(S["att_in"], 48)

                def swap_halves(g, n):
                    for half in range(2):
                        act.wait_ge(S["q_ready"], g * PROJ + (2 * n + half + 1))
                        if n:
                            act.wait_ge(S["q_sin"], g * PROJ + (2 * n + half - 1))
                        act.activation(swap[0:64, half, :], Q_BANK[half][64:P, :], ACT.Copy)
                        act.activation(swap[64:P, half, :], Q_BANK[half][0:64, :], ACT.Copy).then_inc(S["q_swapped"], 1)

                def group(g, last):
                    def exps(k):
                        act.wait_ge(S["s_shift"], g * AU + (k + 1))
                        for nt in range(NT):
                            ins = act.activation(prob[:, k % 4, nt * P:nt * P + (nt + 1) * P],
                                                 prob[:, k % 4, nt * P:nt * P + (nt + 1) * P], ACT.Exp,
                                                 bias=pmin[:, k % 4, nt:nt + 1], scale=-1.0,
                                                 accum_out=psum_[:, k % 4, nt:nt + 1])
                        ins.then_inc(S["p_exp"], 1)

                    def copy_T(k):
                        act.wait_ge(S["pT_ready"], g * AU + (k + 1))
                        if k >= 2:
                            act.wait_ge(S["o_ready"], g * AU + (k - 1))
                        act.activation(probT[:, k % 2, :], PT_BANK[k % 2][:, 0:3 * P], ACT.Copy).then_inc(S["pT_copied"], 1)

                    for k in range(AU + 2):
                        if k < AU and k % B == 1 and k // B + 1 < REP:
                            swap_halves(g, k // B + 2)
                        if k < AU:
                            exps(k)
                        if 0 <= k - 2 < AU:
                            copy_T(k - 2)
                    if not last:
                        swap_halves(g + 1, 0)
                        swap_halves(g + 1, 1)

                swap_halves(0, 0)
                swap_halves(0, 1)
                with act.Fori(0, KV - 1) as g:
                    group(g, False)
                group(KV - 1, True)

            act.wait_ge(S["sim_in"], 64)
            act.wait_ge(S["zero_done"], 1)
            act.activation(gam[:, 1:2], gam[:, 0:1], ACT.Sigmoid).then_inc(S["gam_done"], 1)
            for t in range(T):
                act.wait_ge(S["sim_copied"], t + 1)
                act.activation(sig[:, t, :], sim[:, t, :], ACT.Sigmoid, scale=1.0 / 16).then_inc(S["sig_done"], 1)
            act.wait_ge(S["rstd_done"], 1)
            roots(mv[:, :, 1], 1.0)
            graph_attention()
            act.wait_ge(S["rstd_done"], 2)
            roots(mv[:, :, 1], 1.0)
            act.wait_ge(S["rmax_done"], 1)
            act.activation(route[:, 0, :, 0:E0], route[:, 0, :, 0:E0], ACT.Exp).then_inc(S["rexp_done"], 1)
            mixture(0)
            act.wait_ge(S["rstd_done"], 3)
            roots(mv[:, :, 1], 1.0)
            act.wait_ge(S["rstd_done"], 4)
            roots(mv[:, :, 1], 1.0)
            squares(0)
            scaled_copy(1, 0)
            attention()
            squares(1)
            scaled_copy(2, 1)
            act.wait_ge(S["logit_ready"], 2)
            act.activation(route[:, 0, :, :], bank[2][:, 0:T * E1].rearrange("p (t e) -> p t e", t=T),
                           ACT.Sigmoid).then_inc(S["rexp_done"], 1)
            mixture(1)

        @block.gpsimd
        def _(pool):
            chain = Chain(pool, S["pool_chain"])
            def signal(ins, name, count):
                ins.then_inc(S[name], 1)
                pool.wait_ge(S[name], count)
                pool.sem_inc(S["pool_held"])

            pool.wait_ge(S["gat_in"], 16 * 13)
            with pool.Fori(0, TURNS) as i:
                chain.restart()
                link = chain.link

                def prep(r):
                    layer, p = divmod(r, 2)
                    if layer == 0:
                        pool.wait_ge(S["adj_ready"], i * 2 + p + 1)
                        pool.sem_inc(S["pool_held"])
                        for nt in range(NT):
                            link(pool.tensor_scalar(adj[:, p, nt, :], adj[:, p, nt, :], -1.0, 1.0, ALU.mult, ALU.add))
                            ins = pool.tensor_scalar(adj[:, p, nt, :], adj[:, p, nt, :], MASK, None, ALU.mult)
                            signal(ins, "adj_bias", i * 4 + (2 * r + nt + 1))
                    pool.wait_ge(S["st_copied"], i * ROUNDS + r + 1)
                    signal(pool.tensor_tensor(
                        zl_r[TROW:ZK, p, :].rearrange("k (h m) -> k h m", h=GH),
                        bcast(t_row[TROW:ZK, :], 1, GH),
                        delta[TROW:ZK, :].rearrange("k (h m) -> k h m", h=GH), ALU.mult),
                        "r_ready", i * ROUNDS + (r + 1))

                def before_exp(r, nt):
                    pool.wait_ge(S["g_norm"], i * 2 * ROUNDS + 2 * r + nt + 1)
                    pool.sem_inc(S["pool_held"])
                    link(pool.tensor_tensor(g_out[:, nt, :], g_out[:, nt, :], bvec[:, r // 2, :], ALU.add))
                    signal(pool.tensor_scalar(g_neg[:, nt, :], g_out[:, nt, :], 0.0, None, ALU.min),
                           "g_min", i * 2 * ROUNDS + (2 * r + nt + 1))
                    link(pool.tensor_scalar(g_pos[:, nt, :], g_out[:, nt, :], 0.0, -1.0, ALU.max, ALU.add))

                def after_exp(r, nt):
                    layer, p = divmod(r, 2)
                    pool.wait_ge(S["g_exp"], i * 2 * ROUNDS + 2 * r + nt + 1)
                    if layer == 0:
                        signal(pool.tensor_tensor(h1[:, nt, :], g_pos[:, nt, :], g_neg[:, nt, :], ALU.add),
                               "h1_done", i * 2 * ROUNDS + (2 * r + nt + 1))
                    else:
                        link(pool.tensor_tensor(g_pos[:, nt, :], g_pos[:, nt, :], g_neg[:, nt, :], ALU.add))
                        row = xs[:, bass.ds(i * 4 + (2 * p + nt), 1), :].rearrange("p u c -> p (u c)")
                        signal(pool.tensor_tensor(row, row, g_pos[:, nt, :], ALU.add),
                               "h1_done", i * 2 * ROUNDS + (2 * r + nt + 1))

                for k in range(-1, LAST):
                    if (r := prep_at(k)) is not None:
                        prep(r)
                    if (q := post_at(k, 0)) is not None:
                        before_exp(*q)
                    if (q := post_at(k, 1)) is not None:
                        after_exp(*q)
            chain.restart()
            def low_parts(which):
                m = mix[which]
                I = m["IC"] * P

                def expert(e, par):
                    for j, (w, r) in enumerate(((gate_w[:, par, :, 0:I], gate_r[:, par, :, :, 0:I]),
                                                (up_w[:, par, :, 0:I], up_r[:, par, :, :, 0:I]),
                                                (down_w[:, par, 0:m["IC"], :], down_r[:, par, :, 0:m["IC"], :]))):
                        pool.wait_ge(m["whi"], e * 3 + (j + 1))
                        ins = pool.tensor_tensor(r[:, 1], w, r[:, 0].bitcast(F32), ALU.subtract)
                        ins.then_inc(m["wlo"], 1)

                pairs = m["E"] // 2
                with pool.Fori(0, pairs) as i:
                    for par in range(2):
                        expert(i * 2 + par, par)
                for e in range(2 * pairs, m["E"]):
                    expert(e, e % 2)

            low_parts(0)
            pool.wait_ge(S["att_in"], 48)
            with pool.Fori(0, KV) as g:
                for n in range(REP + 1):
                    tab = rk if n == 0 else rq
                    for half in range(2):
                        pool.wait_ge(S["q_swapped"], g * PROJ + (2 * n + half + 1))
                        if n:
                            pool.wait_ge(S["q_rot"], g * PROJ + (2 * n + half - 1))
                        signal(pool.tensor_tensor(rot_s[:, half].rearrange("p (b n) -> p b n", b=2),
                                                  swap[:, half].rearrange("p (b n) -> p b n", b=2),
                                                  bcast(tab[:, 1, :], 1, 2), ALU.mult),
                               "q_sin", g * PROJ + (2 * n + half + 1))
            low_parts(1)

        @block.vector
        def _(dve):
            chain = Chain(dve, S["dve_chain"])

            def statistics(src):
                for t in range(T):
                    dve.bn_stats(stats[:, t, :], src[:, t, :])
                chain.link(dve.engine_nop())
                for t in range(T):
                    ins = dve.bn_aggr(mv[:, t, :], stats[:, t, :])
                ins.then_inc(S["rstd_done"], 1)

            def inverses(n):
                dve.wait_ge(S["sd_done"], n + 1)
                chain.link(dve.reciprocal(rstd[:], sd[:]))

            def layer_norm_tile(dst, t, src=xs):
                return dve.tensor_scalar(dst, src[:, t, :], mv[:, t, 0:1], rstd[:, t:t + 1], ALU.subtract, ALU.mult)

            def prepare_vectors():
                dve.wait_ge(S["gat_in"], 16 * 13)
                chain.link(dve.memset(wa0[:], 0.0))
                chain.link(dve.memset(wa1[:], 0.0))
                for j in range(2):
                    chain.link(dve.tensor_tensor(wa_tmp[0:FC, j, :], w0[:], avec[0:FC, j, :], ALU.mult))
                    chain.link(dve.tensor_reduce(wa0[:, TROW * j:TROW * j + GH], wa_tmp[0:FC, j, :].rearrange(
                        "p (h o) -> p h o", h=GH), X, ALU.add))
                    for c in range(HC):
                        chain.link(dve.tensor_tensor(wa_tmp[:, 2 + 2 * c + j, :], w1[:, c, :], avec[:, 2 + j, :], ALU.mult))
                        chain.link(dve.tensor_reduce(wa1[:, c, TROW * j:TROW * j + GH], wa_tmp[:, 2 + 2 * c + j, :].rearrange(
                            "p (h o) -> p h o", h=GH), X, ALU.add))
                dve.memset(feat[:, :, :, :, GO:GO + 1], 1.0).then_inc(S["wa_done"], 1)

            def graph_attention():
                MISC, PTB, OB = bank[1], bank[4:6], bank[6:8]
                with dve.Fori(0, TURNS) as i:
                    chain.restart()

                    def prep(r):
                        layer, p = divmod(r, 2)
                        if layer == 0:
                            for nt in range(NT):
                                t = i * 4 + (2 * p + nt)
                                ins = dve.tensor_scalar(
                                    adj[:, p, nt, :], xs[:, bass.ds(t, 1), :].rearrange("p u c -> p (u c)"),
                                    mv[:, bass.ds(t, 1), 0:1].rearrange("p u c -> p (u c)"), rstd[:, bass.ds(t, 1)],
                                    ALU.subtract, ALU.mult)
                            ins.then_inc(S["adj_ready"], 1)
                        dve.wait_ge(S["st_ready"], i * ROUNDS + r + 1)
                        if r >= 1:
                            dve.wait_ge(S["r_ready"], i * ROUNDS + r)
                        dve.tensor_copy(zl_l[0:GH, p, :], MISC[0:GH, 0:N])
                        dve.tensor_copy(t_row[TROW:ZK, :], MISC[TROW:ZK, 0:N]).then_inc(S["st_copied"], 1)

                    def edges(k):
                        r, u = divmod(k, UNITS)
                        nt = u // (GH // 2)
                        dve.wait_ge(S["lrelu_done"], i * ALL + k + 1)
                        if u == 0 and r < 2:
                            dve.wait_ge(S["adj_bias"], i * 4 + 2 * r + 2)
                        if k >= 2:
                            dve.wait_ge(S["alpha_done"], i * ALL + k - 1)
                        chain.link(dve.scalar_tensor_tensor(lrelu[:, k % 2, :], lrelu[:, k % 2, :], NEG,
                                                            lrelu[:, k % 2, :], ALU.mult, ALU.min))
                        for h2 in range(2):
                            ins = dve.tensor_tensor_reduce(
                                out=edge[:, k % 2, h2 * N:h2 * N + N], in0=lrelu[:, k % 2, h2 * N:h2 * N + N],
                                in1=adj[:, r % 2, nt, :], scale=1.0, scalar=3.0e38, op0=ALU.add, op1=ALU.min,
                                accum_out=edge_min[:, k % 2, h2:h2 + 1])
                        ins.then_inc(S["edge_done"], 1)

                    def copy_T(k):
                        dve.wait_ge(S["alphaT_ready"], i * ALL + k + 1)
                        if k >= 2:
                            dve.wait_ge(S["av_done"], i * ALL + k - 1)
                        dve.tensor_copy(alphaT[:, k % 2, :], PTB[k % 2][:]).then_inc(S["alphaT_copied"], 1)

                    def post(r, nt):
                        o = OB[nt][:, 0:GH * (GO + 1)].rearrange("p (h o) -> p h o", h=GH)
                        dve.wait_ge(S["av_done"], i * ALL + r * UNITS + 4 * nt + 4)
                        chain.link(dve.reciprocal(rsum[:, nt, :], o[:, :, GO]))
                        if r >= 1:
                            dve.wait_ge(S["h1_done"], i * 2 * ROUNDS + 2 * (r - 1) + nt + 1)
                        dve.tensor_tensor(g_out[:, nt, :].rearrange("p (h o) -> p h o", h=GH), o[:, :, 0:GO],
                                          bcast(rsum[:, nt, :], 2, GO), ALU.mult).then_inc(S["g_norm"], 1)

                    def copy_h1T(r, nt):
                        if r >= 2:
                            return
                        dve.wait_ge(S["h1T_ready"], i * 4 + 2 * r + nt + 1)
                        dve.tensor_copy(h1T[:, r, :, nt * P:nt * P + P], MISC[:, N:2 * N].rearrange(
                            "p (c n) -> p c n", c=HC)).then_inc(S["h1T_copied"], 1)

                    for k in range(-1, LAST):
                        if (r := prep_at(k)) is not None:
                            prep(r)
                        if 0 <= k < ALL:
                            edges(k)
                        if 0 <= k - 2 < ALL:
                            copy_T(k - 2)
                        if (q := post_at(k, 0)) is not None:
                            post(*q)
                        if (q := post_at(k, 2)) is not None:
                            copy_h1T(*q)
                    dve.wait_ge(S["h1_done"], i * 2 * ROUNDS + 2 * ROUNDS)
                chain.restart()

            def router0():
                R = lambda j: route[:, j, :, 0:E0]
                logits = bank[2][:, 0:T * E0].rearrange("p (t e) -> p t e", t=T)
                dve.wait_ge(S["logit_ready"], 1)
                chain.link(dve.tensor_reduce(rcol[:, 0, :], logits, X, ALU.max))
                dve.tensor_tensor(R(0), logits, bcast(rcol[:, 0, :], 2, E0), ALU.subtract).then_inc(S["rmax_done"], 1)
                dve.wait_ge(S["rexp_done"], 1)
                chain.link(dve.tensor_reduce(rcol[:, 1, :], R(0), X, ALU.add))
                chain.link(dve.reciprocal(rcol[:, 2, :], rcol[:, 1, :]))
                chain.link(dve.memset(padded[:], -1.0))
                chain.link(dve.tensor_tensor(padded[:, :, 0:E0], R(0), bcast(rcol[:, 2, :], 2, E0), ALU.mult))
                for t in range(T):
                    chain.link(dve.max(rtop[:, t, :], padded[:, t, 0:8]))
                chain.link(dve.memset(rtop[:, :, K0:8], -1.0))
                for t in range(T):
                    chain.link(dve.match_replace(kept[:, t, :], rtop[:, t, :], padded[:, t, :], -2.0))
                chain.link(dve.tensor_tensor(R(1), kept[:, :, 0:E0], padded[:, :, 0:E0], ALU.not_equal))
                chain.link(dve.scalar_tensor_tensor(wt0.rearrange("p e t -> p t e"), R(1), 0.25,
                                                    padded[:, :, 0:E0], ALU.mult, ALU.mult))

            def router1():
                dve.wait_ge(S["rexp_done"], 2)
                chain.link(dve.tensor_tensor(route[:, 1], route[:, 0], bcast(eb[:], 1, T), ALU.add))
                for t in range(T):
                    chain.link(dve.max(rtop[:, t, :], route[:, 1, t, :]))
                    chain.link(dve.match_replace(route[:, 2, t, :], rtop[:, t, :], route[:, 1, t, :], -3.0e38))
                chain.link(dve.tensor_tensor(route[:, 3], route[:, 2], route[:, 1], ALU.not_equal))
                chain.link(dve.tensor_tensor(route[:, 4], route[:, 3], route[:, 0], ALU.mult))
                chain.link(dve.tensor_reduce(rcol[:, 0, :], route[:, 4], X, ALU.add))
                chain.link(dve.reciprocal(rcol[:, 1, :], rcol[:, 0, :]))
                dve.memset(wt1[:, E1, :], 1.0)
                chain.link(dve.tensor_tensor(wt1[:, 0:E1, :].rearrange("p e t -> p t e"), route[:, 4],
                                             bcast(rcol[:, 1, :], 2, E1), ALU.mult))
                chain.link(dve.engine_nop())

            def keep_top(e, part):
                row = (lambda a: a[:, e, :]) if isinstance(e, int) else \
                    (lambda a: a[:, bass.ds(e, 1), :].rearrange("p u c -> p (u c)"))
                parts, rounds = 2 * I0 // P, TOPK // 8
                if part == 0:
                    chain.restart()
                    chain.link(dve.tensor_copy(work[:], row(sim)))
                for r in range(part, rounds if part == parts - 1 else part + 1):
                    chain.link(dve.max(top8[:], work[:]))
                    chain.link(dve.match_replace(work[:], top8[:], work[:], -3.0e38))
                if part == parts - 1:
                    chain.link(dve.max(top8[:], work[:]))
                    rest = TOPK % 8
                    chain.link(dve.scalar_tensor_tensor(row(sig), row(sim), top8[:, rest - 1:rest], row(sig),
                                                        ALU.is_ge, ALU.mult))

            def mixture(which):
                m = mix[which]
                IC, wt = m["IC"], m["wt"]
                DB = bank[4:8]

                def multiply(s, mod):
                    if not isinstance(s, int) or s >= 2:
                        dve.wait_ge(m["down"], s * 2 - 2)
                    for ic in range(IC):
                        qp = (mod * IC + ic) % 2
                        dve.wait_ge(m["silu"], s * IC + (ic + 1))
                        dve.tensor_tensor(hidf[:, qp, :], silu[:, qp, :], bank[2 + qp][:], ALU.mult
                                          ).then_inc(m["hidf"], 1)
                        dve.wait_ge(m["hidf"], s * IC + (ic + 1))
                        dve.tensor_copy(hidT[:, mod % 2, 0, ic, :], hidf[:, qp, :]).then_inc(m["hidh"], 1)
                        dve.wait_ge(m["hidh"], s * IC + (ic + 1))
                        dve.tensor_tensor(hidT[:, mod % 2, 1, ic, :], hidf[:, qp, :],
                                          hidT[:, mod % 2, 0, ic, :].bitcast(F32), ALU.subtract
                                          ).then_inc(m["hid"], 1)
                        if which == 0:
                            keep_top(s // 2 if isinstance(s, int) else (s - mod % 2) // 2, mod % 2 * IC + ic)

                def add(s, mod):
                    e = s // 2 if isinstance(s, int) else None
                    for j in range(4):
                        t = 4 * (mod % 2) + j
                        if j % 2 == 0:
                            dve.wait_ge(m["down"], s * 2 + (j // 2 + 1))
                        if j == 0 and (e is None or s >= 2):
                            dve.wait_ge(m["acc"], s * 2 - 2)
                        if e is not None:
                            w = wt[:, e, t:t + 1]
                        else:
                            w = wt[:, bass.ds((s - (mod % 2)) // 2, 1), t:t + 1].rearrange("p e t -> p (e t)")
                        ins = dve.scalar_tensor_tensor(xs[:, t, :], DB[2 * (mod % 2) + j // 2][:, j % 2 * D:j % 2 * D + D],
                                                       w, xs[:, t, :], ALU.mult, ALU.add)
                        if j % 2 == 1:
                            ins.then_inc(m["acc"], 1)

                steps = 2 * m["E"]
                dve.wait_ge(S["normT_copied"], (1 + 2 * which) * T)
                dve.tensor_copy(actT_r[:, 0], actT[:]).then_inc(S["actT_hi"], 1)
                dve.wait_ge(S["actT_hi"], which + 1)
                dve.tensor_tensor(actT_r[:, 1], actT[:], actT_r[:, 0].bitcast(F32), ALU.subtract
                                  ).then_inc(S["actT_lo"], 1)
                multiply(0, 0)

                def body(s, mod):
                    if not isinstance(s, int) or s + 1 < steps:
                        multiply(s + 1, (mod + 1) % 4)
                    add(s, mod)

                expert_steps(dve, steps, body)

            def normalised(which, subtract):
                for t in range(T):
                    if which * T + t >= 2:
                        dve.wait_ge(S["normT_ready"], which * T + t - 1)
                    if subtract:
                        ins = layer_norm_tile(norm[:, t % 2, :], t)
                    else:
                        ins = dve.tensor_scalar(norm[:, t % 2, :], xs[:, t, :], rstd[:, t:t + 1], None, ALU.mult)
                    ins.then_inc(S["norm_done"], 1)
                    if subtract and t >= 1:
                        copy_norm(which, t - 1)
                if subtract:
                    copy_norm(which, T - 1)

            def copy_norm(which, t):
                dve.wait_ge(S["normT_ready"], which * T + t + 1)
                dve.tensor_copy(actT[:, :, t * P:t * P + P], bank[t % 2][:, 0:D].rearrange("p (c n) -> p c n", c=HC)
                                ).then_inc(S["normT_copied"], 1)

            def third():
                dve.wait_ge(S["gam_done"], 1)
                chain.link(dve.tensor_scalar(gam[:, 2:3], gam[:, 1:2], 0.5, None, ALU.mult))
                chain.link(dve.tensor_scalar(gam[:, 3:4], gam[:, 1:2], -1.0, 1.0, ALU.mult, ALU.add))
                for t in range(T):
                    chain.link(layer_norm_tile(sym[:, 0, :], t))
                    chain.link(dve.scalar_tensor_tensor(xs[:, t, :], sym[:, 0, :], gam[:, 3:4], xs[:, t, :],
                                                        ALU.mult, ALU.add))
                    dve.wait_ge(S["aT_ready"], t + 1)
                    chain.link(dve.tensor_tensor(sym[:, 1, :], bank[2 + t % 2][:, 0:N], sig[:, t, :], ALU.add))
                    dve.scalar_tensor_tensor(x3[:, t, :], sym[:, 1, :], gam[:, 2:3], xs[:, t, :],
                                             ALU.mult, ALU.add).then_inc(S["x3_done"], 1)

            def attention():
                dve.wait_ge(S["att_in"], 48)

                def cosines(g, n):
                    tab = rk if n == 0 else rq
                    for half in range(2):
                        dve.wait_ge(S["q_swapped"], g * PROJ + (2 * n + half + 1))
                        if n:
                            dve.wait_ge(S["q_rot"], g * PROJ + (2 * n + half - 1))
                        dve.tensor_tensor(rot_c[:, half].rearrange("p (b n) -> p b n", b=2),
                                          Q_BANK[half].rearrange("p (b n) -> p b n", b=2),
                                          bcast(tab[:, 0, :], 1, 2), ALU.mult).then_inc(S["q_cos"], 1)

                def rotate(g, n):
                    for half in range(2):
                        dve.wait_ge(S["q_cos"], g * PROJ + (2 * n + half + 1))
                        dve.wait_ge(S["q_sin"], g * PROJ + (2 * n + half + 1))
                        dst = kT[:, half * 512:half * 512 + 512] if n == 0 else \
                            qT[:, (n - 1) % 2, half * 512:half * 512 + 512]
                        dve.tensor_tensor(dst, rot_c[:, half], rot_s[:, half], ALU.add).then_inc(S["q_rot"], 1)

                def copy_values(g):
                    for half in range(2):
                        dve.wait_ge(S["v_ready"], g * 2 + (half + 1))
                        dve.tensor_copy(vt[:, 4 * half:4 * half + 4, :], S_BANK[half].rearrange(
                            "p (t n) -> p t n", t=4)).then_inc(S["v_copied"], 1)

                def group(g, last):
                    def shift(k):
                        dve.wait_ge(S["s_ready"], g * AU + (k + 1))
                        if k >= 4:
                            dve.wait_ge(S["pT_ready"], g * AU + (k - 3))
                        dve.sem_inc(S["dve_held"])
                        for nt in range(NT):
                            ins = dve.tensor_tensor_reduce(
                                out=prob[:, k % 4, nt * P:nt * P + (nt + 1) * P],
                                in0=S_BANK[k % 2][:, nt * P:nt * P + (nt + 1) * P],
                                in1=causal[:, P - nt * P:2 * P], scale=1.0, scalar=3.0e38, op0=ALU.add, op1=ALU.min,
                                accum_out=pmin[:, k % 4, nt:nt + 1])
                        ins.then_inc(S["s_shift"], 1)

                    def normalise(k):
                        dve.wait_ge(S["p_exp"], g * AU + (k + 1))
                        dve.reciprocal(pinv[:, k % 4, :], psum_[:, k % 4, :]).then_inc(S["p_inv"], 1)
                        dve.wait_ge(S["p_inv"], g * AU + (k + 1))
                        for nt in range(NT):
                            ins = dve.tensor_scalar(prob[:, k % 4, nt * P:nt * P + (nt + 1) * P],
                                                    prob[:, k % 4, nt * P:nt * P + (nt + 1) * P],
                                                    pinv[:, k % 4, nt:nt + 1], None, ALU.mult)
                        ins.then_inc(S["p_norm"], 1)

                    def copy_out(k):
                        h, b = divmod(k, B)
                        dve.wait_ge(S["o_ready"], g * AU + (k + 1))
                        dve.tensor_copy(oT[:, h, b * N:b * N + N], O_BANK[k % 2][:, 0:N]).then_inc(S["o_copied"], 1)

                    def add_out(j):
                        dve.wait_ge(S["wo_ready"], g * (T // 2) + (j + 1))
                        rows = xs[:, 2 * j:2 * j + 2, :]
                        dve.tensor_tensor(rows, PT_BANK[j % 2].rearrange("p (t c) -> p t c", t=2), rows,
                                          ALU.add).then_inc(S["wo_added"], 1)

                    for k in range(AU + 3):
                        if k < AU and k // B + 1 < REP:
                            if k % B == 2:
                                cosines(g, k // B + 2)
                            if k % B == 3:
                                rotate(g, k // B + 2)
                        if k < AU:
                            shift(k)
                        if 0 <= k - 1 < AU:
                            normalise(k - 1)
                        if 0 <= k - 3 < AU:
                            copy_out(k - 3)
                    if not last:
                        cosines(g + 1, 0)
                        copy_values(g + 1)
                        rotate(g + 1, 0)
                    add_out(0)
                    add_out(1)
                    if not last:
                        cosines(g + 1, 1)
                        rotate(g + 1, 1)
                    add_out(2)
                    add_out(3)

                cosines(0, 0)
                copy_values(0)
                rotate(0, 0)
                cosines(0, 1)
                rotate(0, 1)
                with dve.Fori(0, KV - 1) as g:
                    group(g, False)
                group(KV - 1, True)

            dve.memset(eps[:], EPS).then_inc(S["zero_done"], 1)
            for j in range(2):
                for half in range(2):
                    dve.wait_ge(S["qk_ready"], 2 * j + half + 1)
                    dve.tensor_copy(qkT[:, j, 512 * half:512 * half + 512], bank[half][0:FC, :]).then_inc(S["qk_copied"], 1)
            for t in range(T):
                dve.wait_ge(S["sim_ready"], t + 1)
                dve.tensor_copy(sim[:, t, :], bank[2 + t % 4][:, 0:N]).then_inc(S["sim_copied"], 1)
            dve.wait_ge(S["x_in"], 16)
            statistics(xs)
            prepare_vectors()
            inverses(0)
            graph_attention()
            statistics(xs)
            inverses(1)
            normalised(0, True)
            router0()
            dve.wait_ge(S["sig_done"], T)
            mixture(0)
            dve.wait_ge(S["acc0"], 4 * E0)
            statistics(xs)
            inverses(2)
            third()
            dve.wait_ge(S["x3_done"], T)
            statistics(x3)
            inverses(3)
            for t in range(T):
                layer_norm_tile(xs[:, t, :], t, x3).then_inc(S["y_done"], 1)
            inverses(4)
            normalised(1, False)
            attention()
            inverses(5)
            dve.wait_ge(S["wo_added"], KV * (T // 2))
            normalised(2, False)
            dve.wait_ge(S["rexp_done"], 2)
            dve.engine_nop().then_inc(S["rmax_done"], 1)
            chain.link(dve.tensor_tensor(xs[:], xs[:], x3[:], ALU.add))
            router1()
            mixture(1)


def kernel(**inputs):
    import concourse.bacc as bacc
    from concourse.bass_utils import run_bass_kernel_spmd

    a = {k: np.asarray(v) for k, v in inputs.items()}
    flat = lambda name: a[name].reshape(-1)
    heads_last = lambda w: np.transpose(w, (1, 0, 2)).reshape(w.shape[1], -1)

    pos = np.arange(N, dtype=np.float32)
    inv = (1.0 / 10000.0 ** (np.arange(0, HD, 2, dtype=np.float32) / HD)).astype(np.float32)
    ang = (pos[:, None] * inv[None, :]).astype(np.float32).T
    cos, sin = np.cos(ang), np.sin(ang)
    rope_k = np.stack([np.concatenate([cos, cos]), np.concatenate([-sin, sin])], 1).astype(np.float32)
    rope_q = (rope_k * np.float32(-1.0 / np.sqrt(HD))).astype(np.float32)
    causal = np.zeros((P, 2 * P), np.float32)
    causal[:, P:] = np.triu(np.full((P, P), 1e9, np.float32), 1)
    r_init = np.zeros((ZK, GH, N), np.float32)
    delta = np.zeros((ZK, GH, N), np.float32)
    for h in range(GH):
        r_init[h, h] = 1.0
        delta[TROW + h, h] = 1.0
    l_init = np.zeros((ZK, N), np.float32)
    l_init[TROW:] = 1.0

    arrays = dict(
        x=a["x"], ctxT=np.transpose(a["ctx_512"], (2, 0, 1)),
        W0=heads_last(a["L0_xattn_W0"]), W1=heads_last(a["L0_xattn_W1"]),
        a_self0=flat("L0_xattn_a_self0"), a_neigh0=flat("L0_xattn_a_neigh0"), b0=flat("L0_xattn_b0"),
        a_self1=flat("L0_xattn_a_self1"), a_neigh1=flat("L0_xattn_a_neigh1"), b1=flat("L0_xattn_b1"),
        w_router=a["L0_ffn_w_router"], w_gate=a["L0_ffn_w_gate"], w_up=a["L0_ffn_w_up"],
        w_down=a["L0_ffn_w_down"], WqT=a["L1_xattn_Wq"].T, WkT=a["L1_xattn_Wk"].T,
        gamma=flat("L1_xattn_gamma_raw"), ln1=a["L1_ffn_ln1_w"].reshape(HC, P).T,
        ln2=a["L1_ffn_ln2_w"].reshape(HC, P).T, Wq=a["L1_ffn_Wq"], Wk=a["L1_ffn_Wk"],
        Wv=a["L1_ffn_Wv"], Wo=a["L1_ffn_Wo"], Wr=a["L1_ffn_Wr"], ebias=a["L1_ffn_expert_bias"],
        Wg=np.concatenate([a["L1_ffn_Wg"], a["L1_ffn_Wsg"][None]]),
        Wu=np.concatenate([a["L1_ffn_Wu"], a["L1_ffn_Wsu"][None]]),
        Wd=np.concatenate([a["L1_ffn_Wd"], a["L1_ffn_Wsd"][None]]),
        ident_in=np.eye(P, dtype=np.float32), r_init=r_init.reshape(ZK, -1),
        delta_in=delta.reshape(ZK, -1), l_init=l_init, rope_q=rope_q, rope_k=rope_k, causal_in=causal)

    nc = bacc.Bacc("TRN2", target_bir_lowering=False, num_devices=1)
    feeds, args = {}, {}
    for name, v in arrays.items():
        v = np.ascontiguousarray(v)
        feeds[f"in_{name}"] = v
        args[name] = nc.dram_tensor(f"in_{name}", v.shape, mybir.dt.from_np(v.dtype), kind="ExternalInput").ap()
    args["out"] = nc.dram_tensor("out_0", (B, N, D), F32, kind="ExternalOutput").ap()
    build(nc, **args)
    r = run_bass_kernel_spmd(nc, [feeds], core_ids=[0])
    return r.results[0]["out_0"]
```

```python
from contextlib import ExitStack

import numpy as np
import concourse.bass as bass
from concourse import mybir

P = 128
B, N, D = 4, 256, 256
T = B * N // P
NT = N // P
HC = D // P
FC = 64
GH, GO = 8, 32
E0, I0, K0 = 8, 512, 2
E1, I1, K1 = 32, 128, 8
TOPK = int(N * 0.3)
NH, KV, HD = 32, 4, 128
REP = NH // KV
EPS = 1e-5
MASK = 1e10
NEG = 0.2
ROW = 32
TR = ROW + 8
QUAD = 4

F32 = mybir.dt.float32
F32R = mybir.dt.float32r
ALU = mybir.AluOpType
ACT = mybir.ActivationFunctionType
X = mybir.AxisListType.X


def split_product(pe, out, lhs, rhs, first, last):
    pe.matmul(out, lhs[0], rhs[0], start=first, stop=False)
    pe.matmul(out, lhs[0], rhs[1], start=False, stop=False)
    return pe.matmul(out, lhs[1], rhs[0], start=False, stop=last)


def bcast(ap, where, count):
    return ap.unsqueeze(where).to_broadcast(
        list(ap.shape[:where]) + [count] + list(ap.shape[where:]))


class Chain:

    def __init__(self, eng, sem):
        self.eng, self.sem, self.n = eng, sem, 0

    def link(self, ins):
        self.n += 1
        ins.then_inc(self.sem, 1)
        self.eng.wait_ge(self.sem, self.n)

    def restart(self):
        self.eng.sem_clear(self.sem)
        self.n = 0


def expert_steps(eng, steps, body):
    body(0, 0)
    body(1, 1)
    turns = (steps - 3) // 4
    with eng.Fori(0, turns) as i:
        for m in range(4):
            body(i * 4 + (2 + m), (2 + m) % 4)
    for s in range(2 + 4 * turns, steps):
        body(s, s % 4)


def build(nc, x, ctxT, W0, W1, a_self0, a_neigh0, a_self1, a_neigh1, b01,
          w_router, w_gate, w_up, w_down, WqT, WkT, gamma, ln1, ln2, Wq, Wk, Wv, Wo, Wr, ebias,
          Wg, Wu, Wd, ident_in, ind_in, rope_q, rope_k, causal_in, out):
    with ExitStack() as ctx:
        def sb(name, shape, dt=F32):
            return ctx.enter_context(nc.sbuf_tensor(name, shape, dt))

        def sem(name):
            return ctx.enter_context(nc.semaphore(name))

        bank = [ctx.enter_context(nc.psum_tensor(f"bank{i}", [P, 512], F32)) for i in range(8)]

        xs = sb("xs", [P, T, D])
        actT = sb("actT", [P, HC, B * N])
        actT_r = sb("actT_r", [P, 2, HC, B * N], F32R)
        norm = sb("norm", [P, 2, D])
        ident = sb("ident", [P, P])
        stats = sb("stats", [P, T, 6])
        mv = sb("mv", [P, T, 2])
        sd = sb("sd", [P, T])
        rstd = sb("rstd", [P, T])
        ymean = sb("ymean", [P, T])
        rstd3 = sb("rstd3", [P, T])
        eps = sb("eps", [P, 1])
        sq = sb("sq", [P, D])
        lnw = sb("lnw", [P, 2, HC])

        rq = sb("rq", [P, 2, N])
        rk = sb("rk", [P, 2, N])
        causal = sb("causal", [P, 2 * P])
        wqk = sb("wqk", [FC, 2, FC])
        sim = sb("sim", [P, T, N])
        x3 = sim
        work = sb("work", [P, N])
        top8 = sb("top8", [P, 8])
        gam = sb("gam", [P, 4])

        route = sb("route", [P, 6, T, E1])
        rcol = sb("rcol", [P, 4, T])
        padded = sb("padded", [P, T, 16])
        kept = sb("kept", [P, T, 16])
        rtop = sb("rtop", [P, T, 8])
        wt0 = sb("wt0", [P, E0, T])
        wt1 = sb("wt1", [P, E1 + 1, T])
        wr0 = sb("wr0", [P, HC, E0])
        wr1 = sb("wr1", [P, HC, E1])
        eb = sb("eb", [P, E1])
        incoming = ctx.enter_context(ExitStack())
        gate_w = incoming.enter_context(nc.sbuf_tensor("gate_w", [P, 2, HC, I0], F32))
        up_w = incoming.enter_context(nc.sbuf_tensor("up_w", [P, 2, HC, I0], F32))
        down_w = incoming.enter_context(nc.sbuf_tensor("down_w", [P, 2, I0 // P, D], F32))
        incoming.close()
        wqk_r = sb("wqk_r", [P, 2, HC, (REP + 1) * HD], F32R)
        swap = sb("swap", [P, 2, 512])
        wk_g = sb("wk_g", [P, HC, HD])
        wv_g = sb("wv_g", [P, HC, HD])

        resting = ctx.enter_context(ExitStack())

        def sb_resting(name, shape):
            return resting.enter_context(nc.sbuf_tensor(name, shape, F32))

        ctx_all = sb_resting("ctx_all", [FC, B * N])
        qkT = sb_resting("qkT", [FC, 2, B * N])
        sig = sb_resting("sig", [P, T, N])
        silu = sb_resting("silu", [P, 2, 512])
        hidf = sb_resting("hidf", [P, 2, 512])
        resting.close()
        o_parts = [sb(f"o_part{j}", [P, B * N], F32R) for j in range(7)]

        early = ctx.enter_context(ExitStack())

        def sb_early(name, shape, dt=F32):
            return early.enter_context(nc.sbuf_tensor(name, shape, dt))

        ctx_b = sb_early("ctx_b", [FC, 2, N])
        w0 = sb_early("w0", [FC, D])
        w1 = sb_early("w1", [P, HC, D])
        avec = sb_early("avec", [P, 4, D])
        bT = sb_early("bT", [P, 2, HC])
        bT1 = sb_early("bT1", [P, 2, HC])
        wa_tmp = sb_early("wa_tmp", [P, 6, D])
        was0 = sb_early("was0", [FC, GH])
        wat0 = sb_early("wat0", [FC, TR])
        was1 = sb_early("was1", [P, HC, GH])
        wat1 = sb_early("wat1", [P, HC, TR])
        ind_f = sb_early("ind_f", [TR, GH, P])
        ind = sb_early("ind", [TR, GH, P], F32R)
        neg_s = sb_early("neg_s", [P, 2, NT, GH])
        t_parts = sb_early("t_parts", [TR, 2, N], F32R)
        feat = sb_early("feat", [P, 2, NT, D])
        adj = sb_early("adj", [P, 2, NT, N])
        lrelu = sb_early("lrelu", [P, 2, 2 * N])
        edge = sb_early("edge", [P, 2, 2 * N])
        edge_min = sb_early("edge_min", [P, 2, 2])
        alpha = sb_early("alpha", [P, 2, 2 * N])
        alphaT = sb_early("alphaT", [P, 2, QUAD, NT, N])
        sums = sb_early("sums", [P, 2, NT, QUAD])
        rsum = sb_early("rsum", [P, NT, QUAD])
        rsum_w = sb_early("rsum_w", [P, 2, NT, QUAD, GO])
        g_scale = sb_early("g_scale", [P, 2, N])
        g_out = sb_early("g_out", [P, 2, N])
        g_exp = sb_early("g_exp", [P, 2, N])
        g_pos = sb_early("g_pos", [P, 2, N])
        h1T = sb_early("h1T", [P, 2, HC, N])
        x1T = sb_early("x1T", [P, 2, HC, N])
        early.close()

        parts = ctx.enter_context(ExitStack())

        def sb_parts(name, shape):
            return parts.enter_context(nc.sbuf_tensor(name, shape, F32R))

        gate_r = sb_parts("gate_r", [P, 2, 2, HC, I0])
        up_r = sb_parts("up_r", [P, 2, 2, HC, I0])
        down_r = sb_parts("down_r", [P, 2, 2, I0 // P, D])
        hidT = sb_parts("hidT", [P, 2, 2, I0 // P, 512])
        parts.close()

        wq_g = sb("wq_g", [P, HC, REP * HD])
        wo_g = wq_g.rearrange("p c n -> p (c n)").rearrange("p (h n) -> p h n", h=REP)
        wo_r = sb("wo_r", [P, 2, REP, D], F32R)
        rot_c = sb("rot_c", [P, 2, 512])
        rot_s = sb("rot_s", [P, 2, 512])
        kT = sb("kT", [P, B * N])
        vt = sb("vt", [P, T, HD])
        qT = sb("qT", [P, 2, B * N])
        prob = sb("prob", [P, 4, 3 * P])
        pmin = sb("pmin", [P, 4, 2])
        psum_ = sb("psum_", [P, 4, 2])
        pinv = sb("pinv", [P, 4, 2])
        probT = sb("probT", [P, 2, 3 * P])
        o_parts += [sb(f"o_part{j}", [P, B * N], F32R) for j in range(7, 2 * REP)]
        oT = [o_parts[:REP], o_parts[REP:]]

        S = {n: sem(n) for n in (
            "x_in", "const_in", "gat_in", "sim_in", "ctx_in0", "ctx_in1", "exp_in0", "exp_in1",
            "att_in", "wq_in", "wkv_in", "wo_in", "moe_in0", "moe_in1",
            "dve_held", "pe_held", "pool_held", "sp_held",
            "dve_chain", "pool_chain", "act_chain",
            "zero_done", "wa_done", "sd_done",
            "qk_ready", "qk_copied", "sim_ready", "sim_copied", "sig_done", "gam_done",
            "st_ready", "feat_ready", "feat_copied", "st_copied", "adj_ready",
            "adj_bias", "t_spread", "z_negated", "edge_done", "alpha_done", "alphaT_ready",
            "alphaT_act", "alphaT_dve", "rsum_ready", "sums_spread", "av_done", "g_norm", "g_max", "g_exps", "g_elu",
            "x1_ready", "x1_added",
            "rstd_done", "norm_done", "normT_ready", "normT_copied",
            "aT_ready", "aT_used", "rstd_ready", "ln_done", "x3_done", "var_scaled",
            "logit_ready", "rexp_done", "rmax_done",
            "gu0", "silu0", "hid0", "down0", "acc0", "whi0", "wlo0", "hidf0", "hidh0",
            "gu1", "silu1", "hid1", "down1", "acc1", "whi1", "wlo1", "hidf1", "hidh1", "actT_hi", "actT_lo",
            "wqk_hi", "wqk_lo", "wo_hi", "wo_lo",
            "q_ready", "q_swapped", "q_cos", "q_sin", "q_rot", "v_ready", "v_copied",
            "s_ready", "s_shift", "p_exp", "p_inv", "p_norm", "pT_ready", "pT_copied",
            "o_ready", "o_high", "o_copied", "wo_ready", "wo_added",
            "out_done")}

        expert_in = {0: (S["exp_in0"], S["exp_in1"]), 1: (S["moe_in0"], S["moe_in1"])}
        mix = {
            0: dict(E=E0, IC=I0 // P, scale=0.5, wt=wt0, gu=S["gu0"], silu=S["silu0"],
                    hid=S["hid0"], down=S["down0"], acc=S["acc0"], whi=S["whi0"], wlo=S["wlo0"],
                    hidf=S["hidf0"], hidh=S["hidh0"], src=(w_gate, w_up, w_down)),
            1: dict(E=E1 + 1, IC=I1 // P, scale=1.0, wt=wt1, gu=S["gu1"], silu=S["silu1"],
                    hid=S["hid1"], down=S["down1"], acc=S["acc1"], whi=S["whi1"], wlo=S["wlo1"],
                    hidf=S["hidf1"], hidh=S["hidh1"], src=(Wg, Wu, Wd)),
        }
        ROUNDS = 4
        UNITS = GH
        QUADS = GH // QUAD
        TURNS = B // 2
        ALL = ROUNDS * UNITS
        ALLQ = ROUNDS * QUADS
        LAST = ALL + 8

        def prep_at(k):
            return {-1: 0, UNITS - 2: 1, 2 * UNITS - 1: 2, 3 * UNITS - 1: 3}.get(k)

        def quad_at(k, lag):
            j = (k - lag - 8) // QUAD
            return j if (k - lag - 8) % QUAD == 0 and 0 <= j < ALLQ else None

        def alphaT_copied(i, k):
            return S["alphaT_dve" if k % 2 else "alphaT_act"], i * (ALL // 2) + (k // 2 + 1)

        Q_BANK, S_BANK, PT_BANK, O_BANK = bank[0:2], bank[2:4], bank[4:6], bank[6:8]
        LN_POOL = (T - 3, T - 2, T - 1)
        AU = REP * B
        PROJ = 2 * (REP + 1)

        def half_at(k, lag):
            h, half = divmod(k - lag, B)
            return (h + 2, (half,)) if 0 <= h < REP - 1 and half < 2 else None

        block = ctx.enter_context(nc.Block())

        @block.sync
        def _(sp):
            sp.dma_start(ctx_all[:], ctxT.rearrange("c b n -> c (b n)")).then_inc(S["sim_in"], 16)
            sp.dma_start(wqk[:, 0, :], WqT).then_inc(S["sim_in"], 16)
            sp.dma_start(wqk[:, 1, :], WkT).then_inc(S["sim_in"], 16)
            sp.dma_start(gam[:, 0:1], gamma.partition_broadcast(P)).then_inc(S["sim_in"], 16)
            sp.dma_start(w0[:], W0).then_inc(S["gat_in"], 16)
            sp.dma_start(w1[:], W1.rearrange("(c p) n -> p c n", p=P)).then_inc(S["gat_in"], 16)
            for j, a in enumerate((a_self0, a_neigh0, a_self1, a_neigh1)):
                sp.dma_start(avec[:, j, :], a.partition_broadcast(P)).then_inc(S["gat_in"], 16)
            sp.dma_start(bT[:], b01).then_inc(S["gat_in"], 16)
            sp.dma_start(ind_f[:], ind_in).then_inc(S["gat_in"], 16)
            sp.dma_start(xs[:], x.rearrange("b (u p) c -> p (b u) c", p=P)).then_inc(S["x_in"], 16)
            sp.dma_start(ident[:], ident_in).then_inc(S["const_in"], 16)
            sp.dma_start(wr0[:], w_router.rearrange("(c p) n -> p c n", p=P)).then_inc(S["const_in"], 16)
            sp.dma_start(wr1[:], Wr.rearrange("(c p) n -> p c n", p=P)).then_inc(S["const_in"], 16)
            sp.dma_start(eb[:], ebias.partition_broadcast(P)).then_inc(S["const_in"], 16)
            sp.dma_start(lnw[:, 0, :], ln1).then_inc(S["const_in"], 16)
            sp.dma_start(lnw[:, 1, :], ln2).then_inc(S["const_in"], 16)
            sp.dma_start(rq[:], rope_q).then_inc(S["att_in"], 16)
            sp.dma_start(rk[:], rope_k).then_inc(S["att_in"], 16)
            sp.dma_start(causal[:], causal_in).then_inc(S["att_in"], 16)
            with sp.Fori(0, TURNS) as i:
                for p in range(2):
                    sp.dma_start(ctx_b[:, p, :], ctxT[:, bass.ds(i * 2 + p, 1), :].rearrange(
                        "c b n -> c (b n)")).then_inc(S[f"ctx_in{p}"], 16)
                sp.wait_ge(S["feat_ready"], i * ROUNDS * NT + 2 * NT)
                sp.sem_inc(S["sp_held"])

            def load_expert(which, e, par):
                m = mix[which]
                g, u, d = m["src"]
                I = m["IC"] * P
                s = expert_in[which][par]
                sel = (lambda w: w[bass.ds(e, 1)].rearrange("e (c p) n -> p (e c) n", p=P))
                sp.dma_start(gate_w[:, par, :, 0:I], sel(g)).then_inc(s, 16)
                sp.dma_start(up_w[:, par, :, 0:I], sel(u)).then_inc(s, 16)
                sp.dma_start(down_w[:, par, 0:m["IC"], :], sel(d)).then_inc(s, 16)

            def load_experts(which):
                m = mix[which]
                for e in range(2):
                    load_expert(which, e, e)
                pairs = (m["E"] - 2) // 2
                with sp.Fori(0, pairs) as i:
                    for par in range(2):
                        e = i * 2 + (2 + par)
                        sp.wait_ge(m["wlo"], e * 3 - 3)
                        sp.sem_inc(S["sp_held"])
                        load_expert(which, e, par)
                for e in range(2 + 2 * pairs, m["E"]):
                    sp.wait_ge(m["wlo"], 3 * e - 3)
                    load_expert(which, e, e % 2)

            load_experts(0)
            def load_projections(g):
                sp.dma_start(wq_g[:], Wq.rearrange("(c p) n -> p c n", p=P)[
                    :, :, bass.ds(g * (REP * HD), REP * HD)]).then_inc(S["wq_in"], 16)
                for w, dst in ((Wk, wk_g), (Wv, wv_g)):
                    sp.dma_start(dst[:], w.rearrange("(c p) n -> p c n", p=P)[
                        :, :, bass.ds(g * HD, HD)]).then_inc(S["wkv_in"], 16)

            sp.wait_ge(mix[0]["down"], 4 * E0)
            load_projections(0)

            def load_output(g):
                sp.dma_start(wo_g[:], Wo.rearrange("(g r p) n -> g p r n", g=KV, p=P)[
                    bass.ds(g, 1)].rearrange("g p r n -> p (g r) n")).then_inc(S["wo_in"], 16)

            with sp.Fori(0, KV - 1) as g:
                sp.wait_ge(S["wqk_lo"], 2 * g + 2)
                sp.sem_inc(S["sp_held"])
                load_output(g)
                sp.wait_ge(S["wo_lo"], g + 1)
                sp.wait_ge(S["v_ready"], 2 * g + 2)
                sp.sem_inc(S["sp_held"])
                load_projections(g + 1)
            sp.wait_ge(S["wqk_lo"], 2 * KV)
            load_output(KV - 1)
            sp.wait_ge(S["q_sin"], KV * PROJ)
            sp.wait_ge(S["q_ready"], KV * PROJ)
            sp.wait_ge(S["v_ready"], KV * 2)
            load_experts(1)
            for half in range(2):
                sp.wait_ge(mix[1]["acc"], 4 * E1 + 2 * half + 2)
                sp.dma_start(out.rearrange("b (u p) c -> p (b u) c", p=P)[:, 4 * half:4 * half + 4],
                             xs[:, 4 * half:4 * half + 4, :]).then_inc(S["out_done"], 16)
            sp.wait_ge(S["out_done"], 32)

        @block.tensor
        def _(pe):
            def similarity():
                pe.wait_ge(S["sim_in"], 64)
                for j in range(2):
                    for half in range(2):
                        pe.matmul(bank[2 * j + half][0:FC, :], wqk[:, j, :], ctx_all[:, 512 * half:512 * half + 512],
                                  start=True, stop=True).then_inc(S["qk_ready"], 1)
                pe.wait_ge(S["qk_copied"], 4)
                for t in range(T):
                    if t >= 4:
                        pe.wait_ge(S["sim_copied"], t - 3)
                    pe.matmul(bank[4 + t % 4][:, 0:N], qkT[:, 0, t * P:t * P + P],
                              qkT[:, 1, t // NT * N:t // NT * N + N], start=True, stop=True
                              ).then_inc(S["sim_ready"], 1)

            def graph_attention():
                FEAT, MISC, ZB, PTB, OB = bank[0], bank[1], bank[2:4], bank[4:6], bank[6:8]
                pe.wait_ge(S["wa_done"], 1)
                pe.wait_ge(S["sim_copied"], T)
                with pe.Fori(0, TURNS) as i:
                    def sources(r):
                        layer, p = divmod(r, 2)
                        if layer == 0:
                            return 1, lambda c: ctx_b[:, p, :]
                        return HC, lambda c: h1T[:, p, c, :]

                    def prep(r):
                        layer, p = divmod(r, 2)
                        if layer == 0:
                            pe.wait_ge(S[f"ctx_in{p}"], i * 16 + 16)
                        else:
                            pe.wait_ge(S["g_elu"], i * ALLQ + QUADS * (p + 1))
                        if r >= 1:
                            pe.wait_ge(S["st_copied"], i * ROUNDS * 3 + 3 * r)
                        ks, src = sources(r)
                        wat = (lambda c: wat0[:]) if layer == 0 else (lambda c: wat1[:, c, :])
                        was = (lambda c: was0[:]) if layer == 0 else (lambda c: was1[:, c, :])
                        pe.sem_inc(S["pe_held"])
                        for c in range(ks):
                            mm = pe.matmul(MISC[0:TR, 0:N], wat(c), src(c), start=c == 0, stop=c == ks - 1)
                        for nt in range(NT):
                            for c in range(ks):
                                mm = pe.matmul(MISC[:, N + nt * GH:N + nt * GH + GH], src(c)[:, nt * P:nt * P + P],
                                               was(c), start=c == 0, stop=c == ks - 1)
                        mm.then_inc(S["st_ready"], 1)

                    def features(r, nt):
                        if nt == 0 and r >= 1:
                            pe.wait_ge(S["feat_copied"], i * ROUNDS + r)
                        elif nt == 0:
                            pe.wait_ge(S["x1_added"], i * 4 + 1)
                        ks, src = sources(r)
                        w = (lambda c: w0[:]) if r < 2 else (lambda c: w1[:, c, :])
                        for c in range(ks):
                            mm = pe.matmul(FEAT[:, nt * D:nt * D + D], src(c)[:, nt * P:nt * P + P],
                                           w(c), start=c == 0, stop=c == ks - 1)
                        mm.then_inc(S["feat_ready"], 1)

                    def spread(k):
                        r, h = divmod(k, UNITS)
                        if h == 0:
                            pe.wait_ge(S["st_copied"], i * ROUNDS * 3 + (3 * r + 3))
                        if k >= 2:
                            pe.wait_ge(S["z_negated"], i * ALL + (k - 1))
                        pe.matmul(ZB[k % 2][:, 0:N], ind[:, h, :], t_parts[:, r % 2, :],
                                  start=True, stop=True).then_inc(S["t_spread"], 1)

                    def turn(k):
                        pe.wait_ge(S["alpha_done"], i * ALL + (k + 1))
                        if k >= 2:
                            pe.wait_ge(*alphaT_copied(i, k - 2))
                        for mc in range(NT):
                            for nt in range(NT):
                                mm = pe.transpose(PTB[k % 2][:, mc * N + nt * P:mc * N + nt * P + P],
                                                  alpha[:, k % 2, nt * N + mc * P:nt * N + mc * P + P], ident[:])
                        mm.then_inc(S["alphaT_ready"], 1)

                    def spread_sums(j):
                        pe.wait_ge(S["rsum_ready"], i * ALLQ + (j + 1))
                        if j >= 2:
                            pe.wait_ge(S["g_norm"], i * ALLQ + (j - 1))
                        for nt in range(NT):
                            mm = pe.matmul(OB[j % 2][:, N + nt * P:N + nt * P + P],
                                           rsum_w[:, j % 2, nt].rearrange("p h o -> p (h o)"), ident[:], start=True, stop=True)
                        mm.then_inc(S["sums_spread"], 1)

                    def weigh(j):
                        r, c = divmod(j, QUADS)
                        pe.wait_ge(*alphaT_copied(i, QUAD * j + QUAD - 2))
                        pe.wait_ge(*alphaT_copied(i, QUAD * j + QUAD - 1))
                        if c == 0:
                            pe.wait_ge(S["feat_copied"], i * ROUNDS + (r + 1))
                        pe.wait_ge(S["sums_spread"], i * ALLQ + (j + 1))
                        for mc in range(NT):
                            for h4 in range(QUAD):
                                mm = pe.matmul(OB[j % 2][h4 * GO:(h4 + 1) * GO, 0:N],
                                               feat[:, r % 2, mc, (QUAD * c + h4) * GO:(QUAD * c + h4 + 1) * GO],
                                               alphaT[:, j % 2, h4, mc, :], start=mc == 0, stop=mc == NT - 1)
                        mm.then_inc(S["av_done"], 1)

                    def turn_x1(p):
                        pe.wait_ge(S["g_elu"], i * ALLQ + QUADS * (3 + p))
                        pe.wait_ge(S["feat_copied"], (i + 1) * ROUNDS)
                        for nt in range(NT):
                            if p or nt:
                                pe.wait_ge(S["x1_added"], i * 4 + (2 * p + nt + 1))
                            for c in range(HC):
                                mm = pe.transpose(FEAT[:, c * P:c * P + P], x1T[:, p, c, nt * P:nt * P + P], ident[:])
                            mm.then_inc(S["x1_ready"], 1)

                    for k in range(-1, LAST):
                        if (r := prep_at(k)) is not None:
                            prep(r)
                        if 0 <= k - 3 < ALL:
                            turn(k - 3)
                        if 0 <= k + 1 < ALL:
                            spread(k + 1)
                        if (j := quad_at(k, 0)) is not None:
                            spread_sums(j)
                        for nt in range(NT):
                            if (r := prep_at(k - 1 - nt)) is not None:
                                features(r, nt)
                        if (j := quad_at(k, 0)) is not None:
                            weigh(j)
                        if (j := quad_at(k, 3)) in (2 * QUADS + QUADS - 1, 3 * QUADS + QUADS - 1):
                            turn_x1(j // QUADS - 2)

            def turn_norm(which, w=None):
                for t in range(T + 2):
                    if t < T:
                        pe.wait_ge(S["norm_done"], which * T + t + 1)
                        if which * T + t >= 2:
                            pe.wait_ge(S["normT_copied"], which * T + t - 1)
                        for c in range(HC):
                            mm = pe.transpose(bank[t % 2][:, c * P:c * P + P], norm[:, t % 2, c * P:c * P + P], ident[:])
                        mm.then_inc(S["normT_ready"], 1)
                    if w is not None and t >= 2:
                        E = w.shape[2]
                        pe.wait_ge(S["normT_copied"], which * T + t - 1)
                        for c in range(HC):
                            mm = pe.matmul(bank[2][:, (t - 2) * E:(t - 1) * E], actT[:, c, (t - 2) * P:(t - 1) * P],
                                           w[:, c, :], start=c == 0, stop=c == HC - 1)
                if w is not None:
                    mm.then_inc(S["logit_ready"], 1)

            def mixture(which):
                m = mix[which]
                IC, steps = m["IC"], 2 * m["E"]
                GB, UB, DB = bank[0:2], bank[2:4], bank[4:8]

                def gate_up(s, mod):
                    half, par = mod % 2, mod // 2
                    if half == 0:
                        pe.wait_ge(m["wlo"], 3 * (s // 2) + 3 if isinstance(s, int) else (s // 2) * 3 + 3)
                    for ic in range(IC):
                        q = s * IC + ic
                        if not isinstance(s, int) or q >= 2:
                            pe.wait_ge(m["hid"], q - 1)
                        qp = (mod * IC + ic) % 2
                        for dst, w in ((GB[qp], gate_r), (UB[qp], up_r)):
                            for c in range(HC):
                                mm = split_product(
                                    pe, dst[:], [w[:, par, j, c, ic * P:ic * P + P] for j in range(2)],
                                    [actT_r[:, j, c, half * 512:half * 512 + 512] for j in range(2)],
                                    c == 0, c == HC - 1)
                        mm.then_inc(m["gu"], 1)

                def down(s, mod):
                    pe.wait_ge(m["hid"], s * IC + IC)
                    if not isinstance(s, int) or s >= 2:
                        pe.wait_ge(m["acc"], s * 2 - 2)
                    for j in range(4):
                        for ic in range(IC):
                            mm = split_product(
                                pe, DB[2 * (mod % 2) + j // 2][:, j % 2 * D:j % 2 * D + D],
                                [hidT[:, mod % 2, r, ic, j * P:j * P + P] for r in range(2)],
                                [down_r[:, mod // 2, r, ic, :] for r in range(2)], ic == 0, ic == IC - 1)
                        if j % 2 == 1:
                            mm.then_inc(m["down"], 1)

                def body(s, mod):
                    if not isinstance(s, int) or s + 1 < steps:
                        gate_up(s + 1, (mod + 1) % 4)
                    down(s, mod)

                pe.wait_ge(S["rmax_done"], which + 1)
                pe.wait_ge(S["actT_lo"], 4 * which + 2)
                gate_up(0, 0)
                expert_steps(pe, steps, body)

            def symmetric():
                pe.wait_ge(S["acc0"], 4 * E0)
                for t in range(T):
                    b, nt = divmod(t, NT)
                    if t >= 2:
                        pe.wait_ge(S["aT_used"], t - 1)
                    for mt in range(NT):
                        mm = pe.transpose(bank[2 + t % 2][:, mt * P:mt * P + P],
                                          sig[:, b * NT + mt, nt * P:nt * P + P], ident[:])
                    mm.then_inc(S["aT_ready"], 1)

            def attention():
                pe.wait_ge(S["normT_copied"], 2 * T)

                def project(g, n, halves=(0, 1)):
                    for half in halves:
                        if n:
                            pe.wait_ge(S["q_cos"], g * PROJ + (2 * n + half - 1))
                        for c in range(HC):
                            mm = split_product(
                                pe, Q_BANK[half][:], [wqk_r[:, j, c, n * HD:n * HD + HD] for j in range(2)],
                                [actT_r[:, j, c, half * 512:half * 512 + 512] for j in range(2)],
                                c == 0, c == HC - 1)
                        mm.then_inc(S["q_ready"], 1)

                def keys(g):
                    pe.wait_ge(S["wqk_lo"], g * 2 + 2)
                    project(g, 0)

                def values(g):
                    pe.wait_ge(S["wkv_in"], g * 32 + 32)
                    pe.sem_inc(S["pe_held"])
                    for half in range(2):
                        for j in range(4):
                            t = 4 * half + j
                            for c in range(HC):
                                mm = pe.matmul(S_BANK[half][:, j * HD:j * HD + HD], actT[:, c, t * P:t * P + P],
                                               wv_g[:, c, :], start=c == 0, stop=c == HC - 1)
                        mm.then_inc(S["v_ready"], 1)

                def group(g, last):
                    def scores(k):
                        h, b = divmod(k, B)
                        if b % 2 == 0:
                            pe.wait_ge(S["q_rot"], g * PROJ + (2 * (h + 1) + b // 2 + 1))
                        if k < 2:
                            pe.wait_ge(S["v_copied"], g * 2 + (k + 1))
                        if k >= 2:
                            pe.wait_ge(S["s_shift"], g * AU + (k - 1))
                        for nt in range(NT):
                            mm = pe.matmul(S_BANK[k % 2][:, nt * P:nt * P + (nt + 1) * P],
                                           qT[:, h % 2, b * N + nt * P:b * N + nt * P + P],
                                           kT[:, b * N:b * N + (nt + 1) * P], start=True, stop=True)
                        mm.then_inc(S["s_ready"], 1)

                    def turn(k):
                        pe.wait_ge(S["p_norm"], g * AU + (k + 1))
                        if k >= 2:
                            pe.wait_ge(S["pT_copied"], g * AU + (k - 1))
                        else:
                            pe.wait_ge(S["wo_added"], g * (T // 2) + 1)
                        for j in range(3):
                            mm = pe.transpose(PT_BANK[k % 2][:, j * P:j * P + P], prob[:, k % 4, j * P:j * P + P], ident[:])
                        mm.then_inc(S["pT_ready"], 1)

                    def weigh(k):
                        b = k % B
                        pe.wait_ge(S["pT_copied"], g * AU + (k + 1))
                        if k >= 2:
                            pe.wait_ge(S["o_copied"], g * AU + (k - 1))
                        pe.matmul(O_BANK[k % 2][:, 0:N], vt[:, b * NT, :], probT[:, k % 2, 0:N],
                                  start=True, stop=False)
                        pe.matmul(O_BANK[k % 2][:, P:N], vt[:, b * NT + 1, :], probT[:, k % 2, N:N + P],
                                  start=False, stop=True).then_inc(S["o_ready"], 1)

                    def project_out(pairs):
                        for j in pairs:
                            if j >= 2:
                                pe.wait_ge(S["wo_added"], g * (T // 2) + j)
                            for u in range(2):
                                t = 2 * j + u
                                for h in range(REP):
                                    mm = split_product(
                                        pe, PT_BANK[j % 2][:, u * D:u * D + D],
                                        [oT[r][h][:, t * P:t * P + P] for r in range(2)],
                                        [wo_r[:, r, h, :] for r in range(2)], h == 0, h == REP - 1)
                            mm.then_inc(S["wo_ready"], 1)

                    for k in range(AU + 3):
                        if k == 0:
                            scores(0)
                        if k + 1 < AU:
                            scores(k + 1)
                        if (q := half_at(k, 0)) is not None:
                            project(g, *q)
                        if k == AU and not last:
                            keys(g + 1)
                        if 0 <= k - 2 < AU:
                            turn(k - 2)
                        if 0 <= k - 3 < AU:
                            weigh(k - 3)
                    if not last:
                        values(g + 1)
                    pe.wait_ge(S["o_copied"], g * AU + AU)
                    pe.wait_ge(S["wo_lo"], g + 1)
                    project_out((0, 1))
                    if not last:
                        project(g + 1, 1)
                    project_out((2, 3))

                pe.sem_inc(S["wo_ready"])
                values(0)
                pe.wait_ge(S["actT_lo"], 4)
                keys(0)
                project(0, 1)
                with pe.Fori(0, KV - 1) as g:
                    group(g, False)
                group(KV - 1, True)

            similarity()
            pe.wait_ge(S["const_in"], 16 * 6)
            graph_attention()
            turn_norm(0, wr0)
            mixture(0)
            symmetric()
            turn_norm(1)
            attention()
            turn_norm(2, wr1)
            mixture(1)

        @block.scalar
        def _(act):
            chain = Chain(act, S["act_chain"])

            def roots(src, scale):
                act.activation(sd[:], src, ACT.Sqrt, bias=eps[:, 0:1], scale=scale).then_inc(S["sd_done"], 1)

            def graph_attention():
                FEAT, ZB, PTB = bank[0], bank[2:4], bank[4:6]
                with act.Fori(0, TURNS) as i:
                    def copy_features(r):
                        act.wait_ge(S["feat_ready"], i * ROUNDS * NT + NT * (r + 1))
                        act.activation(feat[:, r % 2].rearrange("p u c -> p (u c)"), FEAT[:], ACT.Copy
                                       ).then_inc(S["feat_copied"], 1)

                    def negate(k):
                        act.wait_ge(S["t_spread"], i * ALL + (k + 1))
                        if k % UNITS == 0:
                            act.wait_ge(S["st_copied"], i * ROUNDS * 3 + (3 * (k // UNITS) + 3))
                        if k >= 2:
                            act.wait_ge(S["edge_done"], i * ALL + (k - 1))
                        r, h = divmod(k, UNITS)
                        for nt in range(NT):
                            ins = act.activation(lrelu[:, k % 2, nt * N:nt * N + N], ZB[k % 2][:, 0:N], ACT.Identity,
                                                 bias=neg_s[:, r % 2, nt, h:h + 1], scale=-1.0)
                        ins.then_inc(S["z_negated"], 1)

                    def exps(k):
                        act.wait_ge(S["edge_done"], i * ALL + (k + 1))
                        if k >= 2:
                            act.wait_ge(S["alphaT_ready"], i * ALL + (k - 1))
                        j, h4 = divmod(k, QUAD)
                        if h4 == 0 and j >= 2:
                            act.wait_ge(S["rsum_ready"], i * ALLQ + (j - 1))
                        for nt in range(NT):
                            ins = act.activation(alpha[:, k % 2, nt * N:nt * N + N], edge[:, k % 2, nt * N:nt * N + N],
                                                 ACT.Exp, bias=edge_min[:, k % 2, nt:nt + 1], scale=-1.0,
                                                 accum_out=sums[:, j % 2, nt, h4:h4 + 1])
                        ins.then_inc(S["alpha_done"], 1)

                    def copy_T(k):
                        act.wait_ge(S["alphaT_ready"], i * ALL + (k + 1))
                        j = k // QUAD
                        if j >= 2:
                            act.wait_ge(S["av_done"], i * ALLQ + (j - 1))
                        act.activation(alphaT[:, j % 2, k % QUAD].rearrange("p m n -> p (m n)"), PTB[k % 2][:],
                                       ACT.Copy).then_inc(S["alphaT_act"], 1)

                    def exp_out(j):
                        layer, c = j // QUADS // 2, j % QUADS
                        act.wait_ge(S["g_norm"], i * ALLQ + (j + 1))
                        act.activation(g_exp[:, j % 2, :], g_out[:, j % 2, :], ACT.Exp, bias=bT[:, layer, c:c + 1]
                                       ).then_inc(S["g_exps"], 1)

                    for k in range(-1, LAST):
                        if 0 <= k < ALL:
                            negate(k)
                        if (j := quad_at(k, 2)) is not None:
                            exp_out(j)
                        if 0 <= k - 2 < ALL:
                            exps(k - 2)
                        if 0 <= k - 4 < ALL and k % 2 == 0:
                            copy_T(k - 4)
                        if (r := prep_at(k - 3)) is not None:
                            copy_features(r)

            def high_parts(which, e, par):
                m = mix[which]
                IC = m["IC"]
                act.wait_ge(expert_in[which][par], e * 24 + (48 - 24 * par))
                if not isinstance(e, int) or e >= 2:
                    act.wait_ge(m["down"], e * 4 - 4)
                I = IC * P
                for w, r in ((gate_w[:, par, :, 0:I], gate_r[:, par, 0, :, 0:I]),
                             (up_w[:, par, :, 0:I], up_r[:, par, 0, :, 0:I]),
                             (down_w[:, par, 0:IC, :], down_r[:, par, 0, 0:IC, :])):
                    act.activation(r, w, ACT.Copy).then_inc(m["whi"], 1)

            def mixture(which):
                m = mix[which]
                IC = m["IC"]
                last = 2 * m["E"] - 2

                def body(s, mod):
                    for ic in range(IC):
                        q = s * IC + ic
                        qp = (mod * IC + ic) % 2
                        act.wait_ge(m["gu"], q + 1)
                        if not isinstance(s, int) or q >= 2:
                            act.wait_ge(m["hid"], q - 1)
                        act.activation(silu[:, qp, :], bank[qp][:], ACT.Silu, scale=m["scale"]
                                       ).then_inc(m["silu"], 1)
                    if mod % 2 == 0 and (not isinstance(s, int) or s < last):
                        high_parts(which, s // 2 + 1, (mod // 2 + 1) % 2)

                expert_steps(act, 2 * m["E"], body)

            def squares():
                for t in range(T):
                    act.wait_ge(S["wo_added"], (KV - 1) * (T // 2) + t // 2 + 2)
                    chain.link(act.activation(sq[:], xs[:, t, :], ACT.Square, accum_out=mv[:, t, 0:1]))
                roots(mv[:, :, 0], 1.0 / D)

            def scaled_copy(which, w):
                for t in range(T):
                    act.wait_ge(S["normT_ready"], which * T + t + 1)
                    for c in range(HC):
                        ins = act.activation(actT[:, c, t * P:t * P + P], bank[t % 2][:, c * P:c * P + P],
                                             ACT.Copy, scale=lnw[:, w, c:c + 1])
                    ins.then_inc(S["normT_copied"], 1)

            def high_weights(g):
                act.wait_ge(S["wkv_in"], g * 32 + 32)
                act.wait_ge(S["wq_in"], g * 16 + 16)
                if not isinstance(g, int):
                    act.wait_ge(S["q_ready"], g * PROJ)
                act.activation(wqk_r[:, 0, :, 0:HD], wk_g[:], ACT.Copy).then_inc(S["wqk_hi"], 1)
                act.activation(wqk_r[:, 0, :, HD:], wq_g[:], ACT.Copy).then_inc(S["wqk_hi"], 1)

            def attention():
                act.wait_ge(S["att_in"], 48)

                def swap_halves(g, n, halves=(0, 1)):
                    for half in halves:
                        act.wait_ge(S["q_ready"], g * PROJ + (2 * n + half + 1))
                        if n:
                            act.wait_ge(S["q_sin"], g * PROJ + (2 * n + half - 1))
                        act.activation(swap[0:64, half, :], Q_BANK[half][64:P, :], ACT.Copy)
                        act.activation(swap[64:P, half, :], Q_BANK[half][0:64, :], ACT.Copy).then_inc(S["q_swapped"], 1)

                def high_outputs(g):
                    act.wait_ge(S["wo_in"], g * 16 + 16)
                    act.wait_ge(S["wo_ready"], g * (T // 2) + 1)
                    act.activation(wo_r[:, 0], wo_g[:], ACT.Copy).then_inc(S["wo_hi"], 1)

                def group(g, last):
                    def exps(k):
                        act.wait_ge(S["s_shift"], g * AU + (k + 1))
                        for nt in range(NT):
                            ins = act.activation(prob[:, k % 4, nt * P:nt * P + (nt + 1) * P],
                                                 prob[:, k % 4, nt * P:nt * P + (nt + 1) * P], ACT.Exp,
                                                 bias=pmin[:, k % 4, nt:nt + 1], scale=-1.0,
                                                 accum_out=psum_[:, k % 4, nt:nt + 1])
                        ins.then_inc(S["p_exp"], 1)

                    def copy_T(k):
                        act.wait_ge(S["pT_ready"], g * AU + (k + 1))
                        if k >= 2:
                            act.wait_ge(S["o_ready"], g * AU + (k - 1))
                        act.activation(probT[:, k % 2, :], PT_BANK[k % 2][:, 0:3 * P], ACT.Copy).then_inc(S["pT_copied"], 1)

                    def high_out(k):
                        h, b = divmod(k, B)
                        act.wait_ge(S["o_ready"], g * AU + (k + 1))
                        act.activation(oT[0][h][:, b * N:b * N + N], O_BANK[k % 2][:, 0:N], ACT.Copy
                                       ).then_inc(S["o_high"], 1)

                    for k in range(AU + 4):
                        if 0 <= k - 4 < AU:
                            high_out(k - 4)
                        if (q := half_at(k, 1)) is not None:
                            swap_halves(g, *q)
                        if k == B:
                            high_outputs(g)
                        if k == AU - B and not last:
                            high_weights(g + 1)
                        if k < AU:
                            exps(k)
                        if 0 <= k - 2 < AU:
                            copy_T(k - 2)
                    if not last:
                        swap_halves(g + 1, 0)
                        swap_halves(g + 1, 1)

                swap_halves(0, 0)
                swap_halves(0, 1)
                with act.Fori(0, KV - 1) as g:
                    group(g, False)
                group(KV - 1, True)

            act.wait_ge(S["sim_in"], 64)
            act.wait_ge(S["zero_done"], 1)
            act.activation(gam[:, 1:2], gam[:, 0:1], ACT.Sigmoid).then_inc(S["gam_done"], 1)
            for j in range(2):
                for half in range(2):
                    act.wait_ge(S["qk_ready"], 2 * j + half + 1)
                    act.activation(qkT[:, j, 512 * half:512 * half + 512], bank[2 * j + half][0:FC, :], ACT.Copy
                                   ).then_inc(S["qk_copied"], 1)
            for t in range(T):
                act.wait_ge(S["sim_ready"], t + 1)
                act.activation(sim[:, t, :], bank[4 + t % 4][:, 0:N], ACT.Copy).then_inc(S["sim_copied"], 1)
                act.wait_ge(S["sim_copied"], t + 1)
                act.activation(sig[:, t, :], sim[:, t, :], ACT.Sigmoid, scale=1.0 / 16).then_inc(S["sig_done"], 1)
            act.wait_ge(S["rstd_done"], 1)
            roots(mv[:, :, 1], 1.0)
            graph_attention()
            act.wait_ge(S["rstd_done"], 2)
            roots(mv[:, :, 1], 1.0)
            high_parts(0, 0, 0)
            act.wait_ge(S["rmax_done"], 1)
            act.activation(route[:, 0, :, 0:E0], route[:, 0, :, 0:E0], ACT.Exp).then_inc(S["rexp_done"], 1)
            mixture(0)
            act.wait_ge(S["rstd_done"], 3)
            roots(mv[:, :, 1], 1.0)
            high_weights(0)
            act.wait_ge(S["rstd_done"], 4)
            roots(mv[:, :, 1], 1.0)
            act.wait_ge(S["var_scaled"], 1)
            roots(ymean[:], 1.0)
            scaled_copy(1, 0)
            attention()
            squares()
            high_parts(1, 0, 0)
            scaled_copy(2, 1)
            act.wait_ge(S["logit_ready"], 2)
            act.activation(route[:, 0, :, :], bank[2][:, 0:T * E1].rearrange("p (t e) -> p t e", t=T),
                           ACT.Sigmoid).then_inc(S["rexp_done"], 1)
            mixture(1)

        @block.gpsimd
        def _(pool):
            chain = Chain(pool, S["pool_chain"])
            def signal(ins, name, count):
                ins.then_inc(S[name], 1)
                pool.wait_ge(S[name], count)
                pool.sem_inc(S["pool_held"])

            pool.wait_ge(S["gat_in"], 16 * 8)
            with pool.Fori(0, TURNS) as i:
                chain.restart()
                for p in range(2):
                    pool.wait_ge(S["adj_ready"], i * 2 + (p + 1))
                    pool.sem_inc(S["pool_held"])
                    both = adj[:, p].rearrange("p u n -> p (u n)")
                    chain.link(pool.tensor_scalar(both, both, -1.0, 1.0, ALU.mult, ALU.add))
                    signal(pool.tensor_scalar(both, both, MASK, 0.0, ALU.mult, ALU.add),
                           "adj_bias", i * 2 + (p + 1))

            def low_parts(which):
                m = mix[which]
                I = m["IC"] * P

                def expert(e, par):
                    for j, (w, r) in enumerate(((gate_w[:, par, :, 0:I], gate_r[:, par, :, :, 0:I]),
                                                (up_w[:, par, :, 0:I], up_r[:, par, :, :, 0:I]),
                                                (down_w[:, par, 0:m["IC"], :], down_r[:, par, :, 0:m["IC"], :]))):
                        pool.wait_ge(m["whi"], e * 3 + (j + 1))
                        ins = pool.tensor_tensor(r[:, 1], w, r[:, 0].bitcast(F32), ALU.subtract)
                        ins.then_inc(m["wlo"], 1)

                pairs = m["E"] // 2
                with pool.Fori(0, pairs) as i:
                    for par in range(2):
                        expert(i * 2 + par, par)
                for e in range(2 * pairs, m["E"]):
                    expert(e, e % 2)

            low_parts(0)
            pool.wait_ge(S["rstd_ready"], 1)
            for j, t in enumerate(LN_POOL):
                signal(pool.tensor_scalar(x3[:, t, :], xs[:, t, :], mv[:, t, 0:1], rstd[:, t:t + 1],
                                          ALU.subtract, ALU.mult), "ln_done", j + 1)

            def low_weights(g):
                for j, (cols, w) in enumerate(((slice(0, HD), wk_g), (slice(HD, None), wq_g))):
                    pool.wait_ge(S["wqk_hi"], g * 2 + (j + 1))
                    signal(pool.tensor_tensor(wqk_r[:, 1, :, cols], w[:], wqk_r[:, 0, :, cols].bitcast(F32),
                                              ALU.subtract), "wqk_lo", g * 2 + (j + 1))

            def group_work(g):
                for n in range(REP + 1):
                    if n == 4:
                        pool.wait_ge(S["wo_hi"], g + 1)
                        signal(pool.tensor_tensor(wo_r[:, 1], wo_g[:], wo_r[:, 0].bitcast(F32), ALU.subtract),
                               "wo_lo", g + 1)
                    tab = rk if n == 0 else rq
                    for half in range(2):
                        pool.wait_ge(S["q_swapped"], g * PROJ + (2 * n + half + 1))
                        if n:
                            pool.wait_ge(S["q_rot"], g * PROJ + (2 * n + half - 1))
                        signal(pool.tensor_tensor(rot_s[:, half].rearrange("p (b n) -> p b n", b=2),
                                                  swap[:, half].rearrange("p (b n) -> p b n", b=2),
                                                  bcast(tab[:, 1, :], 1, 2), ALU.mult),
                               "q_sin", g * PROJ + (2 * n + half + 1))

            pool.wait_ge(S["att_in"], 48)
            low_weights(0)
            with pool.Fori(0, KV - 1) as g:
                group_work(g)
                low_weights(g + 1)
            group_work(KV - 1)
            low_parts(1)

        @block.vector
        def _(dve):
            chain = Chain(dve, S["dve_chain"])

            def statistics(src):
                for t in range(T):
                    dve.bn_stats(stats[:, t, :], src[:, t, :])
                chain.link(dve.engine_nop())
                for t in range(T):
                    ins = dve.bn_aggr(mv[:, t, :], stats[:, t, :])
                ins.then_inc(S["rstd_done"], 1)

            def inverses(n):
                dve.wait_ge(S["sd_done"], n + 1)
                chain.link(dve.reciprocal(rstd[:], sd[:]))

            def layer_norm_tile(dst, t, src=xs):
                return dve.tensor_scalar(dst, src[:, t, :], mv[:, t, 0:1], rstd[:, t:t + 1], ALU.subtract, ALU.mult)

            def prepare_vectors():
                dve.wait_ge(S["gat_in"], 16 * 8)
                chain.link(dve.memset(wat0[:], 0.0))
                chain.link(dve.memset(wat1[:], 0.0))
                heads = lambda ap: ap.rearrange("p (h o) -> p h o", h=GH)
                for j, (wa_0, wa_1) in enumerate(((was0, was1), (wat0, wat1))):
                    chain.link(dve.tensor_tensor(wa_tmp[0:FC, j, :], w0[:], avec[0:FC, j, :], ALU.mult))
                    chain.link(dve.tensor_reduce(wa_0[:, 0:GH], heads(wa_tmp[0:FC, j, :]), X, ALU.add))
                    for c in range(HC):
                        chain.link(dve.tensor_tensor(wa_tmp[:, 2 + 2 * c + j, :], w1[:, c, :], avec[:, 2 + j, :], ALU.mult))
                        chain.link(dve.tensor_reduce(wa_1[:, c, 0:GH], heads(wa_tmp[:, 2 + 2 * c + j, :]), X, ALU.add))
                chain.link(dve.tensor_copy(wat0[:, ROW:], wat0[:, 0:GH]))
                chain.link(dve.tensor_copy(wat1[:, :, ROW:], wat1[:, :, 0:GH]))
                dve.tensor_scalar(bT1[:], bT[:], -1.0, None, ALU.add)
                dve.tensor_copy(ind[:], ind_f[:]).then_inc(S["wa_done"], 1)
                dve.sem_inc(S["x1_added"])
                dve.sem_inc(S["wo_added"])

            def graph_attention():
                FEAT, MISC, PTB, OB = bank[0], bank[1], bank[4:6], bank[6:8]
                with dve.Fori(0, TURNS) as i:
                    chain.restart()

                    def prep(r):
                        layer, p = divmod(r, 2)
                        if layer == 0:
                            for nt in range(NT):
                                t = i * 4 + (2 * p + nt)
                                ins = dve.tensor_scalar(
                                    adj[:, p, nt, :], xs[:, bass.ds(t, 1), :].rearrange("p u c -> p (u c)"),
                                    mv[:, bass.ds(t, 1), 0:1].rearrange("p u c -> p (u c)"), rstd[:, bass.ds(t, 1)],
                                    ALU.subtract, ALU.mult)
                            ins.then_inc(S["adj_ready"], 1)
                        dve.wait_ge(S["st_ready"], i * ROUNDS + (r + 1))
                        dve.tensor_copy(t_parts[:, p, :], MISC[0:TR, 0:N]).then_inc(S["st_copied"], 1)
                        dve.tensor_scalar(neg_s[:, p].rearrange("p u h -> p (u h)"), MISC[:, N:N + NT * GH], -1.0, None,
                                          ALU.mult).then_inc(S["st_copied"], 1)
                        dve.wait_ge(S["st_copied"], i * ROUNDS * 3 + (3 * r + 1))
                        dve.tensor_tensor(t_parts[ROW:, p, :], MISC[ROW:TR, 0:N], t_parts[ROW:, p, :].bitcast(F32),
                                          ALU.subtract).then_inc(S["st_copied"], 1)

                    def edges(k):
                        r, h = divmod(k, UNITS)
                        dve.wait_ge(S["z_negated"], i * ALL + (k + 1))
                        if h == 0 and r < 2:
                            dve.wait_ge(S["adj_bias"], i * 2 + (r + 1))
                        if k >= 2:
                            dve.wait_ge(S["alpha_done"], i * ALL + (k - 1))
                        chain.link(dve.scalar_tensor_tensor(lrelu[:, k % 2, :], lrelu[:, k % 2, :], NEG,
                                                            lrelu[:, k % 2, :], ALU.mult, ALU.min))
                        for nt in range(NT):
                            ins = dve.tensor_tensor_reduce(
                                out=edge[:, k % 2, nt * N:nt * N + N], in0=lrelu[:, k % 2, nt * N:nt * N + N],
                                in1=adj[:, r % 2, nt, :], scale=1.0, scalar=3.0e38, op0=ALU.add, op1=ALU.min,
                                accum_out=edge_min[:, k % 2, nt:nt + 1])
                        ins.then_inc(S["edge_done"], 1)

                    def copy_T(k):
                        dve.wait_ge(S["alphaT_ready"], i * ALL + (k + 1))
                        j = k // QUAD
                        if j >= 2:
                            dve.wait_ge(S["av_done"], i * ALLQ + (j - 1))
                        dve.tensor_copy(alphaT[:, j % 2, k % QUAD].rearrange("p m n -> p (m n)"), PTB[k % 2][:]
                                        ).then_inc(S["alphaT_dve"], 1)

                    def invert(j):
                        dve.wait_ge(S["alpha_done"], i * ALL + (QUAD * j + QUAD))
                        if j >= 2:
                            dve.wait_ge(S["av_done"], i * ALLQ + (j - 1))
                        chain.link(dve.reciprocal(rsum[:], sums[:, j % 2]))
                        dve.tensor_copy(rsum_w[:, j % 2], bcast(rsum[:], 3, GO)).then_inc(S["rsum_ready"], 1)

                    def divide(j):
                        layer, c = j // QUADS // 2, j % QUADS
                        dve.wait_ge(S["av_done"], i * ALLQ + (j + 1))
                        chain.link(dve.tensor_copy(g_scale[:, j % 2, :], OB[j % 2][:, N:2 * N]))
                        dve.tensor_tensor(g_out[:, j % 2, :], OB[j % 2][:, 0:N], g_scale[:, j % 2, :], ALU.mult
                                          ).then_inc(S["g_norm"], 1)
                        dve.wait_ge(S["g_norm"], i * ALLQ + (j + 1))
                        dve.tensor_scalar(g_pos[:, j % 2, :], g_out[:, j % 2, :], bT1[:, layer, c:c + 1], -1.0,
                                          ALU.add, ALU.max).then_inc(S["g_max"], 1)

                    def elu(j):
                        r, c = divmod(j, QUADS)
                        dve.wait_ge(S["g_exps"], i * ALLQ + (j + 1))
                        dve.wait_ge(S["g_max"], i * ALLQ + (j + 1))
                        dst = h1T if r < 2 else x1T
                        dve.scalar_tensor_tensor(dst[:, r % 2, c, :], g_exp[:, j % 2, :], 1.0, g_pos[:, j % 2, :],
                                                 ALU.min, ALU.add).then_inc(S["g_elu"], 1)

                    def add_x1(p):
                        for nt in range(NT):
                            row = xs[:, bass.ds(i * 4 + (2 * p + nt), 1), :].rearrange("p u c -> p (u c)")
                            dve.wait_ge(S["x1_ready"], i * 4 + (2 * p + nt + 1))
                            dve.tensor_tensor(row, FEAT[:, 0:N], row, ALU.add).then_inc(S["x1_added"], 1)

                    for k in range(-1, LAST):
                        if 0 <= k - 1 < ALL:
                            edges(k - 1)
                        if 0 <= k - 4 < ALL and k % 2:
                            copy_T(k - 4)
                        if (r := prep_at(k)) is not None:
                            prep(r)
                        if (j := quad_at(k, -1)) is not None:
                            invert(j)
                        if (j := quad_at(k, 1)) is not None:
                            divide(j)
                        if (j := quad_at(k, 2)) is not None:
                            elu(j)
                        if (j := quad_at(k, 3)) in (2 * QUADS + QUADS - 1, 3 * QUADS + QUADS - 1):
                            add_x1(j // QUADS - 2)
                chain.restart()
                dve.wait_ge(S["x1_added"], 4 * TURNS + 1)

            def router0():
                R = lambda j: route[:, j, :, 0:E0]
                logits = bank[2][:, 0:T * E0].rearrange("p (t e) -> p t e", t=T)
                dve.wait_ge(S["logit_ready"], 1)
                chain.link(dve.tensor_reduce(rcol[:, 0, :], logits, X, ALU.max))
                dve.tensor_tensor(R(0), logits, bcast(rcol[:, 0, :], 2, E0), ALU.subtract).then_inc(S["rmax_done"], 1)
                dve.wait_ge(S["rexp_done"], 1)
                chain.link(dve.tensor_reduce(rcol[:, 1, :], R(0), X, ALU.add))
                chain.link(dve.reciprocal(rcol[:, 2, :], rcol[:, 1, :]))
                chain.link(dve.memset(padded[:], -1.0))
                chain.link(dve.tensor_tensor(padded[:, :, 0:E0], R(0), bcast(rcol[:, 2, :], 2, E0), ALU.mult))
                for t in range(T):
                    dve.max(rtop[:, t, :], padded[:, t, 0:8])
                chain.link(dve.engine_nop())
                chain.link(dve.memset(rtop[:, :, K0:8], -1.0))
                for t in range(T):
                    dve.match_replace(kept[:, t, :], rtop[:, t, :], padded[:, t, :], -2.0)
                chain.link(dve.engine_nop())
                chain.link(dve.tensor_tensor(R(1), kept[:, :, 0:E0], padded[:, :, 0:E0], ALU.not_equal))
                chain.link(dve.scalar_tensor_tensor(wt0.rearrange("p e t -> p t e"), R(1), 0.25,
                                                    padded[:, :, 0:E0], ALU.mult, ALU.mult))

            def router1():
                dve.wait_ge(S["rexp_done"], 2)
                chain.link(dve.tensor_tensor(route[:, 1], route[:, 0], bcast(eb[:], 1, T), ALU.add))
                for t in range(T):
                    dve.max(rtop[:, t, :], route[:, 1, t, :])
                chain.link(dve.engine_nop())
                for t in range(T):
                    dve.match_replace(route[:, 2, t, :], rtop[:, t, :], route[:, 1, t, :], -3.0e38)
                chain.link(dve.engine_nop())
                chain.link(dve.tensor_tensor(route[:, 3], route[:, 2], route[:, 1], ALU.not_equal))
                chain.link(dve.tensor_tensor(route[:, 4], route[:, 3], route[:, 0], ALU.mult))
                chain.link(dve.tensor_reduce(rcol[:, 0, :], route[:, 4], X, ALU.add))
                chain.link(dve.reciprocal(rcol[:, 1, :], rcol[:, 0, :]))
                dve.memset(wt1[:, E1, :], 1.0)
                chain.link(dve.tensor_tensor(wt1[:, 0:E1, :].rearrange("p e t -> p t e"), route[:, 4],
                                             bcast(rcol[:, 1, :], 2, E1), ALU.mult))
                chain.link(dve.engine_nop())

            def keep_top(e, part):
                row = (lambda a: a[:, e, :]) if isinstance(e, int) else \
                    (lambda a: a[:, bass.ds(e, 1), :].rearrange("p u c -> p (u c)"))
                parts, rounds = 2 * I0 // P, TOPK // 8
                if part == 0:
                    chain.restart()
                    chain.link(dve.tensor_copy(work[:], row(sim)))
                for r in range(part, rounds if part == parts - 1 else part + 1):
                    chain.link(dve.max(top8[:], work[:]))
                    chain.link(dve.match_replace(work[:], top8[:], work[:], -3.0e38))
                if part == parts - 1:
                    chain.link(dve.max(top8[:], work[:]))
                    rest = TOPK % 8
                    chain.link(dve.scalar_tensor_tensor(row(sig), row(sim), top8[:, rest - 1:rest], row(sig),
                                                        ALU.is_ge, ALU.mult))

            def split_activations(n):
                for half in range(2):
                    cols = slice(512 * half, 512 * half + 512)
                    dve.wait_ge(S["normT_copied"], n * T + (half + 1) * (T // 2))
                    dve.tensor_copy(actT_r[:, 0, :, cols], actT[:, :, cols]).then_inc(S["actT_hi"], 1)
                    dve.wait_ge(S["actT_hi"], 2 * n + half + 1)
                    dve.tensor_tensor(actT_r[:, 1, :, cols], actT[:, :, cols], actT_r[:, 0, :, cols].bitcast(F32),
                                      ALU.subtract).then_inc(S["actT_lo"], 1)

            def mixture(which):
                m = mix[which]
                IC, wt = m["IC"], m["wt"]
                DB = bank[4:8]

                def multiply(s, mod):
                    if not isinstance(s, int) or s >= 2:
                        dve.wait_ge(m["down"], s * 2 - 2)
                    for ic in range(IC):
                        qp = (mod * IC + ic) % 2
                        dve.wait_ge(m["silu"], s * IC + (ic + 1))
                        dve.tensor_tensor(hidf[:, qp, :], silu[:, qp, :], bank[2 + qp][:], ALU.mult
                                          ).then_inc(m["hidf"], 1)
                        dve.wait_ge(m["hidf"], s * IC + (ic + 1))
                        dve.tensor_copy(hidT[:, mod % 2, 0, ic, :], hidf[:, qp, :]).then_inc(m["hidh"], 1)
                        dve.wait_ge(m["hidh"], s * IC + (ic + 1))
                        dve.tensor_tensor(hidT[:, mod % 2, 1, ic, :], hidf[:, qp, :],
                                          hidT[:, mod % 2, 0, ic, :].bitcast(F32), ALU.subtract
                                          ).then_inc(m["hid"], 1)
                        if which == 0:
                            keep_top(s // 2 if isinstance(s, int) else (s - mod % 2) // 2, mod % 2 * IC + ic)

                def add(s, mod):
                    e = s // 2 if isinstance(s, int) else None
                    for j in range(4):
                        t = 4 * (mod % 2) + j
                        if j % 2 == 0:
                            dve.wait_ge(m["down"], s * 2 + (j // 2 + 1))
                        if j == 0 and (e is None or s >= 2):
                            dve.wait_ge(m["acc"], s * 2 - 2)
                        if e is not None:
                            w = wt[:, e, t:t + 1]
                        else:
                            w = wt[:, bass.ds((s - (mod % 2)) // 2, 1), t:t + 1].rearrange("p e t -> p (e t)")
                        ins = dve.scalar_tensor_tensor(xs[:, t, :], DB[2 * (mod % 2) + j // 2][:, j % 2 * D:j % 2 * D + D],
                                                       w, xs[:, t, :], ALU.mult, ALU.add)
                        if j % 2 == 1:
                            ins.then_inc(m["acc"], 1)

                steps = 2 * m["E"]
                multiply(0, 0)
                if which == 1:
                    chain.link(dve.tensor_tensor(xs[:], xs[:], x3[:], ALU.add))

                def body(s, mod):
                    if not isinstance(s, int) or s + 1 < steps:
                        multiply(s + 1, (mod + 1) % 4)
                    add(s, mod)

                expert_steps(dve, steps, body)

            def normalised(which, subtract, src=xs):
                for t in range(T):
                    if which * T + t >= 2:
                        dve.wait_ge(S["normT_ready"], which * T + t - 1)
                    if subtract:
                        ins = layer_norm_tile(norm[:, t % 2, :], t, src)
                    else:
                        ins = dve.tensor_scalar(norm[:, t % 2, :], xs[:, t, :], rstd[:, t:t + 1], None, ALU.mult)
                    ins.then_inc(S["norm_done"], 1)
                    if which == 0 and t >= 1:
                        copy_norm(which, t - 1)
                if which == 0:
                    copy_norm(which, T - 1)

            def copy_norm(which, t):
                dve.wait_ge(S["normT_ready"], which * T + t + 1)
                dve.tensor_copy(actT[:, :, t * P:t * P + P], bank[t % 2][:, 0:D].rearrange("p (c n) -> p c n", c=HC)
                                ).then_inc(S["normT_copied"], 1)

            def third():
                sums = actT.rearrange("p c n -> p (c n)").rearrange("p (t n) -> p t n", t=T)

                def add_transposed(t):
                    dve.wait_ge(S["aT_ready"], t + 1)
                    dve.tensor_tensor(sums[:, t, :], bank[2 + t % 2][:, 0:N], sig[:, t, :], ALU.add
                                      ).then_inc(S["aT_used"], 1)

                add_transposed(0)
                add_transposed(1)
                inverses(2)
                dve.wait_ge(S["gam_done"], 1)
                dve.tensor_scalar(gam[:, 2:3], gam[:, 1:2], 0.5, None, ALU.mult)
                dve.tensor_scalar(gam[:, 3:4], gam[:, 1:2], -1.0, 1.0, ALU.mult, ALU.add).then_inc(S["rstd_ready"], 1)
                for t in range(2, T):
                    add_transposed(t)
                for t in range(T - len(LN_POOL)):
                    layer_norm_tile(x3[:, t, :], t)
                chain.link(dve.engine_nop())
                for t in range(T):
                    if t in LN_POOL:
                        dve.wait_ge(S["ln_done"], LN_POOL.index(t) + 1)
                    dve.scalar_tensor_tensor(xs[:, t, :], x3[:, t, :], gam[:, 3:4], xs[:, t, :], ALU.mult, ALU.add)
                chain.link(dve.engine_nop())
                dve.wait_ge(S["aT_used"], T)
                for t in range(T):
                    dve.scalar_tensor_tensor(x3[:, t, :], sums[:, t, :], gam[:, 2:3], xs[:, t, :],
                                             ALU.mult, ALU.add).then_inc(S["x3_done"], 1)

            def attention():
                dve.wait_ge(S["att_in"], 48)

                def cosines(g, n, halves=(0, 1)):
                    tab = rk if n == 0 else rq
                    for half in halves:
                        dve.wait_ge(S["q_swapped"], g * PROJ + (2 * n + half + 1))
                        if n:
                            dve.wait_ge(S["q_rot"], g * PROJ + (2 * n + half - 1))
                        dve.tensor_tensor(rot_c[:, half].rearrange("p (b n) -> p b n", b=2),
                                          Q_BANK[half].rearrange("p (b n) -> p b n", b=2),
                                          bcast(tab[:, 0, :], 1, 2), ALU.mult).then_inc(S["q_cos"], 1)

                def rotate(g, n, halves=(0, 1)):
                    for half in halves:
                        dve.wait_ge(S["q_cos"], g * PROJ + (2 * n + half + 1))
                        dve.wait_ge(S["q_sin"], g * PROJ + (2 * n + half + 1))
                        dst = kT[:, half * 512:half * 512 + 512] if n == 0 else \
                            qT[:, (n - 1) % 2, half * 512:half * 512 + 512]
                        dve.tensor_tensor(dst, rot_c[:, half], rot_s[:, half], ALU.add).then_inc(S["q_rot"], 1)

                def copy_values(g):
                    for half in range(2):
                        dve.wait_ge(S["v_ready"], g * 2 + (half + 1))
                        dve.tensor_copy(vt[:, 4 * half:4 * half + 4, :], S_BANK[half].rearrange(
                            "p (t n) -> p t n", t=4)).then_inc(S["v_copied"], 1)

                def group(g, last):
                    def shift(k):
                        dve.wait_ge(S["s_ready"], g * AU + (k + 1))
                        if k >= 4:
                            dve.wait_ge(S["pT_ready"], g * AU + (k - 3))
                        dve.sem_inc(S["dve_held"])
                        for nt in range(NT):
                            ins = dve.tensor_tensor_reduce(
                                out=prob[:, k % 4, nt * P:nt * P + (nt + 1) * P],
                                in0=S_BANK[k % 2][:, nt * P:nt * P + (nt + 1) * P],
                                in1=causal[:, P - nt * P:2 * P], scale=1.0, scalar=3.0e38, op0=ALU.add, op1=ALU.min,
                                accum_out=pmin[:, k % 4, nt:nt + 1])
                        ins.then_inc(S["s_shift"], 1)

                    def normalise(k):
                        dve.wait_ge(S["p_exp"], g * AU + (k + 1))
                        dve.reciprocal(pinv[:, k % 4, :], psum_[:, k % 4, :]).then_inc(S["p_inv"], 1)
                        dve.wait_ge(S["p_inv"], g * AU + (k + 1))
                        for nt in range(NT):
                            ins = dve.tensor_scalar(prob[:, k % 4, nt * P:nt * P + (nt + 1) * P],
                                                    prob[:, k % 4, nt * P:nt * P + (nt + 1) * P],
                                                    pinv[:, k % 4, nt:nt + 1], None, ALU.mult)
                        ins.then_inc(S["p_norm"], 1)

                    def low_out(k):
                        h, b = divmod(k, B)
                        dve.wait_ge(S["o_high"], g * AU + (k + 1))
                        dve.tensor_tensor(oT[1][h][:, b * N:b * N + N], O_BANK[k % 2][:, 0:N],
                                          oT[0][h][:, b * N:b * N + N].bitcast(F32), ALU.subtract
                                          ).then_inc(S["o_copied"], 1)

                    def add_out(j):
                        dve.wait_ge(S["wo_ready"], g * (T // 2) + (j + 2))
                        rows = xs[:, 2 * j:2 * j + 2, :]
                        dve.tensor_tensor(rows, PT_BANK[j % 2].rearrange("p (t c) -> p t c", t=2), rows,
                                          ALU.add).then_inc(S["wo_added"], 1)

                    for k in range(AU + 4):
                        if (q := half_at(k, 3)) is not None:
                            rotate(g, *q)
                        if (q := half_at(k, 2)) is not None:
                            cosines(g, *q)
                        if k < AU:
                            shift(k)
                        if 0 <= k - 1 < AU:
                            normalise(k - 1)
                        if 0 <= k - 4 < AU:
                            low_out(k - 4)
                    if not last:
                        cosines(g + 1, 0)
                        copy_values(g + 1)
                        rotate(g + 1, 0)
                    add_out(0)
                    add_out(1)
                    if not last:
                        cosines(g + 1, 1)
                        rotate(g + 1, 1)
                    add_out(2)
                    add_out(3)

                split_activations(1)
                copy_values(0)
                cosines(0, 0)
                rotate(0, 0)
                cosines(0, 1)
                rotate(0, 1)
                with dve.Fori(0, KV - 1) as g:
                    group(g, False)
                group(KV - 1, True)

            dve.memset(eps[:], EPS).then_inc(S["zero_done"], 1)
            prepare_vectors()
            dve.wait_ge(S["x_in"], 16)
            statistics(xs)
            inverses(0)
            graph_attention()
            statistics(xs)
            inverses(1)
            normalised(0, True)
            split_activations(0)
            router0()
            dve.wait_ge(S["sig_done"], T)
            mixture(0)
            dve.wait_ge(S["acc0"], 4 * E0)
            statistics(xs)
            third()
            dve.wait_ge(S["x3_done"], T)
            statistics(x3)
            inverses(3)
            chain.link(dve.tensor_tensor(ymean[:], mv[:, :, 1], rstd[:], ALU.mult))
            dve.tensor_tensor(ymean[:], ymean[:], rstd[:], ALU.mult).then_inc(S["var_scaled"], 1)
            chain.link(dve.tensor_copy(rstd3[:], rstd[:]))
            inverses(4)
            chain.link(dve.tensor_tensor(rstd[:], rstd[:], rstd3[:], ALU.mult))
            normalised(1, True, x3)
            for t in range(T):
                dve.tensor_scalar(xs[:, t, :], x3[:, t, :], mv[:, t, 0:1], rstd3[:, t:t + 1], ALU.subtract, ALU.mult)
            attention()
            inverses(5)
            dve.wait_ge(S["wo_added"], KV * (T // 2) + 1)
            normalised(2, False)
            split_activations(2)
            dve.wait_ge(S["rexp_done"], 2)
            dve.engine_nop().then_inc(S["rmax_done"], 1)
            router1()
            mixture(1)


def kernel(**inputs):
    import concourse.bacc as bacc
    from concourse.bass_utils import run_bass_kernel_spmd

    a = {k: np.asarray(v) for k, v in inputs.items()}
    flat = lambda name: a[name].reshape(-1)
    heads_last = lambda w: np.transpose(w, (1, 0, 2)).reshape(w.shape[1], -1)

    pos = np.arange(N, dtype=np.float32)
    inv = (1.0 / 10000.0 ** (np.arange(0, HD, 2, dtype=np.float32) / HD)).astype(np.float32)
    ang = (pos[:, None] * inv[None, :]).astype(np.float32).T
    cos, sin = np.cos(ang), np.sin(ang)
    rope_k = np.stack([np.concatenate([cos, cos]), np.concatenate([-sin, sin])], 1).astype(np.float32)
    rope_q = (rope_k * np.float32(-1.0 / np.sqrt(HD))).astype(np.float32)
    causal = np.zeros((P, 2 * P), np.float32)
    causal[:, P:] = np.triu(np.full((P, P), 1e9, np.float32), 1)
    ind = np.zeros((TR, GH, P), np.float32)
    for h in range(GH):
        ind[[h, ROW + h], h] = 1.0

    arrays = dict(
        x=a["x"], ctxT=np.transpose(a["ctx_512"], (2, 0, 1)),
        W0=heads_last(a["L0_xattn_W0"]), W1=heads_last(a["L0_xattn_W1"]),
        a_self0=flat("L0_xattn_a_self0"), a_neigh0=flat("L0_xattn_a_neigh0"),
        a_self1=flat("L0_xattn_a_self1"), a_neigh1=flat("L0_xattn_a_neigh1"),
        b01=np.stack([flat(n).reshape(HC, P).T for n in ("L0_xattn_b0", "L0_xattn_b1")], 1),
        w_router=a["L0_ffn_w_router"], w_gate=a["L0_ffn_w_gate"], w_up=a["L0_ffn_w_up"],
        w_down=a["L0_ffn_w_down"], WqT=a["L1_xattn_Wq"].T, WkT=a["L1_xattn_Wk"].T,
        gamma=flat("L1_xattn_gamma_raw"), ln1=a["L1_ffn_ln1_w"].reshape(HC, P).T,
        ln2=a["L1_ffn_ln2_w"].reshape(HC, P).T, Wq=a["L1_ffn_Wq"], Wk=a["L1_ffn_Wk"],
        Wv=a["L1_ffn_Wv"], Wo=a["L1_ffn_Wo"], Wr=a["L1_ffn_Wr"], ebias=a["L1_ffn_expert_bias"],
        Wg=np.concatenate([a["L1_ffn_Wg"], a["L1_ffn_Wsg"][None]]),
        Wu=np.concatenate([a["L1_ffn_Wu"], a["L1_ffn_Wsu"][None]]),
        Wd=np.concatenate([a["L1_ffn_Wd"], a["L1_ffn_Wsd"][None]]),
        ident_in=np.eye(P, dtype=np.float32), ind_in=ind, rope_q=rope_q, rope_k=rope_k, causal_in=causal)

    nc = bacc.Bacc("TRN2", target_bir_lowering=False, num_devices=1)
    feeds, args = {}, {}
    for name, v in arrays.items():
        v = np.ascontiguousarray(v)
        feeds[f"in_{name}"] = v
        args[name] = nc.dram_tensor(f"in_{name}", v.shape, mybir.dt.from_np(v.dtype), kind="ExternalInput").ap()
    args["out"] = nc.dram_tensor("out_0", (B, N, D), F32, kind="ExternalOutput").ap()
    build(nc, **args)
    r = run_bass_kernel_spmd(nc, [feeds], core_ids=[0])
    return r.results[0]["out_0"]
```
